# Optimizing a Trainium2 kernel written in Bass

```python
import numpy as np
import jax
import jax.numpy as jnp

def _softmax(x, axis=-1):
    return jax.nn.softmax(x, axis=axis)

def _gelu(x):
    return jax.nn.gelu(x, approximate=True)

def _silu(x):
    return jax.nn.silu(x)

def _sigmoid(x):
    return jax.nn.sigmoid(x)

def _layernorm(x, axis=-1, eps=1e-05):
    m = jnp.mean(x, axis=axis, keepdims=True)
    v = jnp.var(x, axis=axis, keepdims=True)
    return (x - m) / jnp.sqrt(v + eps)

def _scatter_add(tgt, idx, src, axis=0):
    return tgt.at[idx].add(src)

def _segment_sum(src, seg, n):
    return jax.ops.segment_sum(src, seg, n)
kernel_name = 'mk_xattn_ffn_d2_seqx_r8_44d623'

def setup_inputs(seed: int=0):
    np.random.seed(seed)
    _w = jnp.asarray

    def _rec_inputs():
        import jax
        import jax.numpy as jnp
        _rk = jax.random.key(seed)
        x = 0.0002417 + 0.9998 * jax.random.normal(jax.random.fold_in(_rk, 1), (32, 128, 128), jnp.float32)
        _lenS = 128 - jax.random.randint(jax.random.fold_in(_rk, 7), (32,), 0, max(1, 128 // 4) + 1, jnp.int32)
        _lenS2 = 120 - jax.random.randint(jax.random.fold_in(_rk, 8), (32,), 0, max(1, 120 // 4) + 1, jnp.int32)
        _ctx_1024P = jax.random.normal(jax.random.fold_in(_rk, 11), (32, 16, 128), jnp.float32)
        _ctx_1024c = jax.random.dirichlet(jax.random.fold_in(_rk, 511), 0.3 * jnp.ones((16,), jnp.float32), (32, 120))
        _ctx_1024t = jnp.einsum('bsk,bkd->bsd', _ctx_1024c, _ctx_1024P)
        _ctx_1024t = _ctx_1024t * jax.lax.rsqrt(jnp.mean(jnp.square(_ctx_1024t)) + 1e-12) * 0.953939
        ctx_1024 = 7.22013e-05 + 1.00017 * (_ctx_1024t + 0.3 * jax.random.normal(jax.random.fold_in(_rk, 611), (32, 120, 128), jnp.float32))
        return (x, ctx_1024)
    x, ctx_1024 = _rec_inputs()

    def _L0_xattn_setup():
        import jax, jax.numpy as jnp
        import numpy as np
        EMBED = 128
        HEADS = 16
        HEAD_DIM = EMBED // HEADS
        EXP_DIM = 2 * HEAD_DIM

        def _feature_map(x, fm_w, fm_b):
            z = jnp.einsum('nshd,ed->nshe', x, fm_w) + fm_b
            return jnp.concatenate([jnp.exp(z), jnp.exp(-z)], axis=-1)
        key = jax.random.key(seed)
        ks = jax.random.split(key, 7)
        N, S = (4, 256)
        values = jax.random.normal(ks[0], (N, S, EMBED), dtype=jnp.float32)
        keys_ = jax.random.normal(ks[1], (N, S, EMBED), dtype=jnp.float32)
        query = jax.random.normal(ks[2], (N, S, EMBED), dtype=jnp.float32)
        fm_w = jnp.eye(HEAD_DIM, dtype=jnp.float32) + 0.02 * jax.random.normal(ks[3], (HEAD_DIM, HEAD_DIM), dtype=jnp.float32)
        fm_b = 0.02 * jax.random.normal(ks[4], (HEAD_DIM,), dtype=jnp.float32)
        fc_w = jax.random.normal(ks[5], (EMBED, HEADS * EXP_DIM), dtype=jnp.float32) * (1.0 / np.sqrt(HEADS * EXP_DIM))
        fc_b = jnp.zeros((EMBED,), dtype=jnp.float32)
        return {'values': values, 'keys': keys_, 'query': query, 'fm_w': fm_w, 'fm_b': fm_b, 'fc_w': fc_w, 'fc_b': fc_b}
    _L0_xattn_all = _L0_xattn_setup()
    _L0_xattn_in = {k: v for k, v in _L0_xattn_all.items() if k in ('fm_w', 'fm_b', 'fc_w', 'fc_b')}
    del _L0_xattn_all

    def _L0_ffn_setup():
        import jax, jax.numpy as jnp
        import numpy as np
        E, D, F, GATE_DIM = (8, 128, 512, 16)
        B, T = (2, 256)
        key = jax.random.key(seed)
        ks = jax.random.split(key, 7)
        s = 0.02
        return {'hidden_states': jax.random.normal(ks[0], (B, T, D), dtype=jnp.float32), 'w_red': jax.random.normal(ks[1], (D, GATE_DIM), dtype=jnp.float32) * s, 'wg': jax.random.normal(ks[2], (E, GATE_DIM), dtype=jnp.float32), 'w1': jax.random.normal(ks[3], (E, D, F), dtype=jnp.float32) * s, 'b1': jax.random.normal(ks[4], (E, F), dtype=jnp.float32) * s, 'w2': jax.random.normal(ks[5], (E, F, D), dtype=jnp.float32) * s, 'b2': jax.random.normal(ks[6], (E, D), dtype=jnp.float32) * s}
    _L0_ffn_all = _L0_ffn_setup()
    _L0_ffn_in = {k: v for k, v in _L0_ffn_all.items() if k in ('w_red', 'wg', 'w1', 'b1', 'w2', 'b2')}
    del _L0_ffn_all

    def _L1_xattn_setup():
        import jax, jax.numpy as jnp
        import numpy as np
        DIM = 128
        CTX_DIM = 128
        HEADS = 16
        DIM_HEAD = 64
        INNER = HEADS * DIM_HEAD
        FF_INNER = 4 * DIM
        EPS = 1e-05

        def layer_norm(x, g, b):
            mu = jnp.mean(x, axis=-1, keepdims=True)
            var = jnp.var(x, axis=-1, keepdims=True)
            return (x - mu) * jax.lax.rsqrt(var + EPS) * g + b
        key = jax.random.key(seed)
        ks = jax.random.split(key, 9)
        b, n, j = (4, 256, 128)
        inp = {'x': jax.random.normal(ks[0], (b, n, DIM), dtype=jnp.float32), 'context': jax.random.normal(ks[1], (b, j, CTX_DIM), dtype=jnp.float32), 'ln_g': jnp.ones((DIM,), jnp.float32), 'ln_b': jnp.zeros((DIM,), jnp.float32), 'cln_g': jnp.ones((CTX_DIM,), jnp.float32), 'cln_b': jnp.zeros((CTX_DIM,), jnp.float32), 'Wq': jax.random.normal(ks[2], (DIM, INNER), dtype=jnp.float32) * DIM ** (-0.5), 'Wkv': jax.random.normal(ks[3], (CTX_DIM, 2 * DIM_HEAD), dtype=jnp.float32) * CTX_DIM ** (-0.5), 'Wo': jax.random.normal(ks[4], (INNER, DIM), dtype=jnp.float32) * INNER ** (-0.5), 'Wff1': jax.random.normal(ks[5], (DIM, 2 * FF_INNER), dtype=jnp.float32) * DIM ** (-0.5), 'Wff2': jax.random.normal(ks[6], (FF_INNER, DIM), dtype=jnp.float32) * FF_INNER ** (-0.5)}
        return inp
    _L1_xattn_all = _L1_xattn_setup()
    _L1_xattn_in = {k: v for k, v in _L1_xattn_all.items() if k in ('ln_g', 'ln_b', 'cln_g', 'cln_b', 'Wq', 'Wkv', 'Wo', 'Wff1', 'Wff2')}
    del _L1_xattn_all

    def _L1_ffn_setup():
        import jax, jax.numpy as jnp
        import numpy as np
        N_EXPERTS = 8
        TOP_K = 2
        key = jax.random.key(seed)
        k1, k2, k3, k4 = jax.random.split(key, 4)
        B, T, C, H, E = (2, 256, 128, 512, N_EXPERTS)
        x = jax.random.normal(k1, (B, T, C), dtype=jnp.float32)
        router_w = jax.random.normal(k2, (E, C), dtype=jnp.float32) * 0.02
        w1 = jax.random.normal(k3, (E, C, H), dtype=jnp.float32) * (1.0 / np.sqrt(C))
        w2 = jax.random.normal(k4, (E, H, C), dtype=jnp.float32) * (1.0 / np.sqrt(H))
        return {'x': x, 'router_w': router_w, 'w1': w1, 'w2': w2}
    _L1_ffn_all = _L1_ffn_setup()
    _L1_ffn_in = {k: v for k, v in _L1_ffn_all.items() if k in ('router_w', 'w1', 'w2')}
    del _L1_ffn_all
    return {'x': x, 'ctx_1024': ctx_1024, 'L0_xattn_fm_w': _L0_xattn_in['fm_w'], 'L0_xattn_fm_b': _L0_xattn_in['fm_b'], 'L0_xattn_fc_w': _L0_xattn_in['fc_w'], 'L0_xattn_fc_b': _L0_xattn_in['fc_b'], 'L0_ffn_w_red': _L0_ffn_in['w_red'], 'L0_ffn_wg': _L0_ffn_in['wg'], 'L0_ffn_w1': _L0_ffn_in['w1'], 'L0_ffn_b1': _L0_ffn_in['b1'], 'L0_ffn_w2': _L0_ffn_in['w2'], 'L0_ffn_b2': _L0_ffn_in['b2'], 'L1_xattn_ln_g': _L1_xattn_in['ln_g'], 'L1_xattn_ln_b': _L1_xattn_in['ln_b'], 'L1_xattn_cln_g': _L1_xattn_in['cln_g'], 'L1_xattn_cln_b': _L1_xattn_in['cln_b'], 'L1_xattn_Wq': _L1_xattn_in['Wq'], 'L1_xattn_Wkv': _L1_xattn_in['Wkv'], 'L1_xattn_Wo': _L1_xattn_in['Wo'], 'L1_xattn_Wff1': _L1_xattn_in['Wff1'], 'L1_xattn_Wff2': _L1_xattn_in['Wff2'], 'L1_ffn_router_w': _L1_ffn_in['router_w'], 'L1_ffn_w1': _L1_ffn_in['w1'], 'L1_ffn_w2': _L1_ffn_in['w2']}

def reference(x, ctx_1024, L0_xattn_fm_w, L0_xattn_fm_b, L0_xattn_fc_w, L0_xattn_fc_b, L0_ffn_w_red, L0_ffn_wg, L0_ffn_w1, L0_ffn_b1, L0_ffn_w2, L0_ffn_b2, L1_xattn_ln_g, L1_xattn_ln_b, L1_xattn_cln_g, L1_xattn_cln_b, L1_xattn_Wq, L1_xattn_Wkv, L1_xattn_Wo, L1_xattn_Wff1, L1_xattn_Wff2, L1_ffn_router_w, L1_ffn_w1, L1_ffn_w2):
    import jax
    import jax.numpy as jnp

    def _L0_xattn_ref(values, keys, query, fm_w, fm_b, fc_w, fc_b):
        import jax, jax.numpy as jnp
        import numpy as np
        EMBED = 128
        HEADS = 16
        HEAD_DIM = EMBED // HEADS
        EXP_DIM = 2 * HEAD_DIM

        def _feature_map(x, fm_w, fm_b):
            z = jnp.einsum('nshd,ed->nshe', x, fm_w) + fm_b
            return jnp.concatenate([jnp.exp(z), jnp.exp(-z)], axis=-1)
        N, S, _ = query.shape
        v = values.reshape(N, -1, HEADS, HEAD_DIM)
        k = keys.reshape(N, -1, HEADS, HEAD_DIM)
        q = query.reshape(N, -1, HEADS, HEAD_DIM)
        v, k, q = (_feature_map(x, fm_w, fm_b) for x in (v, k, q))
        scores = jnp.einsum('nqhd,nkhd->nhqk', q, k) / jnp.sqrt(jnp.float32(EMBED))
        attn = jax.nn.softmax(scores, axis=-1)
        out = jnp.einsum('nhql,nlhd->nqhd', attn, v)
        out = out.reshape(N, S, HEADS * EXP_DIM)
        return out @ fc_w.T + fc_b

    def _L0_ffn_ref(hidden_states, w_red, wg, w1, b1, w2, b2):
        import jax, jax.numpy as jnp
        import numpy as np
        E, D, F, GATE_DIM = (8, 128, 512, 16)
        B, T = (2, 256)
        b, t, c = hidden_states.shape
        x = hidden_states.reshape(-1, c)
        red = x @ w_red
        wg_n = wg / jnp.maximum(jnp.linalg.norm(wg, axis=1, keepdims=True), 0.0001)
        logits = red @ wg_n.T
        gates = jax.nn.softmax(logits, axis=1)
        idx = jnp.argmax(gates, axis=1)
        scores = jnp.take_along_axis(gates, idx[:, None], axis=1)
        h = jax.nn.gelu(jnp.einsum('td,edf->etf', x, w1) + b1[:, None, :], approximate=False)
        y = jnp.einsum('etf,efd->etd', h, w2) + b2[:, None, :]
        out = jnp.take_along_axis(y, idx[None, :, None], axis=0)[0]
        out = out * scores
        return out.reshape(b, t, c)

    def _L1_xattn_ref(x, context, ln_g, ln_b, cln_g, cln_b, Wq, Wkv, Wo, Wff1, Wff2):
        import jax, jax.numpy as jnp
        import numpy as np
        DIM = 128
        CTX_DIM = 128
        HEADS = 16
        DIM_HEAD = 64
        INNER = HEADS * DIM_HEAD
        FF_INNER = 4 * DIM
        EPS = 1e-05

        def layer_norm(x, g, b):
            mu = jnp.mean(x, axis=-1, keepdims=True)
            var = jnp.var(x, axis=-1, keepdims=True)
            return (x - mu) * jax.lax.rsqrt(var + EPS) * g + b
        scale = DIM_HEAD ** (-0.5)
        xn = layer_norm(x, ln_g, ln_b)
        cn = layer_norm(context, cln_g, cln_b)
        b, n, _ = xn.shape
        q = (xn @ Wq).reshape(b, n, HEADS, DIM_HEAD).transpose(0, 2, 1, 3) * scale
        kv = cn @ Wkv
        k, v = (kv[..., :DIM_HEAD], kv[..., DIM_HEAD:])
        sim = jnp.einsum('bhid,bjd->bhij', q, k)
        attn = jax.nn.softmax(sim, axis=-1)
        out = jnp.einsum('bhij,bjd->bhid', attn, v)
        out = out.transpose(0, 2, 1, 3).reshape(b, n, INNER) @ Wo
        ff = xn @ Wff1
        h, gate = (ff[..., :FF_INNER], ff[..., FF_INNER:])
        out = out + jax.nn.silu(gate) * h @ Wff2
        return out

    def _L1_ffn_ref(x, router_w, w1, w2):
        import jax, jax.numpy as jnp
        import numpy as np
        N_EXPERTS = 8
        TOP_K = 2
        B, T, C = x.shape
        E = N_EXPERTS
        xf = x.reshape(-1, C)
        logits = jnp.einsum('nc,ec->ne', xf, router_w)
        probs = jax.nn.softmax(logits, axis=-1)
        top_w, top_i = jax.lax.top_k(probs, TOP_K)
        top_w = top_w / jnp.sum(top_w, axis=-1, keepdims=True)
        comb = jnp.einsum('nk,nke->ne', top_w, jax.nn.one_hot(top_i, E, dtype=xf.dtype))
        h = jax.nn.gelu(jnp.einsum('nc,ech->enh', xf, w1), approximate=False)
        y = jnp.einsum('enh,ehc->enc', h, w2)
        out = jnp.einsum('ne,enc->nc', comb, y)
        return out.reshape(B, T, C)
    x = x + _L0_xattn_ref(ctx_1024, ctx_1024, _layernorm(x, axis=-1), L0_xattn_fm_w, L0_xattn_fm_b, L0_xattn_fc_w, L0_xattn_fc_b)
    x = x + _L0_ffn_ref(_layernorm(x, axis=-1), L0_ffn_w_red, L0_ffn_wg, L0_ffn_w1, L0_ffn_b1, L0_ffn_w2, L0_ffn_b2)
    x = x + _L1_xattn_ref(_layernorm(x, axis=-1), ctx_1024, L1_xattn_ln_g, L1_xattn_ln_b, L1_xattn_cln_g, L1_xattn_cln_b, L1_xattn_Wq, L1_xattn_Wkv, L1_xattn_Wo, L1_xattn_Wff1, L1_xattn_Wff2)
    x = x + _L1_ffn_ref(_layernorm(x, axis=-1), L1_ffn_router_w, L1_ffn_w1, L1_ffn_w2)
    return x

_drawn_inputs = setup_inputs


def setup_inputs(seed=0):
    import zlib

    import numpy as np

    out = dict(_drawn_inputs(seed))
    spreads = {'L0_xattn_fc_b': (0.0, 0.8),
     'L1_xattn_ln_g': (1.0, 0.6),
     'L1_xattn_ln_b': (0.0, 0.8),
     'L1_xattn_cln_g': (1.0, 0.6),
     'L1_xattn_cln_b': (0.0, 0.8)}
    factors = {'L0_ffn_w_red': 8.0,
     'L0_ffn_wg': 8.0,
     'L0_ffn_w1': 8.0,
     'L0_ffn_b1': 21.448,
     'L0_ffn_w2': 8.0,
     'L0_ffn_b2': 53.656,
     'L1_xattn_Wq': 3.26}
    for name, (base, spread) in spreads.items():
        noise = np.random.default_rng([zlib.crc32(name.encode()), seed]).standard_normal(out[name].shape)
        drawn = base * np.exp(spread * noise) if base else spread * noise
        out[name] = jnp.asarray(drawn.astype(out[name].dtype))
    for name, factor in factors.items():
        out[name] = (out[name] * factor).astype(out[name].dtype)
    return out
```

```python
from contextlib import ExitStack

import concourse.bass as bass
from concourse import mybir

F32 = mybir.dt.float32
BF16 = mybir.dt.bfloat16
U32 = mybir.dt.uint32
I32 = mybir.dt.int32
ALU = mybir.AluOpType
ACT = mybir.ActivationFunctionType
AX = mybir.AxisListType.X

B = 32
S = 128
D = 128
C = 120
H = 16
E = 8
F = 512
FC = F // 128
G = 4
HD0 = 8
HD1 = 64
EPS = 1e-5
OFF = -200.0

REGION = B * S + 128
DUMMY = E * REGION
NT0 = B + E - 1
NT1 = 2 * B + E - 1

K_ID, K_TRI, K_ONE, K_SEL0, K_SEL1 = 0, 128, 256, 384, 384 + G * C
K_SIGN = K_SEL1 + (H // 2) * C
K_SCOL = K_SIGN + 512
K_IOTA8 = K_SCOL + 1
K_EOFF = K_IOTA8 + E
K_PART = K_EOFF + E
K_TILE = K_PART + 1
K_N = K_TILE + NT1 + 1


def reached(eng, sem, n):
    if isinstance(n, int) and n <= 0:
        return
    eng.wait_ge(sem, n)


def steps(eng, first, last, end, unroll, body):
    for i in range(-2, first):
        body(i, i % unroll)
    with eng.Fori(first, last + 2 - unroll, unroll) as i:
        for u in range(unroll):
            body(i + u if u else i, (first + u) % unroll)
    for i in range(last + 1, end + 1):
        body(i, i % unroll)


def alone(eng, tick, *waits):
    if all(isinstance(n, int) for _, n in waits):
        for sem, n in waits:
            reached(eng, sem, n)
        return
    for sem, n in waits:
        reached(eng, sem, n)
    eng.sem_inc(tick[eng.engine.name], 1)


def at_step(i, n):
    return isinstance(i, int) and i == n


def inside(i, shift, n=B):
    return not isinstance(i, int) or 0 <= i + shift < n


def build(nc, A):
    ctx = ExitStack()
    with ctx:
        def sb(name, shape, dt=F32):
            return ctx.enter_context(nc.sbuf_tensor(name, shape, dt))

        def sem(name):
            return ctx.enter_context(nc.semaphore(name))

        bank = [ctx.enter_context(nc.psum_tensor(f"bank{n}", [128, 512], F32)) for n in range(8)]

        xs = [nc.dram_tensor(f"sorted{n}", (DUMMY + 128, D), F32, kind="Internal").ap() for n in range(2)]
        ys = [nc.dram_tensor(f"expert_out{n}", (NT * 128, D), F32, kind="Internal").ap()
              for n, NT in enumerate((NT0, NT1))]

        cst = sb("cst", [128, K_N])
        x = sb("x_sb", [S, B, D])
        cx = sb("cx", [C, B, D])
        wz = sb("wz", [D, G, 128])
        wv0 = sb("wv0", [D, 128])
        zbias = sb("zbias", [128, 1])
        vbias = sb("vbias", [128, 128])
        fcw = sb("fcw", [128, 2, D])
        fcb = sb("fcb", [128, D])
        wred = sb("wred", [16, D])
        wg = sb("wg", [E, 16])
        wgn = sb("wgn", [E, 16])
        wgT = sb("wgT", [16, E])
        wsq = sb("wsq", [E, 4])
        halves = sb("halves", [128, 2])
        router = [sb(f"router{n}", [D, E]) for n in range(2)]
        w1 = sb("w1", [D, E, F])
        w2 = sb("w2", [128, E, FC, D])
        b1 = sb("b1", [128, E, F])
        b2 = sb("b2", [128, E, D])
        wq = sb("wq", [D, 1024])
        wk2 = sb("wk2", [D, 2, HD1])
        wv1 = sb("wv1", [D, HD1])
        wo = sb("wo", [128, 8, D])
        wf1 = sb("wf1", [D, 2, F])
        wf2 = sb("wf2", [128, FC, D])
        lnp = sb("lnp", [D, 4])
        identb = sb("identb", [128, 128], BF16)
        trib = sb("trib", [128, 128], BF16)
        oneb = sb("oneb", [128, 128], BF16)
        sel0 = sb("sel0", [128, G, C], BF16)
        sel1 = sb("sel1", [128, 8, C], BF16)
        zero = sb("zero", [128, D])
        ident = cst[:, K_ID:K_ID + 128]

        base = sb("base", [128, E])
        slot = sb("slot", [128, B, 2], U32)
        slotp = sb("slotp", [128, 2, 2], U32)
        gsum = sb("gsum", [128, B])
        gate = sb("gate", [128, 2, B])
        padidx = sb("padidx", [128, E], U32)
        tcnt = sb("tcnt", [128, 6, E])
        tint = sb("tint", [128, E], I32)
        trow = sb("trow", [1, 3, NT1])
        etab = sb("etab", [1, NT1 + 8], I32)
        rtab = sb("rtab", [1, NT1 + 8], I32)
        slotf = sb("slotf", [128, B, 2])
        slott = sb("slott", [128, 2, B, 2])

        mv = sb("mv", [128, 2, 2])
        mvc = sb("mvc", [128, 2, 2])
        st6 = sb("st6", [128, 3, 6])
        rst = sb("rst", [128, 2, 4])
        rstt = sb("rstt", [128, 4])
        mv1 = sb("mv1", [128, 2, 2])
        xn = sb("xn", [128, 2, D])
        cn = sb("cn", [C, 2, D])
        xcT = sb("xcT", [128, 2, 256])
        qf = sb("qf", [128, 2, 1024])
        kf = sb("kf", [128, 2, G * C])
        qb = sb("qb", [128, 2, 1024], BF16)
        kb = sb("kb", [128, 2, G * C], BF16)
        vz = sb("vz", [128, 128])
        v0 = sb("v0", [C, 2, H, 17])
        v1 = sb("v1", [C, 2, HD1 + 1])
        xpb = sb("xpb", [128, 2, D])
        mx = sb("mx", [128, 128], BF16)
        mT = sb("mT", [128, 128], BF16)
        PT = sb("PT", [C, 4, 512])
        rec = sb("rec", [128, H])
        on = sb("on", [128, 1024])
        oT = sb("oT", [128, 1024])
        sg = sb("sg", [128, 3, F])
        xr = sb("xr", [128, 2, D])
        xrT = sb("xrT", [128, 128])
        lgs = sb("lgs", [128, 8])
        top = sb("top", [128, 8])
        topi = sb("topi", [128, 8], U32)
        topf = sb("topf", [128, 2])
        hot = sb("hot", [128, 3, E], BF16)
        pos = sb("pos", [128, E])
        junk = sb("junk", [128, 8])
        junk2 = sb("junk2", [128, 8])
        slf = sb("slf", [128, 2])
        negm = sb("negm", [128, 1])
        yg = sb("yg", [128, 2, 2, D])
        xt = sb("xt", [128, 4, D])
        xtT = sb("xtT", [128, 2, 128])
        hb = sb("hb", [128, 2, F])
        hg = sb("hg", [128, 2, F])
        hT = sb("hT", [128, 2, F])
        yo = sb("yo", [128, 4, D])

        ld_cst, ld_x0, ld_x, ld_w0, ld_moe0 = (sem(n) for n in ("ld_cst", "ld_x0", "ld_x", "ld_w0", "ld_moe0"))
        ld_w1, ld_moe1 = sem("ld_w1"), sem("ld_moe1")
        made = sem("made")
        tick = {"DVE": sem("tick_vector"), "Pool": sem("tick_gpsimd")}
        made_p = sem("made_p")
        made_t = sem("made_t")

        with nc.Block() as block:
            @block.sync
            def _(sp):
                sp.dma_start(cst[:], A["cst"]).then_inc(ld_cst, 16)
                sp.dma_start(x[:, 0:2, :], A["x"][:, 0:2, :]).then_inc(ld_x0, 16)
                sp.dma_start(cx[:, 0:2, :], A["cx"][:, 0:2, :]).then_inc(ld_x0, 16)
                sp.dma_start(x[:, 2:B, :], A["x"][:, 2:B, :]).then_inc(ld_x, 16)
                sp.dma_start(cx[:, 2:B, :], A["cx"][:, 2:B, :]).then_inc(ld_x, 16)
                sp.dma_start(w1[:], A["w1_0"]).then_inc(ld_moe0, 16)
                sp.dma_start(w2[:], A["w2_0"]).then_inc(ld_moe0, 16)
                sp.dma_start(b1[:], A["b1"].partition_broadcast(128)).then_inc(ld_moe0, 16)
                sp.dma_start(b2[:], A["b2"].partition_broadcast(128)).then_inc(ld_moe0, 16)

            @block.scalar
            def _(act):
                for dst, src in ((wz[:], A["wz"]), (zbias[:], A["zb"]), (vbias[:], A["vb"].partition_broadcast(128)),
                                 (fcw[:], A["fcw"]), (fcb[:], A["fcb"].partition_broadcast(128)),
                                 (wred[:], A["wred"]), (wg[:], A["wg"])):
                    act.dma_start(dst, src).then_inc(ld_w0, 16)
                for dst, src in ((wq[:], A["wq"]), (wk2[:, 0, :], A["wk"]), (wk2[:, 1, :], A["wk"]), (wv1[:], A["wv"]),
                                 (wo[:], A["wo"]), (wf1[:], A["wf1"]), (wf2[:], A["wf2"]), (lnp[:], A["lnp"]),
                                 (router[1][:], A["router"])):
                    act.dma_start(dst, src).then_inc(ld_w1, 16)

            @block.vector
            def _(v):
                v.memset(zero[:], 0.0).then_inc(made, 1)
                v.memset(mx[:], 0.0).then_inc(made, 1)
                v.memset(halves[:, 0:1], -0.5).then_inc(made, 1)
                v.memset(halves[:, 1:2], 0.5).then_inc(made, 1)
                v.memset(v0[:, :, :, 16:17], 1.0).then_inc(made, 1)
                v.memset(v1[:, :, HD1:HD1 + 1], 1.0).then_inc(made, 1)
                v.wait_ge(ld_cst, 16)
                v.tensor_copy(identb[:], ident).then_inc(made, 1)
                v.tensor_copy(trib[:], cst[:, K_TRI:K_TRI + 128]).then_inc(made, 1)
                v.tensor_copy(oneb[:], cst[:, K_ONE:K_ONE + 128]).then_inc(made, 1)
                v.tensor_copy(sel0[:].rearrange("p a b -> p (a b)"), cst[:, K_SEL0:K_SEL0 + G * C]).then_inc(made, 1)
                v.tensor_copy(sel1[:].rearrange("p a b -> p (a b)"), cst[:, K_SEL1:K_SEL1 + 8 * C]).then_inc(made, 1)
                v.tensor_copy(base[:], cst[:, K_EOFF:K_EOFF + E]).then_inc(made, 1)
                v.wait_ge(ld_w0, 112)
                v.tensor_tensor(wz[:].rearrange("p g c -> p (g c)"), wz[:].rearrange("p g c -> p (g c)"),
                                cst[:, K_SIGN:K_SIGN + 512], ALU.mult).then_inc(made, 1)
                v.tensor_tensor(zbias[:], zbias[:], cst[:, K_SCOL:K_SCOL + 1], ALU.mult).then_inc(made, 1)
                v.wait_ge(made, 14)
                v.tensor_copy(wv0[:].rearrange("p (g j e) -> p g j e", g=G, j=4),
                              wz[:].rearrange("p g (j e) -> p g j e", j=4)[:, :, :, 0:HD0]).then_inc(made, 1)
                v.tensor_tensor_reduce(wgn[:], wg[:], wg[:], 1.0, 0.0, ALU.mult, ALU.add,
                                       wsq[:, 0:1]).then_inc(made, 1)
                v.wait_ge(made_p, 1)
                v.tensor_scalar(wsq[:, 2:3], wsq[:, 1:2], 1e-4, None, ALU.max).then_inc(made, 1)
                v.wait_ge(made, 17)
                v.reciprocal(wsq[:, 3:4], wsq[:, 2:3]).then_inc(made, 1)
                v.wait_ge(made, 18)
                v.tensor_scalar(wgn[:], wg[:], wsq[:, 3:4], None, ALU.mult).then_inc(made, 1)
                v.wait_ge(made_t, 1)
                v.tensor_copy(wgT[:], bank[0][0:16, 0:E]).then_inc(made, 1)
                v.wait_ge(made_t, 2)
                v.tensor_copy(router[0][:], bank[1][:, 0:E]).then_inc(made, 1)

            @block.gpsimd
            def _(pool):
                pool.wait_ge(made, 16)
                pool.tensor_tensor(wsq[:, 1:2], wsq[:, 0:1], halves[0:E, 1:2], ALU.pow).then_inc(made_p, 1)

            @block.tensor
            def _(pe):
                pe.wait_ge(made, 19)
                pe.transpose(bank[0][0:16, 0:E], wgn[:], ident[0:E, 0:E]).then_inc(made_t, 1)
                pe.wait_ge(made, 20)
                pe.matmul(bank[1][:, 0:E], wred[:], wgT[:], start=True, stop=True).then_inc(made_t, 1)

        def route(layer, v, p, b, sems, part):
            logits, ranks, totals = sems["logits"], sems["ranks"], sems["totals"]
            chain = sems["chain"]
            K = sems["K"]
            c0 = b * K

            def after(n):
                reached(v, chain, c0 + n)

            if part == 0:
                v.tensor_copy(lgs[:], logits).then_inc(chain, 1)
                alone(v, tick, (chain, c0 + 1))
                v.max(top[:], lgs[:]).then_inc(chain, 1)
                alone(v, tick, (chain, c0 + 2))
                v.max_index(topi[:], top[:], lgs[:]).then_inc(chain, 1)
                if layer == 0:
                    v.tensor_scalar(negm[:], top[:, 0:1], -1.0, None, ALU.mult).then_inc(chain, 1)
                else:
                    v.tensor_tensor(gsum[:, bass.ds(b, 1)], top[:, 1:2], top[:, 0:1],
                                    ALU.subtract).then_inc(chain, 1)
                after(4)
                v.tensor_copy(topf[:], topi[:, 0:2]).then_inc(chain, 1)
                after(5)
                v.tensor_scalar(hot[:, 0, :], cst[:, K_IOTA8:K_IOTA8 + E], topf[:, 0:1], None,
                                ALU.is_equal).then_inc(chain, 1)
                if layer == 1:
                    v.tensor_scalar(hot[:, 1, :], cst[:, K_IOTA8:K_IOTA8 + E], topf[:, 1:2], None,
                                    ALU.is_equal).then_inc(chain, 1)
                    after(7)
                    v.tensor_tensor(hot[:, 2, :], hot[:, 0, :], hot[:, 1, :], ALU.add).then_inc(chain, 1)
            else:
                n = 6 if layer == 0 else 8
                v.tensor_tensor(pos[:], ranks, base[:], ALU.add).then_inc(chain, 1)
                after(n + 1)
                v.tensor_tensor_reduce(junk2[:], pos[:], hot[:, 0, :], 1.0, 0.0, ALU.mult, ALU.add,
                                       slf[:, 0:1]).then_inc(chain, 1)
                if layer == 1:
                    v.tensor_tensor_reduce(junk[:], pos[:], hot[:, 1, :], 1.0, 0.0, ALU.mult, ALU.add,
                                           slf[:, 1:2]).then_inc(chain, 1)
                v.tensor_tensor(base[:], base[:], totals, ALU.add).then_inc(chain, 1)
                n += 3 + layer
                after(n)
                reached(v, sems["kept"], b - 1)
                v.tensor_copy(slotp[:, p, 0:1 + layer], slf[:, 0:1 + layer]).then_inc(chain, 1)

        (x_stat, x_rstd, x_norm, tf_done, tf_out, zq_done, zk_done, zv_done, q_exp, k_exp, vz_done, v_exp,
         qk_cast, xpb_done) = (sem("a_" + n) for n in (
             "x_stat", "x_rstd", "x_norm", "tf_done", "tf_out", "zq_done", "zk_done", "zv_done", "q_exp",
             "k_exp", "vz_done", "v_exp", "qk_cast", "xpb_done"))
        (sm_done, max_done, mt_done, mt_out, st_done, p_exp, pv_done, rec_done, on_done, ot_done, ot_out,
         fc_done, x1_done) = (sem("a_" + n) for n in (
             "sm_done", "max_done", "mt_done", "mt_out", "st_done", "p_exp", "pv_done", "rec_done", "on_done",
             "ot_done", "ot_out", "fc_done", "x1_done"))
        (xr_stat, xr_rstd, xr_norm, tr_done, tr_out, lg_done, rk_done, chain, gexp) = (sem("a_" + n) for n in (
            "xr_stat", "xr_rstd", "xr_norm", "tr_done", "tr_out", "lg_done", "rk_done", "chain", "gexp"))
        scat = [sem(f"a_scat{p}") for p in range(2)]
        c_copy = sem("a_c_copy")
        kept0 = sem("a_kept")
        ROUTE0 = dict(logits=bank[6][:, 128:128 + E], ranks=bank[6][:, 256:256 + E],
                      totals=bank[6][:, 384:384 + E], chain=chain, kept=kept0, K=10)

        with nc.Block() as block:
            @block.tensor
            def _(pe):
                def body(i, p):
                    q = 1 - p
                    nxt = i + 1 if inside(i, 1) else B - 1
                    if inside(i, 0):
                        pe.wait_ge(qk_cast, 2 * i + 2)
                        for j in range(4):
                            reached(pe, p_exp, 4 * i - 4 + j + 1)
                            for g in range(G):
                                mm = pe.matmul(bank[j][:, C * g:C * g + C], qb[32 * j:32 * j + 16, p, 128 * g:128 * g + 128],
                                               kb[32 * j:32 * j + 16, p, C * g:C * g + C], start=True, stop=True)
                            mm.then_inc(sm_done, 1)
                    if inside(i, 1):
                        pe.wait_ge(x_norm, i + 2)
                        reached(pe, vz_done, i + 1)
                        pe.transpose(bank[4][:, 0:128], xn[:, q, :], ident)
                        pe.wait_ge(c_copy, i + 2)
                        pe.transpose(bank[4][:, 128:128 + C], cn[:, q, :], ident[0:C, 0:C]).then_inc(tf_done, 1)
                        pe.wait_ge(tf_out, i + 2)
                        if inside(i, -2):
                            pe.wait_ge(chain, 10 * (i - 1))
                        for g in range(G):
                            mm = pe.matmul(bank[6][:, 128 * g:128 * g + 128], wz[:, g, :], xcT[:, q, 0:128],
                                           start=True, stop=True)
                        mm.then_inc(zq_done, 1)
                        reached(pe, ot_out, i)
                        for g in range(G):
                            mm = pe.matmul(bank[5][:, C * g:C * g + C], wz[:, g, :], xcT[:, q, 128:128 + C],
                                           start=True, stop=True)
                        mm.then_inc(zk_done, 1)
                        pe.matmul(bank[4][0:C, 256:384], xcT[:, q, 128:128 + C], wv0[:], start=True,
                                  stop=True).then_inc(zv_done, 1)
                    if inside(i, 0):
                        pe.wait_ge(max_done, 4 * i + 4)
                        pe.wait_ge(k_exp, nxt + 1)
                        pe.transpose(mtp, mx[:], identb[:]).then_inc(mt_done, 1)
                    if inside(i, -1):
                        pe.wait_ge(xr_norm, i)
                        pe.wait_ge(q_exp, nxt + 1)
                        pe.transpose(bank[6][:, 0:128], xr[:, q, :], ident).then_inc(tr_done, 1)

                    def st(j):
                        for g in range(G):
                            o = bank[j][0:C, 128 * g:128 * g + 128]
                            pe.matmul(o, kf[32 * j:32 * j + 16, p, C * g:C * g + C],
                                      qf[32 * j:32 * j + 16, p, 128 * g:128 * g + 128], start=True, stop=False)
                            mm = pe.matmul(o, sel0[32 * j:32 * j + 32, g, :], mT[32 * j:32 * j + 32, :],
                                           start=False, stop=True)
                        mm.then_inc(st_done, 1)

                    def pv(j):
                        pe.wait_ge(p_exp, 4 * i + j + 1)
                        for g in range(G):
                            h = 4 * g + j
                            mm = pe.matmul(bank[7][:, 17 * h:17 * h + 17], PT[:, j, 128 * g:128 * g + 128],
                                           v0[:, p, h, :], start=True, stop=True)
                        mm.then_inc(pv_done, 1)

                    if inside(i, 0):
                        pe.wait_ge(mt_out, i + 1)
                        st(0)
                        st(1)
                    if inside(i, -1):
                        pe.wait_ge(tr_out, i)
                        pe.matmul(ROUTE0["logits"], xrT[:], router[0][:], start=True, stop=True).then_inc(lg_done, 1)
                    if inside(i, 0):
                        pe.wait_ge(v_exp, 2 * i + 2)
                        reached(pe, x1_done, i)
                        pv(0)
                        st(2)
                        pv(1)
                        st(3)
                        pv(2)
                    if inside(i, -1):
                        pe.wait_ge(chain, 10 * (i - 1) + 6)
                        pe.matmul(ROUTE0["ranks"], trib[:], hot[:, 0, :], start=True, stop=True)
                        pe.matmul(ROUTE0["totals"], oneb[:], hot[:, 0, :], start=True, stop=True).then_inc(rk_done, 1)
                    if inside(i, 0):
                        pv(3)
                        pe.wait_ge(on_done, i + 1)
                        for c in range(2):
                            mm = pe.transpose(bank[5][:, 128 * c:128 * c + 128], on[:, 128 * c:128 * c + 128], ident)
                        mm.then_inc(ot_done, 1)
                        pe.wait_ge(ot_out, i + 1)
                        for c in range(2):
                            mm = pe.matmul(bank[7][:, 0:D], oT[:, 128 * c:128 * c + 128], fcw[:, c, :],
                                           start=(c == 0), stop=(c == 1))
                        mm.then_inc(fc_done, 1)

                mtp = bank[5][:, 0:64].bitcast(BF16)
                steps(pe, 3, 28, B, 2, body)

            @block.scalar
            def _(act):
                def body(i, p):
                    q = 1 - p
                    if inside(i, 1):
                        act.wait_ge(tf_done, i + 2)
                        act.activation(xcT[:, q, 0:128 + C], bank[4][:, 0:128 + C], ACT.Copy).then_inc(tf_out, 1)
                        act.wait_ge(zq_done, i + 2)
                        act.activation(qf[:, q, 0:512], bank[6][:, :], ACT.Exp, bias=zbias[:]).then_inc(q_exp, 1)
                        act.wait_ge(zk_done, i + 2)
                        act.activation(kf[:, q, :], bank[5][:, 0:G * C], ACT.Exp, bias=zbias[:]).then_inc(k_exp, 1)
                        act.wait_ge(vz_done, i + 2)
                        zv = vz[0:C, :].rearrange("p (h e) -> p h e", e=HD0)
                        act.activation(v0[:, q, :, 0:HD0], zv, ACT.Exp).then_inc(v_exp, 1)
                        act.activation(v0[:, q, :, HD0:16], zv, ACT.Exp, scale=-1.0).then_inc(v_exp, 1)
                    if inside(i, 0):
                        for j in range(4):
                            act.wait_ge(st_done, 4 * i + j + 1)
                            reached(act, pv_done, 4 * i + j - 3)
                            act.activation(PT[:, j, :], bank[j][0:C, :], ACT.Exp,
                                           scale=float(D) ** -0.5).then_inc(p_exp, 1)
                            if j == 0 and inside(i, -1):
                                act.wait_ge(tr_done, i)
                                act.activation(xrT[:], bank[6][:, 0:128], ACT.Copy).then_inc(tr_out, 1)
                    elif inside(i, -1):
                        act.wait_ge(tr_done, i)
                        act.activation(xrT[:], bank[6][:, 0:128], ACT.Copy).then_inc(tr_out, 1)
                    if inside(i, -1):
                        act.wait_ge(chain, 10 * (i - 1) + 4)
                        act.activation(junk[:], lgs[:], ACT.Exp, bias=negm[:],
                                       accum_out=gsum[:, bass.ds(i - 1, 1)]).then_inc(gexp, 1)
                    if inside(i, 0):
                        act.wait_ge(ot_done, i + 1)
                        act.activation(oT[:, 0:256], bank[5][:, 0:256], ACT.Copy).then_inc(ot_out, 1)

                steps(act, 3, 28, B, 2, body)

            @block.vector
            def _(v):
                def body(i, p):
                    q = 1 - p
                    if inside(i, 0):
                        for j in range(4):
                            v.wait_ge(sm_done, 4 * i + j + 1)
                            reached(v, mt_done, i)
                            v.tensor_reduce(mx[:, 32 * j:32 * j + G],
                                            bank[j][:, 0:G * C].rearrange("p (g k) -> p g k", g=G), AX,
                                            ALU.max).then_inc(max_done, 1)
                            if j == 1 and inside(i, -1):
                                norm_r(i, q)
                    elif inside(i, -1):
                        norm_r(i, q)
                    if inside(i, 1):
                        v.wait_ge(zv_done, i + 2)
                        reached(v, v_exp, 2 * i + 2)
                        v.tensor_tensor(vz[0:C, :], bank[4][0:C, 256:384], vbias[0:C, :], ALU.add).then_inc(vz_done, 1)
                    if inside(i, 0):
                        v.wait_ge(mt_done, i + 1)
                        v.tensor_copy(mT[:], bank[5][:, 0:64].bitcast(BF16)).then_inc(mt_out, 1)
                    if inside(i, 2):
                        if at_step(i, -2):
                            v.wait_ge(ld_x0, 32)
                            v.wait_ge(made, 21)
                        elif at_step(i, 0):
                            v.wait_ge(ld_x, 32)
                        v.bn_stats(st6[:, 0, :], x[:, bass.ds(i + 2, 1), :].rearrange("p b d -> p (b d)")).then_inc(x_stat, 1)
                        alone(v, tick, (x_stat, 2 * (i + 2) + 1))
                        v.bn_aggr(mv[:, p, :], st6[:, 0, :]).then_inc(x_stat, 1)
                    if inside(i, -1):
                        v.wait_ge(lg_done, i)
                        reached(v, gexp, i - 1)
                        route(0, v, q, i - 1, ROUTE0, 0)
                    if inside(i, 2):
                        v.wait_ge(x_rstd, 2 * (i + 2) + 2)
                        reached(v, tf_done, i + 1)
                        v.tensor_scalar(xn[:, p, :], x[:, bass.ds(i + 2, 1), :].rearrange("p b d -> p (b d)"),
                                        mv[:, p, 0:1], rst[:, p, 0:1], ALU.subtract, ALU.mult).then_inc(x_norm, 1)
                    if inside(i, -1):
                        v.wait_ge(rk_done, i)
                        route(0, v, q, i - 1, ROUTE0, 1)
                    if inside(i, 0):
                        v.wait_ge(pv_done, 4 * i + 4)
                        o = bank[7][:, 0:H * 17].rearrange("p (h e) -> p h e", e=17)
                        v.reciprocal(rec[:].rearrange("p (h e) -> p h e", e=1), o[:, :, 16:17]).then_inc(rec_done, 1)
                        v.wait_ge(rec_done, i + 1)
                        v.tensor_tensor(on[:, 0:256].rearrange("p (h e) -> p h e", e=16), o[:, :, 0:16],
                                        rec[:].rearrange("p (h e) -> p h e", e=1).broadcast_to([128, H, 16]),
                                        ALU.mult).then_inc(on_done, 1)
                        v.wait_ge(fc_done, i + 1)
                        v.wait_ge(xpb_done, i + 1)
                        xi = x[:, bass.ds(i, 1), :].rearrange("p b d -> p (b d)")
                        v.tensor_tensor(xi, bank[7][:, 0:D], xpb[:, p, :], ALU.add).then_inc(x1_done, 1)
                        alone(v, tick, (x1_done, i + 1))
                        v.bn_stats(st6[:, 1, :], xi).then_inc(xr_stat, 1)
                        alone(v, tick, (xr_stat, 2 * i + 1))
                        v.bn_aggr(mv1[:, p, :], st6[:, 1, :]).then_inc(xr_stat, 1)

                def norm_r(i, q):
                    v.wait_ge(xr_rstd, 2 * i)
                    if inside(i, -3):
                        v.wait_ge(scat[q], 8 * (i - 1 - q))
                    v.tensor_scalar(xr[:, q, :], x[:, bass.ds(i - 1, 1), :].rearrange("p b d -> p (b d)"),
                                    mv1[:, q, 0:1], rst[:, q, 1:2], ALU.subtract, ALU.mult).then_inc(xr_norm, 1)

                steps(v, 3, 28, B, 2, body)

            @block.gpsimd
            def _(pool):
                def body(i, p):
                    q = 1 - p
                    if inside(i, 1):
                        alone(pool, tick, (q_exp, i + 2))
                        pool.tensor_copy(qb[:, q, 0:512], qf[:, q, 0:512]).then_inc(qk_cast, 1)
                        alone(pool, tick, (k_exp, i + 2))
                        pool.tensor_copy(kb[:, q, :], kf[:, q, :]).then_inc(qk_cast, 1)
                        reached(pool, x1_done, i)
                        pool.tensor_tensor(xpb[:, q, :], x[:, bass.ds(i + 1, 1), :].rearrange("p b d -> p (b d)"),
                                           fcb[:], ALU.add).then_inc(xpb_done, 1)
                    if inside(i, 2):
                        if at_step(i, -2):
                            pool.wait_ge(ld_x0, 32)
                        elif at_step(i, 0):
                            pool.wait_ge(ld_x, 32)
                        reached(pool, tf_done, i + 1)
                        pool.tensor_copy(cn[:, p, :], cx[:, bass.ds(i + 2, 1), :].rearrange(
                            "p b d -> p (b d)")).then_inc(c_copy, 1)
                        alone(pool, tick, (x_stat, 2 * (i + 2) + 2), (x_norm, i + 1))
                        pool.tensor_scalar(rstt[:, 0:1], mv[:, p, 1:2], EPS, None, ALU.add).then_inc(x_rstd, 1)
                        pool.wait_ge(x_rstd, 2 * (i + 2) + 1)
                        pool.tensor_tensor(rst[:, p, 0:1], rstt[:, 0:1], halves[:, 0:1], ALU.pow).then_inc(x_rstd, 1)
                    if inside(i, -1):
                        alone(pool, tick, (chain, 10 * i))
                        pool.tensor_copy(slot[:, bass.ds(i - 1, 1), 0:1].rearrange("p a b -> p (a b)"),
                                         slotp[:, q, 0:1]).then_inc(kept0, 1)
                        pool.indirect_dma_start(xs[0], bass.IndirectOffsetOnAxis(ap=slotp[:, q, 0:1], axis=0),
                                                xr[:, q, :], None).then_inc(scat[q], 16)
                    if inside(i, 0):
                        alone(pool, tick, (xr_stat, 2 * i + 2))
                        pool.tensor_scalar(rstt[:, 1:2], mv1[:, p, 1:2], EPS, None, ALU.add).then_inc(xr_rstd, 1)
                        pool.wait_ge(xr_rstd, 2 * i + 1)
                        pool.tensor_tensor(rst[:, p, 1:2], rstt[:, 1:2], halves[:, 0:1], ALU.pow).then_inc(xr_rstd, 1)

                steps(pool, 3, 28, B, 2, body)

        def table_and_pads(layer, NT, tag):
            tab, pads = sem(tag + "tab"), sem(tag + "pads")
            gt = sem(tag + "gates")
            ge = sem(tag + "gate_exp")
            with nc.Block() as block:
                @block.vector
                def _(v):
                    count = [0]

                    def step(ins):
                        count[0] += 1
                        ins.then_inc(tab, 1)
                        v.wait_ge(tab, count[0])

                    n, tl, cum, dd = (tcnt[:, k, :] for k in range(4))
                    step(v.tensor_scalar(pos[:], base[:], cst[:, K_PART:K_PART + 1], None, ALU.add))
                    step(v.tensor_copy(padidx[:], pos[:]))
                    v.memset(junk[:], 1.0).then_inc(gt, 1)
                    step(v.tensor_tensor(n, base[:], cst[:, K_EOFF:K_EOFF + E], ALU.subtract))
                    step(v.tensor_scalar(n, n, 127.0, None, ALU.add))
                    step(v.tensor_copy(tint[:], n))
                    step(v.tensor_scalar(tint[:], tint[:], 7, None, ALU.arith_shift_right))
                    step(v.tensor_copy(tl, tint[:]))
                    v.wait_ge(gt, 1)
                    step(v.tensor_tensor_scan(cum, junk[:], tl, 0.0, ALU.mult, ALU.add))
                    step(v.tensor_scalar(dd, tl, -128.0, float(REGION), ALU.mult, ALU.add))
                    t = cst[0:1, K_TILE:K_TILE + NT]
                    ex, row, s1 = (trow[:, k, 0:NT] for k in range(3))
                    step(v.memset(ex, 0.0))
                    step(v.tensor_scalar(row, t, 128.0, None, ALU.mult))
                    for e in range(E):
                        step(v.scalar_tensor_tensor(out=ex, in0=t, scalar=cum[0:1, e:e + 1], in1=ex,
                                                    op0=ALU.is_ge, op1=ALU.add))
                        step(v.tensor_scalar(s1, t, cum[0:1, e:e + 1], dd[0:1, e:e + 1], ALU.is_ge, ALU.mult))
                        step(v.tensor_tensor(row, row, s1, ALU.add))
                    step(v.tensor_scalar(s1, ex, float(E - 1), None, ALU.min))
                    step(v.tensor_copy(etab[:, 0:NT], s1))
                    step(v.tensor_scalar(s1, row, float(DUMMY), None, ALU.min))
                    step(v.tensor_copy(rtab[:, 0:NT], s1))
                    dl, diff = tcnt[:, 4, :], tcnt[:, 5, :]
                    step(v.tensor_tensor(dl, cum, tl, ALU.subtract))
                    step(v.scalar_tensor_tensor(out=dl, in0=dl, scalar=128.0, in1=cst[:, K_EOFF:K_EOFF + E],
                                                op0=ALU.mult, op1=ALU.subtract))
                    step(v.tensor_tensor(diff[:, 1:E], dl[:, 1:E], dl[:, 0:E - 1], ALU.subtract))
                    part = slice(0, 1 + layer)
                    step(v.tensor_copy(slotf[:, :, part], slot[:, :, part]))
                    step(v.tensor_copy(slott[:, 1, :, part], slotf[:, :, part]))
                    for e in range(1, E):
                        step(v.tensor_scalar(slott[:, 0, :, part], slotf[:, :, part], float(e * REGION),
                                             diff[:, e:e + 1], ALU.is_ge, ALU.mult))
                        step(v.tensor_tensor(slott[:, 1, :, part], slott[:, 1, :, part], slott[:, 0, :, part], ALU.add))
                    step(v.tensor_copy(slot[:, :, part], slott[:, 1, :, part]))
                    step(v.tensor_copy(base[:], cst[:, K_EOFF:K_EOFF + E]))
                    if layer == 0:
                        step(v.reciprocal(gate[:, 0, :], gsum[:]))
                    else:
                        v.wait_ge(ge, 1)
                        step(v.tensor_scalar(gsum[:], gate[:, 1, :], 1.0, None, ALU.add))
                        step(v.reciprocal(gate[:, 0, :], gsum[:]))
                        step(v.tensor_tensor(gate[:, 1, :], gate[:, 1, :], gate[:, 0, :], ALU.mult))

                if layer == 1:
                    @block.scalar
                    def _(act):
                        act.activation(gate[:, 1, :], gsum[:], ACT.Exp).then_inc(ge, 1)

                @block.gpsimd
                def _(pool):
                    pool.dma_start(xs[layer][DUMMY:DUMMY + 128, :], zero[:]).then_inc(pads, 16)
                    pool.wait_ge(tab, 2)
                    for e in range(E):
                        pool.indirect_dma_start(xs[layer], bass.IndirectOffsetOnAxis(ap=padidx[:, e:e + 1], axis=0),
                                                zero[:], None).then_inc(pads, 16)
                    pool.wait_ge(pads, 16 * (E + 1))
                    if layer == 0:
                        for q in range(2):
                            pool.wait_ge(scat[q], 8 * B)
                    else:
                        for q in range(2):
                            pool.wait_ge(scat2[q], 16 * B)

        table_and_pads(0, NT0, "t0_")

        def experts(layer, NT, tag):
            last = NT - 3
            x_in = [sem(f"{tag}x_in{k}") for k in range(4)]
            y_out = [sem(f"{tag}y_out{k}") for k in range(4)]
            (t_done, t_out, h_done, hb_done, g_done, ht_done, ht_out, y_done, y_sb) = (
                sem(tag + n) for n in ("t_done", "t_out", "h_done", "hb_done", "g_done", "ht_done", "ht_out",
                                       "y_done", "y_sb"))
            ld = (ld_moe0, 64) if layer == 0 else (ld_moe1, 32)
            with nc.Block() as block:
                @block.sync
                def _(sp):
                    def load(t, k):
                        r = sp.value_load(rtab[0:1, bass.ds(t, 1)], min_val=0, max_val=DUMMY)
                        reached(sp, t_done, t - 3)
                        sp.dma_start(xt[:, k, :], xs[layer][bass.ds(r, 128), :]).then_inc(x_in[k], 16)

                    def body(t, k):
                        if at_step(t, -2):
                            load(0, 0)
                            load(1, 1)
                        if inside(t, 4, NT):
                            load(t + 4, k)

                    steps(sp, 5, last - 4, NT, 4, body)

                @block.gpsimd
                def _(pool):
                    def body(t, k):
                        if inside(t, -1, NT):
                            k1 = (k - 1) % 4
                            pool.wait_ge(y_sb, t)
                            pool.dma_start(ys[layer][bass.ds((t - 1) * 128, 128), :],
                                           yo[:, k1, :]).then_inc(y_out[k1], 16)

                    steps(pool, 5, last, NT, 4, body)
                    for k in range(4):
                        pool.wait_ge(y_out[k], 16 * len(range(k, NT, 4)))

                @block.tensor
                def _(pe):
                    def body(t, k):
                        p = k % 2
                        if inside(t, 2, NT):
                            k2 = (k + 2) % 4
                            pe.wait_ge(x_in[k2], 4 * (t + 2 - k2) + 16)
                            reached(pe, t_out, t + 1)
                            pe.transpose(bank[6 + p][:, 0:128], xt[:, k2, :], ident).then_inc(t_done, 1)
                        if inside(t, 1, NT):
                            if at_step(t, -1):
                                pe.wait_ge(*ld)
                            e = pe.value_load(etab[0:1, bass.ds(t + 1, 1)], min_val=0, max_val=E - 1)
                            reached(pe, (hb_done if layer == 0 else g_done), t)
                            pe.wait_ge(t_out, t + 2)
                            pe.matmul(bank[1 - p][:, :], xtT[:, 1 - p, :],
                                      w1[:].rearrange("p e f -> p (e f)")[:, bass.ds(e * F, F)],
                                      start=True, stop=True).then_inc(h_done, 1)
                        if inside(t, -1, NT):
                            e = pe.value_load(etab[0:1, bass.ds(t - 1, 1)], min_val=0, max_val=E - 1)
                            pe.wait_ge(ht_out, t)
                            reached(pe, y_sb, t - 2)
                            for c in range(FC):
                                mm = pe.matmul(bank[5 - p][:, 0:D], hT[:, 1 - p, 128 * c:128 * c + 128],
                                               w2[:].rearrange("p e c d -> p (e c d)")[:, bass.ds(e * F + c * D, D)],
                                               start=(c == 0), stop=(c == FC - 1))
                            mm.then_inc(y_done, 1)
                        if inside(t, 0, NT):
                            pe.wait_ge(g_done, t + 1)
                            reached(pe, ht_out, t - 1)
                            for c in range(FC):
                                mm = pe.transpose(bank[2 + p][:, 128 * c:128 * c + 128],
                                                  hg[:, p, 128 * c:128 * c + 128], ident)
                            mm.then_inc(ht_done, 1)

                    steps(pe, 5, last, NT, 4, body)

                @block.scalar
                def _(act):
                    def body(t, k):
                        p = k % 2
                        if inside(t, 2, NT):
                            act.wait_ge(t_done, t + 3)
                            reached(act, h_done, t + 1)
                            act.activation(xtT[:, p, :], bank[6 + p][:, 0:128], ACT.Copy).then_inc(t_out, 1)
                        if inside(t, 1, NT):
                            reached(act, ht_done, t)
                            if layer == 0:
                                act.wait_ge(hb_done, t + 2)
                                act.activation(hg[:, 1 - p, :], hb[:, 1 - p, :], ACT.Gelu).then_inc(g_done, 1)
                            else:
                                act.wait_ge(h_done, t + 2)
                                act.activation(hg[:, 1 - p, :], bank[1 - p][:, :], ACT.Gelu).then_inc(g_done, 1)

                    steps(act, 5, last, NT, 4, body)

                @block.vector
                def _(v):
                    def body(t, k):
                        p = k % 2
                        if inside(t, 1, NT) and layer == 0:
                            if at_step(t, -1):
                                v.wait_ge(ld_moe0, 64)
                            e = v.value_load(etab[0:1, bass.ds(t + 1, 1)], min_val=0, max_val=E - 1)
                            reached(v, g_done, t)
                            v.wait_ge(h_done, t + 2)
                            v.tensor_tensor(hb[:, 1 - p, :], bank[1 - p][:, :],
                                            b1[:].rearrange("p e f -> p (e f)")[:, bass.ds(e * F, F)],
                                            ALU.add).then_inc(hb_done, 1)
                        if inside(t, -1, NT):
                            if layer == 0:
                                e = v.value_load(etab[0:1, bass.ds(t - 1, 1)], min_val=0, max_val=E - 1)
                            v.wait_ge(y_done, t)
                            k1 = (k - 1) % 4
                            if inside(t, -5, NT):
                                v.wait_ge(y_out[k1], 4 * (t - 1 - k1))
                            if layer == 0:
                                v.tensor_tensor(yo[:, k1, :], bank[5 - p][:, 0:D],
                                                b2[:].rearrange("p e d -> p (e d)")[:, bass.ds(e * D, D)],
                                                ALU.add).then_inc(y_sb, 1)
                            else:
                                v.tensor_copy(yo[:, k1, :], bank[5 - p][:, 0:D]).then_inc(y_sb, 1)
                        if inside(t, 0, NT):
                            v.wait_ge(ht_done, t + 1)
                            reached(v, y_done, t - 1)
                            v.tensor_copy(hT[:, p, :], bank[2 + p][:, :]).then_inc(ht_out, 1)

                    steps(v, 5, last, NT, 4, body)

        experts(0, NT0, "e0_")

        scat2 = [sem(f"b_scat{p}") for p in range(2)]
        gidx = sb("gidx", [128, 2, 2], U32)
        gi_done, gi2_done = sem("gi_done"), sem("gi2_done")
        gath = [sem(f"b_gath{p}") for p in range(2)]
        (x2_done, x_stat, c_stat, x_rstd, x_norm, c_norm, tf_done, tf_out, q_done, q_out, kv_done, kv_out,
         qk_cast) = (sem("b_" + n) for n in (
             "x2_done", "x_stat", "c_stat", "x_rstd", "x_norm", "c_norm", "tf_done", "tf_out", "q_done", "q_out",
             "kv_done", "kv_out", "qk_cast"))
        q_out_v = sem("b_q_out_v")
        (sm_done, max_done, mt_done, mt_out, st_done, p_exp, pv_done, rec_done, on_done, ot_done, ot_out,
         ff_done, g_exp, s_step, x3_done, acc_done) = (sem("b_" + n) for n in (
             "sm_done", "max_done", "mt_done", "mt_out", "st_done", "p_exp", "pv_done", "rec_done", "on_done",
             "ot_done", "ot_out", "ff_done", "g_exp", "s_step", "x3_done", "acc_done"))
        ot_out_v = sem("b_ot_out_v")
        (xr_stat, xr_rstd, xr_norm, tr_done, tr_out, lg_done, rk_done, chain) = (sem("b_" + n) for n in (
            "xr_stat", "xr_rstd", "xr_norm", "tr_done", "tr_out", "lg_done", "rk_done", "chain"))
        K1 = 13
        kept1 = sem("b_kept")
        ROUTE1 = dict(logits=bank[7][:, 128:128 + E], ranks=bank[7][:, 256:256 + E],
                      totals=bank[7][:, 384:384 + E], chain=chain, kept=kept1, K=K1)

        with nc.Block() as block:
            @block.sync
            def _(sp):
                sp.dma_start(w1[:], A["w1_1"]).then_inc(ld_moe1, 16)
                sp.dma_start(w2[:], A["w2_1"]).then_inc(ld_moe1, 16)

            @block.tensor
            def _(pe):
                mtp = bank[7][:, 0:64].bitcast(BF16)

                def body(i, p):
                    q = 1 - p
                    if inside(i, 0):
                        pe.wait_ge(qk_cast, 3 * i + 3)
                        for k in range(4):
                            r, c0 = 64 * (k // 2), 4 * (k % 2)
                            if k == 0:
                                reached(pe, x3_done, i)
                            else:
                                reached(pe, on_done, 4 * i - 4 + k + 1)
                            for c in range(4):
                                mm = pe.matmul(bank[k][:, C * c:C * c + C],
                                               qb[r:r + 64, p, 128 * (c0 + c):128 * (c0 + c) + 128],
                                               kb[r:r + 64, p, 0:C], start=True, stop=True)
                            mm.then_inc(sm_done, 1)
                    if inside(i, 1):
                        pe.wait_ge(x_norm, i + 2)
                        pe.wait_ge(c_norm, i + 2)
                        reached(pe, ot_out, i)
                        pe.transpose(bank[7][:, 0:128], xn[:, q, :], ident)
                        pe.transpose(bank[7][:, 128:128 + C], cn[:, q, :], ident[0:C, 0:C]).then_inc(tf_done, 1)
                        pe.wait_ge(tf_out, 2 * i + 4)
                        reached(pe, s_step, 4 * i)
                        for k in range(2):
                            for c in range(4):
                                mm = pe.matmul(bank[4 + k][:, 128 * c:128 * c + 128],
                                               wq[:, 128 * (4 * k + c):128 * (4 * k + c) + 128], xcT[:, q, 0:128],
                                               start=True, stop=True)
                            mm.then_inc(q_done, 1)
                        reached(pe, ot_out_v, i)
                        pe.matmul(bank[6][:, 0:C], wk2[:].rearrange("p a b -> p (a b)"), xcT[:, q, 128:128 + C],
                                  start=True, stop=True)
                        pe.matmul(bank[6][0:C, 128:128 + HD1], xcT[:, q, 128:128 + C], wv1[:], start=True,
                                  stop=True).then_inc(kv_done, 1)
                    if inside(i, 0):
                        pe.wait_ge(max_done, 4 * i + 4)
                        pe.transpose(mtp, mx[:], identb[:]).then_inc(mt_done, 1)
                    if inside(i, -1):
                        pe.wait_ge(xr_norm, i)
                        if inside(i, 0):
                            pe.wait_ge(mt_out, i + 1)
                        pe.transpose(bank[7][:, 0:128], xr[:, q, :], ident).then_inc(tr_done, 1)

                    def st(k):
                        r, c0 = 64 * (k // 2), 4 * (k % 2)
                        for c in range(4):
                            o = bank[k][0:C, 128 * c:128 * c + 128]
                            pe.matmul(o, kf[r:r + 64, p, 0:C],
                                      qf[r:r + 64, p, 128 * (c0 + c):128 * (c0 + c) + 128], start=True, stop=False)
                            mm = pe.matmul(o, sel1[r:r + 64, c0 + c, :], mT[r:r + 64, :], start=False, stop=True)
                        mm.then_inc(st_done, 1)

                    def pv(k):
                        pe.wait_ge(p_exp, 4 * i + k + 1)
                        for c in range(4):
                            mm = pe.matmul(bank[k][:, 65 * c:65 * c + 65], PT[:, k, 128 * c:128 * c + 128],
                                           v1[:, p, :], start=True, stop=True)
                        mm.then_inc(pv_done, 1)

                    if inside(i, 0):
                        pe.wait_ge(mt_out, i + 1)
                        st(0)
                        st(1)
                    if inside(i, -1):
                        pe.wait_ge(tr_out, i)
                        pe.matmul(ROUTE1["logits"], xrT[:], router[1][:], start=True, stop=True).then_inc(lg_done, 1)
                    if inside(i, 0):
                        pv(0)
                        st(2)
                        pv(1)
                        st(3)
                        pv(2)
                        nx = i + 1 if inside(i, 1) else i
                        pe.wait_ge(q_out, nx + 1)
                        pe.wait_ge(q_out_v, nx + 1)
                        for k, half in enumerate((1, 0)):
                            for c in range(FC):
                                mm = pe.matmul(bank[4 + k][:, 128 * c:128 * c + 128],
                                               wf1[:, half, 128 * c:128 * c + 128], xcT[:, p, 0:128],
                                               start=True, stop=True)
                            mm.then_inc(ff_done, 1)
                    if inside(i, -1):
                        pe.wait_ge(chain, K1 * (i - 1) + 8)
                        pe.matmul(ROUTE1["ranks"], trib[:], hot[:, 2, :], start=True, stop=True)
                        pe.matmul(ROUTE1["totals"], oneb[:], hot[:, 2, :], start=True, stop=True).then_inc(rk_done, 1)
                    if inside(i, 0):
                        pv(3)
                        pe.wait_ge(on_done, 4 * i + 4)
                        if inside(i, 1):
                            pe.wait_ge(kv_out, 2 * i + 4)
                        for c in range(4):
                            mm = pe.transpose(bank[6][:, 128 * c:128 * c + 128], on[:, 512 + 128 * c:512 + 128 * c + 128], ident)
                        mm.then_inc(ot_done, 1)
                        if inside(i, -1):
                            pe.wait_ge(chain, K1 * i)
                        for c in range(4):
                            mm = pe.transpose(bank[7][:, 128 * c:128 * c + 128], on[:, 128 * c:128 * c + 128], ident)
                        mm.then_inc(ot_done, 1)
                        pe.wait_ge(s_step, 4 * i + 4)
                        for c in range(FC):
                            pe.matmul(bank[0][:, 0:D], sg[:, 2, 128 * c:128 * c + 128], wf2[:, c, :],
                                      start=(c == 0), stop=False)
                        pe.wait_ge(ot_out, i + 1)
                        pe.wait_ge(ot_out_v, i + 1)
                        for c in range(8):
                            mm = pe.matmul(bank[0][:, 0:D], oT[:, 128 * c:128 * c + 128], wo[:, c, :],
                                           start=False, stop=(c == 7))
                        mm.then_inc(acc_done, 1)

                pe.wait_ge(ld_w1, 144)
                steps(pe, 3, 28, B, 2, body)

            @block.scalar
            def _(act):
                def evac_r(i):
                    act.wait_ge(tr_done, i)
                    act.activation(xrT[:], bank[7][:, 0:128], ACT.Copy).then_inc(tr_out, 1)

                def body(i, p):
                    q = 1 - p
                    if inside(i, 1):
                        act.wait_ge(tf_done, i + 2)
                        act.activation(xcT[:, q, 0:128], bank[7][:, 0:128], ACT.Identity, bias=lnp[:, 1:2],
                                       scale=lnp[:, 0:1]).then_inc(tf_out, 1)
                        act.activation(xcT[:, q, 128:128 + C], bank[7][:, 128:128 + C], ACT.Identity,
                                       bias=lnp[:, 3:4], scale=lnp[:, 2:3]).then_inc(tf_out, 1)
                        act.wait_ge(q_done, 2 * i + 3)
                        act.activation(qf[:, q, 0:512], bank[4][:, :], ACT.Copy).then_inc(q_out, 1)
                        act.wait_ge(kv_done, i + 2)
                        act.activation(kf[:, q, 0:C], bank[6][:, 0:C], ACT.Copy).then_inc(kv_out, 1)
                        act.activation(v1[:, q, 0:HD1], bank[6][0:C, 128:128 + HD1], ACT.Copy).then_inc(kv_out, 1)
                    if inside(i, 0):
                        for k in range(4):
                            act.wait_ge(st_done, 4 * i + k + 1)
                            act.activation(PT[:, k, :], bank[k][0:C, :], ACT.Exp,
                                           scale=float(HD1) ** -0.5).then_inc(p_exp, 1)
                            if k == 0 and inside(i, -1):
                                evac_r(i)
                        act.wait_ge(ff_done, 2 * i + 1)
                        act.activation(sg[:, 0, :], bank[4][:, :], ACT.Exp, scale=-1.0).then_inc(g_exp, 1)
                        act.wait_ge(ot_done, 2 * i + 2)
                        act.activation(oT[:, 0:512], bank[7][:, :], ACT.Copy).then_inc(ot_out, 1)
                    elif inside(i, -1):
                        evac_r(i)

                if True:
                    act.wait_ge(ld_w1, 144)
                steps(act, 3, 28, B, 2, body)

            @block.vector
            def _(v):
                def norm_r(i, q):
                    v.wait_ge(xr_rstd, 2 * i)
                    if inside(i, -3):
                        v.wait_ge(scat2[q], 16 * (i - 1 - q))
                    v.tensor_scalar(xr[:, q, :], x[:, bass.ds(i - 1, 1), :].rearrange("p b d -> p (b d)"),
                                    mv1[:, q, 0:1], rst[:, q, 1:2], ALU.subtract, ALU.mult).then_inc(xr_norm, 1)

                def body(i, p):
                    q = 1 - p
                    if inside(i, 0):
                        for k in range(4):
                            v.wait_ge(sm_done, 4 * i + k + 1)
                            reached(v, mt_done, i)
                            m0 = 64 * (k // 2) + 4 * (k % 2)
                            v.tensor_reduce(mx[:, m0:m0 + 4], bank[k][:, 0:4 * C].rearrange("p (g k) -> p g k", g=4),
                                            AX, ALU.max).then_inc(max_done, 1)
                            if k == 1 and inside(i, -1):
                                norm_r(i, q)
                    elif inside(i, -1):
                        norm_r(i, q)
                    if inside(i, 0):
                        v.wait_ge(mt_done, i + 1)
                        v.tensor_copy(mT[:], bank[7][:, 0:64].bitcast(BF16)).then_inc(mt_out, 1)
                    if inside(i, 1):
                        v.wait_ge(q_done, 2 * i + 4)
                        v.tensor_copy(qf[:, q, 512:1024], bank[5][:, :]).then_inc(q_out_v, 1)
                    if inside(i, 2):
                        xi = x[:, bass.ds(i + 2, 1), :].rearrange("p b d -> p (b d)")
                        ci = cx[:, bass.ds(i + 2, 1), :].rearrange("p b d -> p (b d)")
                        v.wait_ge(gath[p], 8 * (i + 2 - p) + 16)
                        v.scalar_tensor_tensor(out=xi, in0=yg[:, p, 0, :], scalar=gate[:, 0, bass.ds(i + 2, 1)],
                                               in1=xi, op0=ALU.mult, op1=ALU.add).then_inc(x2_done, 1)
                        v.bn_stats(st6[0:C, 2, :], ci).then_inc(c_stat, 1)
                        alone(v, tick, (x2_done, i + 3))
                        v.bn_stats(st6[:, 0, :], xi).then_inc(x_stat, 1)
                        alone(v, tick, (c_stat, 2 * (i + 2) + 1))
                        v.bn_aggr(mvc[0:C, p, :], st6[0:C, 2, :]).then_inc(c_stat, 1)
                        alone(v, tick, (x_stat, 2 * (i + 2) + 1))
                        v.bn_aggr(mv[:, p, :], st6[:, 0, :]).then_inc(x_stat, 1)
                    if inside(i, -1):
                        v.wait_ge(lg_done, i)
                        route(1, v, q, i - 1, ROUTE1, 0)
                    if inside(i, 2):
                        reached(v, tf_done, i + 1)
                        v.wait_ge(x_rstd, 4 * (i + 2) + 4)
                        v.tensor_scalar(xn[:, p, :], xi, mv[:, p, 0:1], rst[:, p, 0:1], ALU.subtract,
                                        ALU.mult).then_inc(x_norm, 1)
                        v.tensor_scalar(cn[:, p, :], ci, mvc[0:C, p, 0:1], rst[0:C, p, 2:3], ALU.subtract,
                                        ALU.mult).then_inc(c_norm, 1)

                    def norm_o(k):
                        r, c0 = k // 2, 4 * (k % 2)
                        o = bank[k][:, 0:4 * 65].rearrange("p (c e) -> p c e", e=65)
                        rk = rec[:, 4 * k:4 * k + 4].rearrange("p (c e) -> p c e", e=1)
                        v.wait_ge(pv_done, 4 * i + k + 1)
                        v.reciprocal(rk, o[:, :, 64:65]).then_inc(rec_done, 1)
                        v.wait_ge(rec_done, 4 * i + k + 1)
                        if k == 0:
                            reached(v, ot_done, 2 * i)
                        dst = on[:].rearrange("p (c r e) -> p c r e", c=8, r=2)[:, c0:c0 + 4, r, :]
                        v.tensor_tensor(dst, o[:, :, 0:64], rk.broadcast_to([128, 4, 64]),
                                        ALU.mult).then_inc(on_done, 1)

                    if inside(i, 0):
                        norm_o(0)
                        norm_o(1)
                        norm_o(2)
                    if inside(i, -1):
                        v.wait_ge(rk_done, i)
                        route(1, v, q, i - 1, ROUTE1, 1)
                    if inside(i, 0):
                        norm_o(3)
                        v.wait_ge(g_exp, i + 1)
                        v.tensor_scalar(sg[:, 0, :], sg[:, 0, :], 1.0, None, ALU.add).then_inc(s_step, 1)
                        v.wait_ge(s_step, 4 * i + 1)
                        v.reciprocal(sg[:, 1, :], sg[:, 0, :]).then_inc(s_step, 1)
                        v.wait_ge(s_step, 4 * i + 2)
                        v.tensor_tensor(sg[:, 1, :], bank[4][:, :], sg[:, 1, :], ALU.mult).then_inc(s_step, 1)
                        v.wait_ge(s_step, 4 * i + 3)
                        v.wait_ge(ff_done, 2 * i + 2)
                        reached(v, acc_done, i)
                        v.tensor_tensor(sg[:, 2, :], bank[5][:, :], sg[:, 1, :], ALU.mult).then_inc(s_step, 1)
                        v.wait_ge(ot_done, 2 * i + 1)
                        v.tensor_copy(oT[:, 512:1024], bank[6][:, :]).then_inc(ot_out_v, 1)
                        v.wait_ge(acc_done, i + 1)
                        xo = x[:, bass.ds(i, 1), :].rearrange("p b d -> p (b d)")
                        v.tensor_tensor(xo, bank[0][:, 0:D], xo, ALU.add).then_inc(x3_done, 1)
                        alone(v, tick, (x3_done, i + 1))
                        v.bn_stats(st6[:, 1, :], xo).then_inc(xr_stat, 1)
                        alone(v, tick, (xr_stat, 2 * i + 1))
                        v.bn_aggr(mv1[:, p, :], st6[:, 1, :]).then_inc(xr_stat, 1)

                steps(v, 3, 28, B, 2, body)

            @block.gpsimd
            def _(pool):
                def gather(b, p):
                    pool.tensor_copy(gidx[:, p, 0:1], slot[:, bass.ds(b, 1), 0:1].rearrange(
                        "p a b -> p (a b)")).then_inc(gi_done, 1)
                    alone(pool, tick, (gi_done, b + 1))
                    pool.indirect_dma_start(yg[:, p, 0, :], None, ys[0], bass.IndirectOffsetOnAxis(
                        ap=gidx[:, p, 0:1], axis=0)).then_inc(gath[p], 16)

                def body(i, p):
                    q = 1 - p
                    if at_step(i, -2):
                        gather(0, 0)
                        gather(1, 1)
                    if inside(i, 1):
                        alone(pool, tick, (kv_out, 2 * i + 3))
                        pool.tensor_copy(kb[:, q, 0:C], kf[:, q, 0:C]).then_inc(qk_cast, 1)
                        alone(pool, tick, (q_out, i + 2))
                        pool.tensor_copy(qb[:, q, 0:512], qf[:, q, 0:512]).then_inc(qk_cast, 1)
                        alone(pool, tick, (q_out_v, i + 2))
                        pool.tensor_copy(qb[:, q, 512:1024], qf[:, q, 512:1024]).then_inc(qk_cast, 1)
                    if inside(i, 2):
                        alone(pool, tick, (x_stat, 2 * (i + 2) + 2), (c_stat, 2 * (i + 2) + 2))
                        pool.tensor_scalar(rstt[:, 0:1], mv[:, p, 1:2], 1.0 + EPS, EPS * EPS, ALU.mult,
                                           ALU.add).then_inc(x_rstd, 1)
                        pool.tensor_scalar(rstt[0:C, 2:3], mvc[0:C, p, 1:2], EPS, None, ALU.add).then_inc(x_rstd, 1)
                        pool.wait_ge(x_rstd, 4 * (i + 2) + 2)
                        pool.tensor_tensor(rst[:, p, 0:1], rstt[:, 0:1], halves[:, 0:1], ALU.pow).then_inc(x_rstd, 1)
                        pool.tensor_tensor(rst[0:C, p, 2:3], rstt[0:C, 2:3], halves[0:C, 0:1],
                                           ALU.pow).then_inc(x_rstd, 1)
                    if inside(i, 4):
                        pool.wait_ge(x2_done, i + 3)
                        gather(i + 4, p)
                    if inside(i, -1):
                        alone(pool, tick, (chain, K1 * i))
                        pool.tensor_copy(slot[:, bass.ds(i - 1, 1), :].rearrange("p a b -> p (a b)"),
                                         slotp[:, q, :]).then_inc(kept1, 1)
                        for n in range(2):
                            pool.indirect_dma_start(xs[1], bass.IndirectOffsetOnAxis(ap=slotp[:, q, n:n + 1], axis=0),
                                                    xr[:, q, :], None).then_inc(scat2[q], 16)
                    if inside(i, 0):
                        alone(pool, tick, (xr_stat, 2 * i + 2))
                        pool.tensor_scalar(rstt[:, 1:2], mv1[:, p, 1:2], EPS, None, ALU.add).then_inc(xr_rstd, 1)
                        pool.wait_ge(xr_rstd, 2 * i + 1)
                        pool.tensor_tensor(rst[:, p, 1:2], rstt[:, 1:2], halves[:, 0:1], ALU.pow).then_inc(xr_rstd, 1)

                steps(pool, 3, 26, B, 2, body)

        table_and_pads(1, NT1, "t1_")
        experts(1, NT1, "e1_")

        gath2 = [sem(f"c_gath{p}") for p in range(2)]
        o_step, o_store = sem("o_step"), sem("o_store")
        with nc.Block() as block:
            @block.gpsimd
            def _(pool):
                def body(b, p):
                    alone(pool, tick, (o_step, 2 * b - 2))
                    pool.tensor_copy(gidx[:, p, :], slot[:, bass.ds(b, 1), :].rearrange(
                        "p a b -> p (a b)")).then_inc(gi2_done, 1)
                    alone(pool, tick, (gi2_done, b + 1))
                    for n in range(2):
                        pool.indirect_dma_start(yg[:, p, n, :], None, ys[1], bass.IndirectOffsetOnAxis(
                            ap=gidx[:, p, n:n + 1], axis=0)).then_inc(gath2[p], 16)

                body(0, 0)
                body(1, 1)
                with pool.Fori(2, B - 1, 2) as b:
                    body(b, 0)
                    body(b + 1, 1)

            @block.vector
            def _(v):
                with v.Fori(0, B - 1, 2) as b0:
                    for p in range(2):
                        b = b0 + p if p else b0
                        xi = x[:, bass.ds(b, 1), :].rearrange("p b d -> p (b d)")
                        v.wait_ge(gath2[p], 16 * b0 + 32)
                        v.scalar_tensor_tensor(out=xi, in0=yg[:, p, 0, :], scalar=gate[:, 0, bass.ds(b, 1)], in1=xi,
                                               op0=ALU.mult, op1=ALU.add).then_inc(o_step, 1)
                        v.wait_ge(o_step, 2 * b + 1)
                        v.scalar_tensor_tensor(out=xi, in0=yg[:, p, 1, :], scalar=gate[:, 1, bass.ds(b, 1)], in1=xi,
                                               op0=ALU.mult, op1=ALU.add).then_inc(o_step, 1)

            @block.sync
            def _(sp):
                for n in range(8):
                    sp.wait_ge(o_step, 8 * n + 8)
                    sp.dma_start(A["out"][:, 4 * n:4 * n + 4, :], x[:, 4 * n:4 * n + 4, :]).then_inc(o_store, 16)
                sp.wait_ge(o_store, 128)


def shape_constants(np):
    k = np.zeros((128, K_N), np.float32)
    r = np.arange(128)
    k[:, K_ID:K_ID + 128] = np.eye(128)
    k[:, K_TRI:K_TRI + 128] = r[:, None] < r[None, :]
    k[:, K_ONE:K_ONE + 128] = 1
    for g in range(G):
        k[[32 * j + g for j in range(4)], K_SEL0 + C * g:K_SEL0 + C * g + C] = -1
    for c in range(8):
        k[[c, 64 + c], K_SEL1 + C * c:K_SEL1 + C * c + C] = -1
    k[:, K_SIGN:K_SIGN + 512] = np.where(np.arange(512) % 16 < 8, 1, -1)
    k[:, K_SCOL] = np.where(r % 32 < 8, 1, np.where(r % 32 < 16, -1, 1))
    k[:, K_IOTA8:K_IOTA8 + E] = np.arange(E)
    k[:, K_EOFF:K_EOFF + E] = np.arange(E) * REGION
    k[:, K_PART] = r
    k[:, K_TILE:K_TILE + NT1 + 1] = np.arange(NT1 + 1)
    return k


def kernel(x, ctx_1024, L0_xattn_fm_w, L0_xattn_fm_b, L0_xattn_fc_w, L0_xattn_fc_b, L0_ffn_w_red, L0_ffn_wg,
           L0_ffn_w1, L0_ffn_b1, L0_ffn_w2, L0_ffn_b2, L1_xattn_ln_g, L1_xattn_ln_b, L1_xattn_cln_g,
           L1_xattn_cln_b, L1_xattn_Wq, L1_xattn_Wkv, L1_xattn_Wo, L1_xattn_Wff1, L1_xattn_Wff2,
           L1_ffn_router_w, L1_ffn_w1, L1_ffn_w2):
    import numpy as np
    import concourse.bacc as bacc
    from concourse.bass_utils import run_bass_kernel_spmd

    n = np.asarray
    fm_w, fm_b = n(L0_xattn_fm_w), n(L0_xattn_fm_b)
    wz = np.zeros((D, G, 128), np.float32)
    zb = np.full((128, 1), OFF, np.float32)
    for h in range(H):
        g, j = divmod(h, 4)
        for s in range(2):
            wz[HD0 * h:HD0 * h + HD0, g, 32 * j + 8 * s:32 * j + 8 * s + 8] = fm_w.T
            zb[32 * j + 8 * s:32 * j + 8 * s + 8, 0] = fm_b
    wkv = n(L1_xattn_Wkv)
    w2_layout = lambda w: n(w).reshape(E, FC, 128, D).transpose(2, 0, 1, 3)
    arrays = dict(
        cst=shape_constants(np), x=n(x).transpose(1, 0, 2), cx=n(ctx_1024).transpose(1, 0, 2), wz=wz, zb=zb,
        vb=np.concatenate([fm_b] * H), fcw=n(L0_xattn_fc_w).T.reshape(2, 128, D).transpose(1, 0, 2),
        fcb=n(L0_xattn_fc_b), wred=n(L0_ffn_w_red).T, wg=n(L0_ffn_wg), w1_0=n(L0_ffn_w1).transpose(1, 0, 2),
        w2_0=w2_layout(L0_ffn_w2), b1=n(L0_ffn_b1), b2=n(L0_ffn_b2), wq=n(L1_xattn_Wq), wk=wkv[:, :HD1],
        wv=wkv[:, HD1:], wo=n(L1_xattn_Wo).reshape(8, 128, D).transpose(1, 0, 2),
        wf1=n(L1_xattn_Wff1).reshape(D, 2, F), wf2=n(L1_xattn_Wff2).reshape(FC, 128, D).transpose(1, 0, 2),
        lnp=np.stack([n(L1_xattn_ln_g), n(L1_xattn_ln_b), n(L1_xattn_cln_g), n(L1_xattn_cln_b)], 1),
        router=n(L1_ffn_router_w).T, w1_1=n(L1_ffn_w1).transpose(1, 0, 2), w2_1=w2_layout(L1_ffn_w2))
    arrays = {"in_" + k: np.ascontiguousarray(a) for k, a in arrays.items()}
    nc = bacc.Bacc("TRN2", target_bir_lowering=False, num_devices=1)
    A = {k[3:]: nc.dram_tensor(k, a.shape, mybir.dt.from_np(a.dtype), kind="ExternalInput").ap()
         for k, a in arrays.items()}
    A["out"] = nc.dram_tensor("out_x", (S, B, D), F32, kind="ExternalOutput").ap()
    build(nc, A)
    r = run_bass_kernel_spmd(nc, [arrays], core_ids=[0])
    return np.ascontiguousarray(r.results[0]["out_x"].transpose(1, 0, 2))
```

```python
from contextlib import ExitStack

import concourse.bass as bass
from concourse import mybir

F32 = mybir.dt.float32
BF16 = mybir.dt.bfloat16
U32 = mybir.dt.uint32
I32 = mybir.dt.int32
ALU = mybir.AluOpType
ACT = mybir.ActivationFunctionType
AX = mybir.AxisListType.X

B = 32
S = 128
D = 128
C = 120
H = 16
E = 8
F = 512
FC = F // 128
G = 4
HD0 = 8
HD1 = 64
EPS = 1e-5
OFF = -200.0

REGION = B * S + 128
DUMMY = E * REGION
NT0 = B + E - 1
NT1 = 2 * B + E - 1

K_ID, K_TRI, K_ONE, K_SEL0, K_SEL1 = 0, 128, 256, 384, 384 + G * C
K_SIGN = K_SEL1 + (H // 2) * C
K_SCOL = K_SIGN + 512
K_IOTA8 = K_SCOL + 1
K_EOFF = K_IOTA8 + E
K_PART = K_EOFF + E
K_TILE = K_PART + 1
K_QUART = K_TILE + NT1 + 1
K_N = K_QUART + 4


def reached(eng, sem, n):
    if isinstance(n, int) and n <= 0:
        return
    eng.wait_ge(sem, n)


def steps(eng, begin, first, last, end, unroll, body):
    for i in range(begin, first):
        body(i, i % unroll)
    with eng.Fori(first, last + 2 - unroll, unroll) as i:
        for u in range(unroll):
            body(i + u if u else i, (first + u) % unroll)
    for i in range(last + 1, end + 1):
        body(i, i % unroll)


def alone(eng, tick, *waits):
    if all(isinstance(n, int) for _, n in waits):
        for sem, n in waits:
            reached(eng, sem, n)
        return
    for sem, n in waits:
        reached(eng, sem, n)
    eng.sem_inc(tick[eng.engine.name], 1)


def at_step(i, n):
    return isinstance(i, int) and i == n


def inside(i, shift, n=B):
    return not isinstance(i, int) or 0 <= i + shift < n


def build(nc, A):
    ctx = ExitStack()
    with ctx:
        def sb(name, shape, dt=F32):
            return ctx.enter_context(nc.sbuf_tensor(name, shape, dt))

        def sem(name):
            return ctx.enter_context(nc.semaphore(name))

        bank = [ctx.enter_context(nc.psum_tensor(f"bank{n}", [128, 512], F32)) for n in range(8)]

        xs = [nc.dram_tensor(f"sorted{n}", (DUMMY + 128, D), F32, kind="Internal").ap() for n in range(2)]
        ys = [nc.dram_tensor(f"expert_out{n}", (NT * 128, D), F32, kind="Internal").ap()
              for n, NT in enumerate((NT0, NT1))]

        cst = sb("cst", [128, K_N])
        x = sb("x_sb", [S, B, D])
        cx = sb("cx", [C, B, D])
        wz = sb("wz", [D, G, 128])
        wv0 = sb("wv0", [D, 128])
        zbias = sb("zbias", [128, 1])
        vbias = sb("vbias", [128, 128])
        fcw = sb("fcw", [128, 2, D])
        fcb = sb("fcb", [128, D])
        wred = sb("wred", [16, D])
        wg = sb("wg", [E, 16])
        wgn = sb("wgn", [E, 16])
        wgT = sb("wgT", [16, E])
        wsq = sb("wsq", [E, 4])
        halves = sb("halves", [128, 2])
        router = [sb(f"router{n}", [D, E]) for n in range(2)]
        w1 = sb("w1", [D, E, F])
        w2 = sb("w2", [128, E, FC, D])
        shared = sb("shared", [128, E * F])
        kz = shared[:, 0:2 * 4 * G * C].rearrange("p (s j c) -> p s j c", s=2, j=4)
        b1 = shared[:].rearrange("p (e f) -> p e f", e=E)
        b2 = sb("b2", [128, E, D])
        wq = sb("wq", [D, 1024])
        wk2 = sb("wk2", [D, 2, HD1])
        wv1 = sb("wv1", [D, HD1])
        wo = sb("wo", [128, 8, D])
        wf1 = sb("wf1", [D, 2, F])
        wf2 = sb("wf2", [128, FC, D])
        lnp = sb("lnp", [D, 4])
        identb = sb("identb", [128, 128], BF16)
        trib = sb("trib", [128, 128], BF16)
        oneb = sb("oneb", [128, 128], BF16)
        sel0 = sb("sel0", [128, 4, G * C], BF16)
        sel1 = sb("sel1", [128, 8, C], BF16)
        zero = sb("zero", [128, D])
        ident = cst[:, K_ID:K_ID + 128]

        base = sb("base", [128, E])
        slot = sb("slot", [128, B, 2], U32)
        slotp = sb("slotp", [128, 2, 2], U32)
        gsum = sb("gsum", [128, B])
        gate = sb("gate", [128, 2, B])
        padidx = sb("padidx", [128, E], U32)
        tcnt = sb("tcnt", [128, 6, E])
        tint = sb("tint", [128, E], I32)
        trow = sb("trow", [1, 3, NT1])
        etab = sb("etab", [1, NT1 + 8], I32)
        rtab = sb("rtab", [1, NT1 + 8], I32)
        slotf = sb("slotf", [128, B, 2])
        slott = sb("slott", [128, 2, B, 2])

        mv = sb("mv", [128, 2, 2])
        mvc = sb("mvc", [128, 2, 2])
        st6 = sb("st6", [128, 3, 6])
        rst = sb("rst", [128, 2, 4])
        rstt = sb("rstt", [128, 4])
        mv1 = sb("mv1", [128, 2, 2])
        xn = sb("xn", [128, 2, D])
        cn = sb("cn", [C, 2, D])
        xcT = sb("xcT", [128, 2, 256])
        qf = sb("qf", [128, 2, 1024])
        kf = sb("kf", [128, 2, C])
        qb = sb("qb", [128, 2, 1024], BF16)
        kb = sb("kb", [128, 2, C], BF16)
        kb0 = sb("kb0", [128, G * C], BF16)
        vz = sb("vz", [128, 128])
        v0 = sb("v0", [C, 2, H, 17])
        v1 = sb("v1", [C, 2, HD1 + 1])
        xpb = sb("xpb", [128, 2, D])
        mx = sb("mx", [128, 128], BF16)
        mT = sb("mT", [128, 128], BF16)
        PT = sb("PT", [C, 4, 512])
        rec = sb("rec", [128, H])
        on = sb("on", [128, 1024])
        oT = sb("oT", [128, 1024])
        sg = sb("sg", [128, 3, F])
        xr = sb("xr", [128, 2, D])
        xrT = sb("xrT", [128, 128])
        lgs = sb("lgs", [128, 8])
        top = sb("top", [128, 8])
        topi = sb("topi", [128, 8], U32)
        topf = sb("topf", [128, 2])
        hot = sb("hot", [128, 3, E], BF16)
        pos = sb("pos", [128, E])
        junk = sb("junk", [128, 8])
        junk2 = sb("junk2", [128, 8])
        slf = sb("slf", [128, 2])
        negm = sb("negm", [128, 1])
        yg = sb("yg", [128, 2, 2, D])
        xt = sb("xt", [128, 4, D])
        xtT = sb("xtT", [128, 2, 128])
        hb = sb("hb", [128, 2, F])
        hg = sb("hg", [128, 2, F])
        hT = sb("hT", [128, 2, F])
        yo = sb("yo", [128, 4, D])

        ld_cst, ld_x0, ld_x, ld_w0, ld_moe0 = (sem(n) for n in ("ld_cst", "ld_x0", "ld_x", "ld_w0", "ld_moe0"))
        ld_w1, ld_moe1 = sem("ld_w1"), sem("ld_moe1")
        made = sem("made")
        tick = {"DVE": sem("tick_vector"), "Pool": sem("tick_gpsimd")}
        made_p = sem("made_p")
        made_t = sem("made_t")
        made_z = sem("made_z")

        with nc.Block() as block:
            @block.sync
            def _(sp):
                sp.dma_start(cst[:], A["cst"]).then_inc(ld_cst, 16)
                sp.dma_start(x[:, 0:2, :], A["x"][:, 0:2, :]).then_inc(ld_x0, 16)
                sp.dma_start(cx[:, 0:2, :], A["cx"][:, 0:2, :]).then_inc(ld_x0, 16)
                sp.dma_start(x[:, 2:B, :], A["x"][:, 2:B, :]).then_inc(ld_x, 16)
                sp.dma_start(cx[:, 2:B, :], A["cx"][:, 2:B, :]).then_inc(ld_x, 16)
                sp.dma_start(w1[:], A["w1_0"]).then_inc(ld_moe0, 16)
                sp.dma_start(w2[:], A["w2_0"]).then_inc(ld_moe0, 16)
                sp.dma_start(b2[:], A["b2"].partition_broadcast(128)).then_inc(ld_moe0, 16)

            @block.scalar
            def _(act):
                for dst, src in ((wz[:], A["wz"]), (zbias[:], A["zb"]), (vbias[:], A["vb"].partition_broadcast(128)),
                                 (fcw[:], A["fcw"]), (fcb[:], A["fcb"].partition_broadcast(128)),
                                 (wred[:], A["wred"]), (wg[:], A["wg"])):
                    act.dma_start(dst, src).then_inc(ld_w0, 16)
                for dst, src in ((wq[:], A["wq"]), (wk2[:, 0, :], A["wk"]), (wk2[:, 1, :], A["wk"]), (wv1[:], A["wv"]),
                                 (wo[:], A["wo"]), (wf1[:], A["wf1"]), (wf2[:], A["wf2"]), (lnp[:], A["lnp"]),
                                 (router[1][:], A["router"])):
                    act.dma_start(dst, src).then_inc(ld_w1, 16)

            @block.vector
            def _(v):
                v.memset(zero[:], 0.0).then_inc(made, 1)
                v.memset(mx[:], 0.0).then_inc(made, 1)
                v.memset(halves[:, 0:1], -0.5).then_inc(made, 1)
                v.memset(halves[:, 1:2], 0.5).then_inc(made, 1)
                v.memset(v0[:, :, :, 16:17], 1.0).then_inc(made, 1)
                v.memset(v1[:, :, HD1:HD1 + 1], 1.0).then_inc(made, 1)
                v.wait_ge(ld_cst, 16)
                v.tensor_copy(identb[:], ident).then_inc(made, 1)
                v.tensor_copy(trib[:], cst[:, K_TRI:K_TRI + 128]).then_inc(made, 1)
                v.tensor_copy(oneb[:], cst[:, K_ONE:K_ONE + 128]).then_inc(made, 1)
                for j in range(4):
                    v.tensor_scalar(sel0[:, j, :], cst[:, K_SEL0:K_SEL0 + G * C], cst[:, K_QUART + j:K_QUART + j + 1],
                                    None, ALU.mult).then_inc(made, 1)
                v.tensor_copy(sel1[:].rearrange("p a b -> p (a b)"), cst[:, K_SEL1:K_SEL1 + 8 * C]).then_inc(made, 1)
                v.tensor_copy(base[:], cst[:, K_EOFF:K_EOFF + E]).then_inc(made, 1)
                v.wait_ge(ld_w0, 112)
                v.tensor_tensor(wz[:].rearrange("p g c -> p (g c)"), wz[:].rearrange("p g c -> p (g c)"),
                                cst[:, K_SIGN:K_SIGN + 512], ALU.mult).then_inc(made, 1)
                v.tensor_tensor(zbias[:], zbias[:], cst[:, K_SCOL:K_SCOL + 1], ALU.mult).then_inc(made, 1)
                v.wait_ge(made, 17)
                v.tensor_copy(wv0[:].rearrange("p (g j e) -> p g j e", g=G, j=4),
                              wz[:].rearrange("p g (j e) -> p g j e", j=4)[:, :, :, 0:HD0]).then_inc(made, 1)
                v.tensor_tensor_reduce(wgn[:], wg[:], wg[:], 1.0, 0.0, ALU.mult, ALU.add,
                                       wsq[:, 0:1]).then_inc(made, 1)
                v.wait_ge(made_p, 1)
                v.tensor_scalar(wsq[:, 2:3], wsq[:, 1:2], 1e-4, None, ALU.max).then_inc(made, 1)
                v.wait_ge(made, 20)
                v.reciprocal(wsq[:, 3:4], wsq[:, 2:3]).then_inc(made, 1)
                v.wait_ge(made, 21)
                v.tensor_scalar(wgn[:], wg[:], wsq[:, 3:4], None, ALU.mult).then_inc(made, 1)
                v.wait_ge(made_t, 1)
                v.tensor_copy(wgT[:], bank[0][0:16, 0:E]).then_inc(made, 1)
                v.wait_ge(made_t, 2)
                v.tensor_copy(router[0][:], bank[1][:, 0:E]).then_inc(made, 1)

            @block.gpsimd
            def _(pool):
                pool.memset(kz, 0.0).then_inc(made_z, 1)
                pool.wait_ge(made, 19)
                pool.tensor_tensor(wsq[:, 1:2], wsq[:, 0:1], halves[0:E, 1:2], ALU.pow).then_inc(made_p, 1)

            @block.tensor
            def _(pe):
                pe.wait_ge(made, 22)
                pe.transpose(bank[0][0:16, 0:E], wgn[:], ident[0:E, 0:E]).then_inc(made_t, 1)
                pe.wait_ge(made, 23)
                pe.matmul(bank[1][:, 0:E], wred[:], wgT[:], start=True, stop=True).then_inc(made_t, 1)

        def route(layer, v, p, b, sems, part):
            logits, ranks, totals = sems["logits"], sems["ranks"], sems["totals"]
            chain = sems["chain"]
            K = sems["K"]
            c0 = b * K

            def after(n):
                reached(v, chain, c0 + n)

            if part == 0:
                v.tensor_copy(lgs[:], logits).then_inc(chain, 1)
                alone(v, tick, (chain, c0 + 1))
                v.max(top[:], lgs[:]).then_inc(chain, 1)
                alone(v, tick, (chain, c0 + 2))
                v.max_index(topi[:], top[:], lgs[:]).then_inc(chain, 1)
                if layer == 0:
                    v.tensor_scalar(negm[:], top[:, 0:1], -1.0, None, ALU.mult).then_inc(chain, 1)
                else:
                    v.tensor_tensor(gsum[:, bass.ds(b, 1)], top[:, 1:2], top[:, 0:1],
                                    ALU.subtract).then_inc(chain, 1)
                after(4)
                v.tensor_copy(topf[:], topi[:, 0:2]).then_inc(chain, 1)
                after(5)
                v.tensor_scalar(hot[:, 0, :], cst[:, K_IOTA8:K_IOTA8 + E], topf[:, 0:1], None,
                                ALU.is_equal).then_inc(chain, 1)
                if layer == 1:
                    v.tensor_scalar(hot[:, 1, :], cst[:, K_IOTA8:K_IOTA8 + E], topf[:, 1:2], None,
                                    ALU.is_equal).then_inc(chain, 1)
                    after(7)
                    v.tensor_tensor(hot[:, 2, :], hot[:, 0, :], hot[:, 1, :], ALU.add).then_inc(chain, 1)
            else:
                n = 6 if layer == 0 else 8
                v.tensor_tensor(pos[:], ranks, base[:], ALU.add).then_inc(chain, 1)
                after(n + 1)
                v.tensor_tensor_reduce(junk2[:], pos[:], hot[:, 0, :], 1.0, 0.0, ALU.mult, ALU.add,
                                       slf[:, 0:1]).then_inc(chain, 1)
                if layer == 1:
                    v.tensor_tensor_reduce(junk[:], pos[:], hot[:, 1, :], 1.0, 0.0, ALU.mult, ALU.add,
                                           slf[:, 1:2]).then_inc(chain, 1)
                v.tensor_tensor(base[:], base[:], totals, ALU.add).then_inc(chain, 1)
                n += 3 + layer
                after(n)
                reached(v, sems["kept"], b - 1)
                v.tensor_copy(slotp[:, p, 0:1 + layer], slf[:, 0:1 + layer]).then_inc(chain, 1)

        (x_stat, x_rstd, x_norm, tf_done, tf_out, zq_done, zk_done, zv_done, q_exp, k_exp, vz_done, v_exp,
         q_cast, xpb_done) = (sem("a_" + n) for n in (
             "x_stat", "x_rstd", "x_norm", "tf_done", "tf_out", "zq_done", "zk_done", "zv_done", "q_exp",
             "k_exp", "vz_done", "v_exp", "q_cast", "xpb_done"))
        (sm_done, max_done, mt_done, mt_out, st_done, p_exp, pv_done, rec_done, on_done, ot_done, ot_out,
         fc_done, x1_done) = (sem("a_" + n) for n in (
             "sm_done", "max_done", "mt_done", "mt_out", "st_done", "p_exp", "pv_done", "rec_done", "on_done",
             "ot_done", "ot_out", "fc_done", "x1_done"))
        (xr_stat, xr_rstd, xr_norm, tr_done, tr_out, lg_done, rk_done, chain, gexp) = (sem("a_" + n) for n in (
            "xr_stat", "xr_rstd", "xr_norm", "tr_done", "tr_out", "lg_done", "rk_done", "chain", "gexp"))
        scat = [sem(f"a_scat{p}") for p in range(2)]
        c_copy = sem("a_c_copy")
        kept0 = sem("a_kept")
        ROUTE0 = dict(logits=bank[0][:, 0:E], ranks=bank[2][:, 0:E], totals=bank[2][:, 64:64 + E], chain=chain, kept=kept0, K=10)

        with nc.Block() as block:
            @block.tensor
            def _(pe):
                mtp = bank[3][:, 0:64].bitcast(BF16)

                def body(i, p):
                    q = 1 - p
                    nxt = i + 1 if inside(i, 1) else B - 1

                    def st(j):
                        pe.wait_ge(k_exp, 5 * i + j + 2)
                        for g in range(G):
                            o = bank[j][0:C, 128 * g:128 * g + 128]
                            pe.matmul(o, kz[:, p, j, C * g:C * g + C], qf[:, p, 128 * g:128 * g + 128],
                                      start=True, stop=False)
                            mm = pe.matmul(o, sel0[:, j, C * g:C * g + C], mT[:], start=False, stop=True)
                        mm.then_inc(st_done, 1)

                    def pv(j):
                        pe.wait_ge(p_exp, 4 * i + j + 1)
                        for g in range(G):
                            h = 4 * g + j
                            mm = pe.matmul(bank[7][:, 17 * h:17 * h + 17], PT[:, j, 128 * g:128 * g + 128],
                                           v0[:, p, h, :], start=True, stop=True)
                        mm.then_inc(pv_done, 1)

                    if inside(i, 0):
                        pe.wait_ge(q_exp, i + 1)
                        pe.wait_ge(mt_out, i + 1)
                        st(0)
                        st(1)
                    if inside(i, -2):
                        pe.wait_ge(xr_norm, i - 1)
                        pe.wait_ge(q_exp, nxt + 1)
                        pe.transpose(bank[6][:, 256:384], xr[:, p, :], ident).then_inc(tr_done, 1)
                    if inside(i, -1):
                        pe.wait_ge(q_exp, nxt + 1)
                        pe.wait_ge(on_done, i)
                        for c in range(2):
                            mm = pe.transpose(bank[6][:, 128 * c:128 * c + 128], on[:, 128 * c:128 * c + 128], ident)
                        mm.then_inc(ot_done, 1)
                    if inside(i, 0):
                        pe.wait_ge(v_exp, 2 * i + 2)
                        pv(0)
                        st(2)
                    if inside(i, -2):
                        pe.wait_ge(tr_out, i - 1)
                        pe.matmul(ROUTE0["logits"], xrT[:], router[0][:], start=True, stop=True).then_inc(lg_done, 1)
                    if inside(i, 2):
                        pe.wait_ge(x_norm, i + 3)
                        pe.wait_ge(c_copy, i + 3)
                        reached(pe, vz_done, i + 2)
                        pe.transpose(bank[4][:, 0:128], xn[:, p, :], ident)
                        pe.transpose(bank[4][:, 128:128 + C], cn[:, p, :], ident[0:C, 0:C]).then_inc(tf_done, 1)
                    if inside(i, 0):
                        pv(1)
                        st(3)
                    if inside(i, -1):
                        pe.wait_ge(ot_out, i)
                        reached(pe, x1_done, i - 1)
                        for c in range(2):
                            mm = pe.matmul(bank[1][:, 0:D], oT[:, 128 * c:128 * c + 128], fcw[:, c, :],
                                           start=(c == 0), stop=(c == 1))
                        mm.then_inc(fc_done, 1)
                    if inside(i, 0):
                        pv(2)
                    if inside(i, -2):
                        pe.wait_ge(chain, 10 * (i - 2) + 6)
                        pe.matmul(ROUTE0["ranks"], trib[:], hot[:, 0, :], start=True, stop=True)
                        pe.matmul(ROUTE0["totals"], oneb[:], hot[:, 0, :], start=True, stop=True).then_inc(rk_done, 1)
                    if inside(i, 0):
                        pv(3)
                    if inside(i, 1):
                        pe.wait_ge(q_cast, i + 2)
                        pe.wait_ge(k_exp, 5 * i + 6)
                        for j in range(4):
                            reached(pe, p_exp, 4 * i + j + 1)
                            if j == 1:
                                reached(pe, x1_done, i)
                            if j == 2:
                                reached(pe, chain, 10 * (i - 2) + 9)
                            for g in range(G):
                                mm = pe.matmul(bank[j][:, C * g:C * g + C], qb[32 * j:32 * j + 16, 0, 128 * g:128 * g + 128],
                                               kb0[32 * j:32 * j + 16, C * g:C * g + C], start=True, stop=True)
                            mm.then_inc(sm_done, 1)
                    if inside(i, 2):
                        pe.wait_ge(tf_out, i + 3)
                        for g in range(G):
                            mm = pe.matmul(bank[6][:, 128 * g:128 * g + 128], wz[:, g, :], xcT[:, p, 0:128],
                                           start=True, stop=True)
                        mm.then_inc(zq_done, 1)
                        reached(pe, k_exp, 5 * (i + 2))
                        for g in range(G):
                            mm = pe.matmul(bank[5][:, C * g:C * g + C], wz[:, g, :], xcT[:, p, 128:128 + C],
                                           start=True, stop=True)
                        mm.then_inc(zk_done, 1)
                        pe.matmul(bank[4][0:C, 256:384], xcT[:, p, 128:128 + C], wv0[:], start=True,
                                  stop=True).then_inc(zv_done, 1)
                    if inside(i, 1):
                        pe.wait_ge(max_done, 4 * i + 8)
                        pe.transpose(mtp, mx[:], identb[:]).then_inc(mt_done, 1)

                steps(pe, -3, 5, 28, B + 1, 2, body)

            @block.scalar
            def _(act):
                def body(i, p):
                    q = 1 - p

                    def probs(j):
                        act.wait_ge(st_done, 4 * i + j + 1)
                        reached(act, pv_done, 4 * i + j - 3)
                        act.activation(PT[:, j, :], bank[j][0:C, :], ACT.Exp, scale=float(D) ** -0.5).then_inc(p_exp, 1)

                    def keys(s, j):
                        r = 32 * j
                        act.activation(kz[r:r + 32, s, j, :], bank[5][r:r + 32, 0:G * C], ACT.Exp,
                                       bias=zbias[r:r + 32]).then_inc(k_exp, 1)

                    if inside(i, 0):
                        probs(0)
                    if inside(i, 1):
                        keys(q, 2)
                    if inside(i, -2):
                        act.wait_ge(tr_done, i - 1)
                        if inside(i, -1):
                            act.wait_ge(ot_done, i)
                        act.activation(xrT[:], bank[6][:, 256:384], ACT.Copy).then_inc(tr_out, 1)
                    if inside(i, 0):
                        probs(1)
                    if inside(i, 1):
                        keys(q, 3)
                    if inside(i, -1):
                        act.wait_ge(ot_done, i)
                        act.activation(oT[:, 0:256], bank[6][:, 0:256], ACT.Copy).then_inc(ot_out, 1)
                    if inside(i, 0):
                        probs(2)
                    if inside(i, 2):
                        act.wait_ge(tf_done, i + 3)
                        act.activation(xcT[:, p, 0:128 + C], bank[4][:, 0:128 + C], ACT.Copy).then_inc(tf_out, 1)
                    if inside(i, 0):
                        probs(3)
                    if inside(i, 2):
                        act.wait_ge(zq_done, i + 3)
                        act.activation(qf[:, p, 0:512], bank[6][:, :], ACT.Exp, bias=zbias[:]).then_inc(q_exp, 1)
                        act.wait_ge(zk_done, i + 3)
                        act.activation(kb0[:], bank[5][:, 0:G * C], ACT.Exp, bias=zbias[:]).then_inc(k_exp, 1)
                        if at_step(i, -2):
                            act.wait_ge(made_z, 1)
                        keys(p, 0)
                        keys(p, 1)
                        act.wait_ge(vz_done, i + 3)
                        reached(act, pv_done, 4 * i + 4)
                        zv = vz[0:C, :].rearrange("p (h e) -> p h e", e=HD0)
                        act.activation(v0[:, p, :, 0:HD0], zv, ACT.Exp).then_inc(v_exp, 1)
                        act.activation(v0[:, p, :, HD0:16], zv, ACT.Exp, scale=-1.0).then_inc(v_exp, 1)
                    if inside(i, -2):
                        act.wait_ge(chain, 10 * (i - 2) + 4)
                        act.activation(junk[:], lgs[:], ACT.Exp, bias=negm[:],
                                       accum_out=gsum[:, bass.ds(i - 2, 1)]).then_inc(gexp, 1)

                steps(act, -3, 5, 28, B + 1, 2, body)

            @block.vector
            def _(v):
                def body(i, p):
                    q = 1 - p
                    if inside(i, -1):
                        v.wait_ge(pv_done, 4 * i)
                        o = bank[7][:, 0:H * 17].rearrange("p (h e) -> p h e", e=17)
                        v.reciprocal(rec[:].rearrange("p (h e) -> p h e", e=1), o[:, :, 16:17]).then_inc(rec_done, 1)
                        v.wait_ge(rec_done, i)
                        v.tensor_tensor(on[:, 0:256].rearrange("p (h e) -> p h e", e=16), o[:, :, 0:16],
                                        rec[:].rearrange("p (h e) -> p h e", e=1).broadcast_to([128, H, 16]),
                                        ALU.mult).then_inc(on_done, 1)
                    if inside(i, -2):
                        v.wait_ge(xr_rstd, 2 * (i - 1))
                        if inside(i, -4):
                            v.wait_ge(scat[p], 8 * (i - 2 - p))
                        v.tensor_scalar(xr[:, p, :], x[:, bass.ds(i - 2, 1), :].rearrange("p b d -> p (b d)"),
                                        mv1[:, p, 0:1], rst[:, p, 1:2], ALU.subtract, ALU.mult).then_inc(xr_norm, 1)
                    if inside(i, 3):
                        if at_step(i, -3):
                            v.wait_ge(ld_x0, 32)
                            v.wait_ge(made, 24)
                        elif at_step(i, -1):
                            v.wait_ge(ld_x, 32)
                        xi = x[:, bass.ds(i + 3, 1), :].rearrange("p b d -> p (b d)")
                        v.bn_stats(st6[:, 0, :], xi).then_inc(x_stat, 1)
                        alone(v, tick, (x_stat, 2 * (i + 3) + 1))
                        v.bn_aggr(mv[:, q, :], st6[:, 0, :]).then_inc(x_stat, 1)
                    if inside(i, -2):
                        v.wait_ge(lg_done, i - 1)
                        reached(v, gexp, i - 2)
                        route(0, v, p, i - 2, ROUTE0, 0)
                    if inside(i, -1):
                        v.wait_ge(fc_done, i)
                        v.wait_ge(xpb_done, i)
                        xo = x[:, bass.ds(i - 1, 1), :].rearrange("p b d -> p (b d)")
                        v.tensor_tensor(xo, bank[1][:, 0:D], xpb[:, q, :], ALU.add).then_inc(x1_done, 1)
                        alone(v, tick, (x1_done, i))
                        v.bn_stats(st6[:, 1, :], xo).then_inc(xr_stat, 1)
                        alone(v, tick, (xr_stat, 2 * i - 1))
                        v.bn_aggr(mv1[:, q, :], st6[:, 1, :]).then_inc(xr_stat, 1)
                    if inside(i, 3):
                        v.wait_ge(x_rstd, 2 * (i + 3) + 2)
                        reached(v, tf_done, i + 2)
                        v.tensor_scalar(xn[:, q, :], xi, mv[:, q, 0:1], rst[:, q, 0:1], ALU.subtract,
                                        ALU.mult).then_inc(x_norm, 1)
                    if inside(i, -2):
                        v.wait_ge(rk_done, i - 1)
                        route(0, v, p, i - 2, ROUTE0, 1)
                    if inside(i, 1):
                        for j in range(4):
                            v.wait_ge(sm_done, 4 * i + j + 5)
                            v.tensor_reduce(mx[:, 32 * j:32 * j + G],
                                            bank[j][:, 0:G * C].rearrange("p (g k) -> p g k", g=G), AX,
                                            ALU.max).then_inc(max_done, 1)
                    if inside(i, 2):
                        v.wait_ge(zv_done, i + 3)
                        reached(v, v_exp, 2 * i + 4)
                        v.tensor_tensor(vz[0:C, :], bank[4][0:C, 256:384], vbias[0:C, :], ALU.add).then_inc(vz_done, 1)
                    if inside(i, 1):
                        v.wait_ge(mt_done, i + 2)
                        v.tensor_copy(mT[:], mtp_v).then_inc(mt_out, 1)

                mtp_v = bank[3][:, 0:64].bitcast(BF16)
                steps(v, -3, 5, 28, B + 1, 2, body)

            @block.gpsimd
            def _(pool):
                def body(i, p):
                    q = 1 - p
                    if inside(i, 1):
                        reached(pool, sm_done, 4 * (i + 1))
                        alone(pool, tick, (q_exp, i + 2))
                        pool.tensor_copy(qb[:, 0, 0:512], qf[:, q, 0:512]).then_inc(q_cast, 1)
                    if inside(i, 3):
                        if at_step(i, -3):
                            pool.wait_ge(ld_x0, 32)
                        elif at_step(i, -1):
                            pool.wait_ge(ld_x, 32)
                        reached(pool, tf_done, i + 2)
                        pool.tensor_copy(cn[:, q, :], cx[:, bass.ds(i + 3, 1), :].rearrange(
                            "p b d -> p (b d)")).then_inc(c_copy, 1)
                        alone(pool, tick, (x_stat, 2 * (i + 3) + 2), (x_norm, i + 2))
                        pool.tensor_scalar(rstt[:, 0:1], mv[:, q, 1:2], EPS, None, ALU.add).then_inc(x_rstd, 1)
                        pool.wait_ge(x_rstd, 2 * (i + 3) + 1)
                        pool.tensor_tensor(rst[:, q, 0:1], rstt[:, 0:1], halves[:, 0:1], ALU.pow).then_inc(x_rstd, 1)
                    if inside(i, 0):
                        reached(pool, x1_done, i - 1)
                        pool.tensor_tensor(xpb[:, p, :], x[:, bass.ds(i, 1), :].rearrange("p b d -> p (b d)"),
                                           fcb[:], ALU.add).then_inc(xpb_done, 1)
                    if inside(i, -1):
                        alone(pool, tick, (xr_stat, 2 * i))
                        pool.tensor_scalar(rstt[:, 1:2], mv1[:, q, 1:2], EPS, None, ALU.add).then_inc(xr_rstd, 1)
                        pool.wait_ge(xr_rstd, 2 * i - 1)
                        pool.tensor_tensor(rst[:, q, 1:2], rstt[:, 1:2], halves[:, 0:1], ALU.pow).then_inc(xr_rstd, 1)
                    if inside(i, -2):
                        alone(pool, tick, (chain, 10 * (i - 1)))
                        pool.tensor_copy(slot[:, bass.ds(i - 2, 1), 0:1].rearrange("p a b -> p (a b)"),
                                         slotp[:, p, 0:1]).then_inc(kept0, 1)
                        pool.indirect_dma_start(xs[0], bass.IndirectOffsetOnAxis(ap=slotp[:, p, 0:1], axis=0),
                                                xr[:, p, :], None).then_inc(scat[p], 16)

                steps(pool, -3, 5, 28, B + 1, 2, body)

        def table_and_pads(layer, NT, tag):
            tab, pads = sem(tag + "tab"), sem(tag + "pads")
            gt = sem(tag + "gates")
            ge = sem(tag + "gate_exp")
            with nc.Block() as block:
                @block.vector
                def _(v):
                    count = [0]

                    def step(ins):
                        count[0] += 1
                        ins.then_inc(tab, 1)
                        v.wait_ge(tab, count[0])

                    n, tl, cum, dd = (tcnt[:, k, :] for k in range(4))
                    step(v.tensor_scalar(pos[:], base[:], cst[:, K_PART:K_PART + 1], None, ALU.add))
                    step(v.tensor_copy(padidx[:], pos[:]))
                    v.memset(junk[:], 1.0).then_inc(gt, 1)
                    step(v.tensor_tensor(n, base[:], cst[:, K_EOFF:K_EOFF + E], ALU.subtract))
                    step(v.tensor_scalar(n, n, 127.0, None, ALU.add))
                    step(v.tensor_copy(tint[:], n))
                    step(v.tensor_scalar(tint[:], tint[:], 7, None, ALU.arith_shift_right))
                    step(v.tensor_copy(tl, tint[:]))
                    v.wait_ge(gt, 1)
                    step(v.tensor_tensor_scan(cum, junk[:], tl, 0.0, ALU.mult, ALU.add))
                    step(v.tensor_scalar(dd, tl, -128.0, float(REGION), ALU.mult, ALU.add))
                    t = cst[0:1, K_TILE:K_TILE + NT]
                    ex, row, s1 = (trow[:, k, 0:NT] for k in range(3))
                    step(v.memset(ex, 0.0))
                    step(v.tensor_scalar(row, t, 128.0, None, ALU.mult))
                    for e in range(E):
                        step(v.scalar_tensor_tensor(out=ex, in0=t, scalar=cum[0:1, e:e + 1], in1=ex,
                                                    op0=ALU.is_ge, op1=ALU.add))
                        step(v.tensor_scalar(s1, t, cum[0:1, e:e + 1], dd[0:1, e:e + 1], ALU.is_ge, ALU.mult))
                        step(v.tensor_tensor(row, row, s1, ALU.add))
                    step(v.tensor_scalar(s1, ex, float(E - 1), None, ALU.min))
                    step(v.tensor_copy(etab[:, 0:NT], s1))
                    step(v.tensor_scalar(s1, row, float(DUMMY), None, ALU.min))
                    step(v.tensor_copy(rtab[:, 0:NT], s1))
                    dl, diff = tcnt[:, 4, :], tcnt[:, 5, :]
                    step(v.tensor_tensor(dl, cum, tl, ALU.subtract))
                    step(v.scalar_tensor_tensor(out=dl, in0=dl, scalar=128.0, in1=cst[:, K_EOFF:K_EOFF + E],
                                                op0=ALU.mult, op1=ALU.subtract))
                    step(v.tensor_tensor(diff[:, 1:E], dl[:, 1:E], dl[:, 0:E - 1], ALU.subtract))
                    part = slice(0, 1 + layer)
                    step(v.tensor_copy(slotf[:, :, part], slot[:, :, part]))
                    step(v.tensor_copy(slott[:, 1, :, part], slotf[:, :, part]))
                    for e in range(1, E):
                        step(v.tensor_scalar(slott[:, 0, :, part], slotf[:, :, part], float(e * REGION),
                                             diff[:, e:e + 1], ALU.is_ge, ALU.mult))
                        step(v.tensor_tensor(slott[:, 1, :, part], slott[:, 1, :, part], slott[:, 0, :, part], ALU.add))
                    step(v.tensor_copy(slot[:, :, part], slott[:, 1, :, part]))
                    step(v.tensor_copy(base[:], cst[:, K_EOFF:K_EOFF + E]))
                    if layer == 0:
                        step(v.reciprocal(gate[:, 0, :], gsum[:]))
                    else:
                        v.wait_ge(ge, 1)
                        step(v.tensor_scalar(gsum[:], gate[:, 1, :], 1.0, None, ALU.add))
                        step(v.reciprocal(gate[:, 0, :], gsum[:]))
                        step(v.tensor_tensor(gate[:, 1, :], gate[:, 1, :], gate[:, 0, :], ALU.mult))

                if layer == 0:
                    @block.sync
                    def _(sp):
                        sp.dma_start(b1, A["b1"].partition_broadcast(128)).then_inc(ld_moe0, 16)
                else:
                    @block.scalar
                    def _(act):
                        act.activation(gate[:, 1, :], gsum[:], ACT.Exp).then_inc(ge, 1)

                @block.gpsimd
                def _(pool):
                    pool.dma_start(xs[layer][DUMMY:DUMMY + 128, :], zero[:]).then_inc(pads, 16)
                    pool.wait_ge(tab, 2)
                    for e in range(E):
                        pool.indirect_dma_start(xs[layer], bass.IndirectOffsetOnAxis(ap=padidx[:, e:e + 1], axis=0),
                                                zero[:], None).then_inc(pads, 16)
                    pool.wait_ge(pads, 16 * (E + 1))
                    if layer == 0:
                        for q in range(2):
                            pool.wait_ge(scat[q], 8 * B)
                    else:
                        for q in range(2):
                            pool.wait_ge(scat2[q], 16 * B)

        table_and_pads(0, NT0, "t0_")

        def experts(layer, NT, tag):
            last = NT - 3
            x_in = [sem(f"{tag}x_in{k}") for k in range(4)]
            y_out = [sem(f"{tag}y_out{k}") for k in range(4)]
            (t_done, t_out, h_done, hb_done, g_done, ht_done, ht_out, y_done, y_sb) = (
                sem(tag + n) for n in ("t_done", "t_out", "h_done", "hb_done", "g_done", "ht_done", "ht_out",
                                       "y_done", "y_sb"))
            ld = (ld_moe0, 64) if layer == 0 else (ld_moe1, 32)
            with nc.Block() as block:
                @block.sync
                def _(sp):
                    def load(t, k):
                        r = sp.value_load(rtab[0:1, bass.ds(t, 1)], min_val=0, max_val=DUMMY)
                        reached(sp, t_done, t - 3)
                        sp.dma_start(xt[:, k, :], xs[layer][bass.ds(r, 128), :]).then_inc(x_in[k], 16)

                    def body(t, k):
                        if at_step(t, -2):
                            load(0, 0)
                            load(1, 1)
                        if inside(t, 4, NT):
                            load(t + 4, k)

                    steps(sp, -2, 5, last - 4, NT, 4, body)

                @block.gpsimd
                def _(pool):
                    def body(t, k):
                        if inside(t, -1, NT):
                            k1 = (k - 1) % 4
                            pool.wait_ge(y_sb, t)
                            pool.dma_start(ys[layer][bass.ds((t - 1) * 128, 128), :],
                                           yo[:, k1, :]).then_inc(y_out[k1], 16)

                    steps(pool, -2, 5, last, NT, 4, body)
                    for k in range(4):
                        pool.wait_ge(y_out[k], 16 * len(range(k, NT, 4)))

                @block.tensor
                def _(pe):
                    def body(t, k):
                        p = k % 2
                        if inside(t, 2, NT):
                            k2 = (k + 2) % 4
                            pe.wait_ge(x_in[k2], 4 * (t + 2 - k2) + 16)
                            reached(pe, t_out, t + 1)
                            pe.transpose(bank[6 + p][:, 0:128], xt[:, k2, :], ident).then_inc(t_done, 1)
                        if inside(t, 1, NT):
                            if at_step(t, -1):
                                pe.wait_ge(*ld)
                            e = pe.value_load(etab[0:1, bass.ds(t + 1, 1)], min_val=0, max_val=E - 1)
                            reached(pe, (hb_done if layer == 0 else g_done), t)
                            pe.wait_ge(t_out, t + 2)
                            pe.matmul(bank[1 - p][:, :], xtT[:, 1 - p, :],
                                      w1[:].rearrange("p e f -> p (e f)")[:, bass.ds(e * F, F)],
                                      start=True, stop=True).then_inc(h_done, 1)
                        if inside(t, -1, NT):
                            e = pe.value_load(etab[0:1, bass.ds(t - 1, 1)], min_val=0, max_val=E - 1)
                            pe.wait_ge(ht_out, t)
                            reached(pe, y_sb, t - 2)
                            for c in range(FC):
                                mm = pe.matmul(bank[5 - p][:, 0:D], hT[:, 1 - p, 128 * c:128 * c + 128],
                                               w2[:].rearrange("p e c d -> p (e c d)")[:, bass.ds(e * F + c * D, D)],
                                               start=(c == 0), stop=(c == FC - 1))
                            mm.then_inc(y_done, 1)
                        if inside(t, 0, NT):
                            pe.wait_ge(g_done, t + 1)
                            reached(pe, ht_out, t - 1)
                            for c in range(FC):
                                mm = pe.transpose(bank[2 + p][:, 128 * c:128 * c + 128],
                                                  hg[:, p, 128 * c:128 * c + 128], ident)
                            mm.then_inc(ht_done, 1)

                    steps(pe, -2, 5, last, NT, 4, body)

                @block.scalar
                def _(act):
                    def body(t, k):
                        p = k % 2
                        if inside(t, 2, NT):
                            act.wait_ge(t_done, t + 3)
                            reached(act, h_done, t + 1)
                            act.activation(xtT[:, p, :], bank[6 + p][:, 0:128], ACT.Copy).then_inc(t_out, 1)
                        if inside(t, 1, NT):
                            reached(act, ht_done, t)
                            if layer == 0:
                                act.wait_ge(hb_done, t + 2)
                                act.activation(hg[:, 1 - p, :], hb[:, 1 - p, :], ACT.Gelu).then_inc(g_done, 1)
                            else:
                                act.wait_ge(h_done, t + 2)
                                act.activation(hg[:, 1 - p, :], bank[1 - p][:, :], ACT.Gelu).then_inc(g_done, 1)

                    steps(act, -2, 5, last, NT, 4, body)

                @block.vector
                def _(v):
                    def body(t, k):
                        p = k % 2
                        if inside(t, 1, NT) and layer == 0:
                            if at_step(t, -1):
                                v.wait_ge(ld_moe0, 64)
                            e = v.value_load(etab[0:1, bass.ds(t + 1, 1)], min_val=0, max_val=E - 1)
                            reached(v, g_done, t)
                            v.wait_ge(h_done, t + 2)
                            v.tensor_tensor(hb[:, 1 - p, :], bank[1 - p][:, :],
                                            shared[:, bass.ds(e * F, F)],
                                            ALU.add).then_inc(hb_done, 1)
                        if inside(t, -1, NT):
                            if layer == 0:
                                e = v.value_load(etab[0:1, bass.ds(t - 1, 1)], min_val=0, max_val=E - 1)
                            v.wait_ge(y_done, t)
                            k1 = (k - 1) % 4
                            if inside(t, -5, NT):
                                v.wait_ge(y_out[k1], 4 * (t - 1 - k1))
                            if layer == 0:
                                v.tensor_tensor(yo[:, k1, :], bank[5 - p][:, 0:D],
                                                b2[:].rearrange("p e d -> p (e d)")[:, bass.ds(e * D, D)],
                                                ALU.add).then_inc(y_sb, 1)
                            else:
                                v.tensor_copy(yo[:, k1, :], bank[5 - p][:, 0:D]).then_inc(y_sb, 1)
                        if inside(t, 0, NT):
                            v.wait_ge(ht_done, t + 1)
                            reached(v, y_done, t - 1)
                            v.tensor_copy(hT[:, p, :], bank[2 + p][:, :]).then_inc(ht_out, 1)

                    steps(v, -2, 5, last, NT, 4, body)

        experts(0, NT0, "e0_")

        scat2 = [sem(f"b_scat{p}") for p in range(2)]
        gidx = sb("gidx", [128, 2, 2], U32)
        gi_done, gi2_done = sem("gi_done"), sem("gi2_done")
        gath = [sem(f"b_gath{p}") for p in range(2)]
        (x2_done, x_stat, c_stat, x_rstd, x_norm, c_norm, tf_done, tf_out, q_done, q_out, kv_done, kv_out,
         qk_cast) = (sem("b_" + n) for n in (
             "x2_done", "x_stat", "c_stat", "x_rstd", "x_norm", "c_norm", "tf_done", "tf_out", "q_done", "q_out",
             "kv_done", "kv_out", "qk_cast"))
        q_out_v = sem("b_q_out_v")
        (sm_done, max_done, mt_done, mt_out, st_done, p_exp, pv_done, rec_done, on_done, ot_done, ot_out,
         ff_done, g_exp, s_step, x3_done, acc_done) = (sem("b_" + n) for n in (
             "sm_done", "max_done", "mt_done", "mt_out", "st_done", "p_exp", "pv_done", "rec_done", "on_done",
             "ot_done", "ot_out", "ff_done", "g_exp", "s_step", "x3_done", "acc_done"))
        ot_out_v = sem("b_ot_out_v")
        (xr_stat, xr_rstd, xr_norm, tr_done, tr_out, lg_done, rk_done, chain) = (sem("b_" + n) for n in (
            "xr_stat", "xr_rstd", "xr_norm", "tr_done", "tr_out", "lg_done", "rk_done", "chain"))
        K1 = 13
        kept1 = sem("b_kept")
        ROUTE1 = dict(logits=bank[7][:, 128:128 + E], ranks=bank[7][:, 256:256 + E],
                      totals=bank[7][:, 384:384 + E], chain=chain, kept=kept1, K=K1)

        with nc.Block() as block:
            @block.sync
            def _(sp):
                sp.dma_start(w1[:], A["w1_1"]).then_inc(ld_moe1, 16)
                sp.dma_start(w2[:], A["w2_1"]).then_inc(ld_moe1, 16)

            @block.tensor
            def _(pe):
                mtp = bank[7][:, 0:64].bitcast(BF16)

                def body(i, p):
                    q = 1 - p
                    if inside(i, 0):
                        pe.wait_ge(qk_cast, 3 * i + 3)
                        for k in range(4):
                            r, c0 = 64 * (k // 2), 4 * (k % 2)
                            if k == 0:
                                reached(pe, x3_done, i)
                            else:
                                reached(pe, on_done, 4 * i - 4 + k + 1)
                            for c in range(4):
                                mm = pe.matmul(bank[k][:, C * c:C * c + C],
                                               qb[r:r + 64, p, 128 * (c0 + c):128 * (c0 + c) + 128],
                                               kb[r:r + 64, p, 0:C], start=True, stop=True)
                            mm.then_inc(sm_done, 1)
                    if inside(i, 1):
                        pe.wait_ge(x_norm, i + 2)
                        pe.wait_ge(c_norm, i + 2)
                        reached(pe, ot_out, i)
                        pe.transpose(bank[7][:, 0:128], xn[:, q, :], ident)
                        pe.transpose(bank[7][:, 128:128 + C], cn[:, q, :], ident[0:C, 0:C]).then_inc(tf_done, 1)
                        pe.wait_ge(tf_out, 2 * i + 4)
                        reached(pe, s_step, 4 * i)
                        for k in range(2):
                            for c in range(4):
                                mm = pe.matmul(bank[4 + k][:, 128 * c:128 * c + 128],
                                               wq[:, 128 * (4 * k + c):128 * (4 * k + c) + 128], xcT[:, q, 0:128],
                                               start=True, stop=True)
                            mm.then_inc(q_done, 1)
                        reached(pe, ot_out_v, i)
                        pe.matmul(bank[6][:, 0:C], wk2[:].rearrange("p a b -> p (a b)"), xcT[:, q, 128:128 + C],
                                  start=True, stop=True)
                        pe.matmul(bank[6][0:C, 128:128 + HD1], xcT[:, q, 128:128 + C], wv1[:], start=True,
                                  stop=True).then_inc(kv_done, 1)
                    if inside(i, 0):
                        pe.wait_ge(max_done, 4 * i + 4)
                        pe.transpose(mtp, mx[:], identb[:]).then_inc(mt_done, 1)
                    if inside(i, -1):
                        pe.wait_ge(xr_norm, i)
                        if inside(i, 0):
                            pe.wait_ge(mt_out, i + 1)
                        pe.transpose(bank[7][:, 0:128], xr[:, q, :], ident).then_inc(tr_done, 1)

                    def st(k):
                        r, c0 = 64 * (k // 2), 4 * (k % 2)
                        for c in range(4):
                            o = bank[k][0:C, 128 * c:128 * c + 128]
                            pe.matmul(o, kf[r:r + 64, p, 0:C],
                                      qf[r:r + 64, p, 128 * (c0 + c):128 * (c0 + c) + 128], start=True, stop=False)
                            mm = pe.matmul(o, sel1[r:r + 64, c0 + c, :], mT[r:r + 64, :], start=False, stop=True)
                        mm.then_inc(st_done, 1)

                    def pv(k):
                        pe.wait_ge(p_exp, 4 * i + k + 1)
                        for c in range(4):
                            mm = pe.matmul(bank[k][:, 65 * c:65 * c + 65], PT[:, k, 128 * c:128 * c + 128],
                                           v1[:, p, :], start=True, stop=True)
                        mm.then_inc(pv_done, 1)

                    if inside(i, 0):
                        pe.wait_ge(mt_out, i + 1)
                        st(0)
                        st(1)
                    if inside(i, -1):
                        pe.wait_ge(tr_out, i)
                        pe.matmul(ROUTE1["logits"], xrT[:], router[1][:], start=True, stop=True).then_inc(lg_done, 1)
                    if inside(i, 0):
                        pv(0)
                        st(2)
                        pv(1)
                        st(3)
                        pv(2)
                        nx = i + 1 if inside(i, 1) else i
                        pe.wait_ge(q_out, nx + 1)
                        pe.wait_ge(q_out_v, nx + 1)
                        for k, half in enumerate((1, 0)):
                            for c in range(FC):
                                mm = pe.matmul(bank[4 + k][:, 128 * c:128 * c + 128],
                                               wf1[:, half, 128 * c:128 * c + 128], xcT[:, p, 0:128],
                                               start=True, stop=True)
                            mm.then_inc(ff_done, 1)
                    if inside(i, -1):
                        pe.wait_ge(chain, K1 * (i - 1) + 8)
                        pe.matmul(ROUTE1["ranks"], trib[:], hot[:, 2, :], start=True, stop=True)
                        pe.matmul(ROUTE1["totals"], oneb[:], hot[:, 2, :], start=True, stop=True).then_inc(rk_done, 1)
                    if inside(i, 0):
                        pv(3)
                        pe.wait_ge(on_done, 4 * i + 4)
                        if inside(i, 1):
                            pe.wait_ge(kv_out, 2 * i + 4)
                        for c in range(4):
                            mm = pe.transpose(bank[6][:, 128 * c:128 * c + 128], on[:, 512 + 128 * c:512 + 128 * c + 128], ident)
                        mm.then_inc(ot_done, 1)
                        if inside(i, -1):
                            pe.wait_ge(chain, K1 * i)
                        for c in range(4):
                            mm = pe.transpose(bank[7][:, 128 * c:128 * c + 128], on[:, 128 * c:128 * c + 128], ident)
                        mm.then_inc(ot_done, 1)
                        pe.wait_ge(s_step, 4 * i + 4)
                        for c in range(FC):
                            pe.matmul(bank[0][:, 0:D], sg[:, 2, 128 * c:128 * c + 128], wf2[:, c, :],
                                      start=(c == 0), stop=False)
                        pe.wait_ge(ot_out, i + 1)
                        pe.wait_ge(ot_out_v, i + 1)
                        for c in range(8):
                            mm = pe.matmul(bank[0][:, 0:D], oT[:, 128 * c:128 * c + 128], wo[:, c, :],
                                           start=False, stop=(c == 7))
                        mm.then_inc(acc_done, 1)

                pe.wait_ge(ld_w1, 144)
                steps(pe, -2, 3, 28, B, 2, body)

            @block.scalar
            def _(act):
                def evac_r(i):
                    act.wait_ge(tr_done, i)
                    act.activation(xrT[:], bank[7][:, 0:128], ACT.Copy).then_inc(tr_out, 1)

                def body(i, p):
                    q = 1 - p
                    if inside(i, 1):
                        act.wait_ge(tf_done, i + 2)
                        act.activation(xcT[:, q, 0:128], bank[7][:, 0:128], ACT.Identity, bias=lnp[:, 1:2],
                                       scale=lnp[:, 0:1]).then_inc(tf_out, 1)
                        act.activation(xcT[:, q, 128:128 + C], bank[7][:, 128:128 + C], ACT.Identity,
                                       bias=lnp[:, 3:4], scale=lnp[:, 2:3]).then_inc(tf_out, 1)
                        act.wait_ge(q_done, 2 * i + 3)
                        act.activation(qf[:, q, 0:512], bank[4][:, :], ACT.Copy).then_inc(q_out, 1)
                        act.wait_ge(kv_done, i + 2)
                        act.activation(kf[:, q, 0:C], bank[6][:, 0:C], ACT.Copy).then_inc(kv_out, 1)
                        act.activation(v1[:, q, 0:HD1], bank[6][0:C, 128:128 + HD1], ACT.Copy).then_inc(kv_out, 1)
                    if inside(i, 0):
                        for k in range(4):
                            act.wait_ge(st_done, 4 * i + k + 1)
                            act.activation(PT[:, k, :], bank[k][0:C, :], ACT.Exp,
                                           scale=float(HD1) ** -0.5).then_inc(p_exp, 1)
                            if k == 0 and inside(i, -1):
                                evac_r(i)
                        act.wait_ge(ff_done, 2 * i + 1)
                        act.activation(sg[:, 0, :], bank[4][:, :], ACT.Exp, scale=-1.0).then_inc(g_exp, 1)
                        act.wait_ge(ot_done, 2 * i + 2)
                        act.activation(oT[:, 0:512], bank[7][:, :], ACT.Copy).then_inc(ot_out, 1)
                    elif inside(i, -1):
                        evac_r(i)

                if True:
                    act.wait_ge(ld_w1, 144)
                steps(act, -2, 3, 28, B, 2, body)

            @block.vector
            def _(v):
                def norm_r(i, q):
                    v.wait_ge(xr_rstd, 2 * i)
                    if inside(i, -3):
                        v.wait_ge(scat2[q], 16 * (i - 1 - q))
                    v.tensor_scalar(xr[:, q, :], x[:, bass.ds(i - 1, 1), :].rearrange("p b d -> p (b d)"),
                                    mv1[:, q, 0:1], rst[:, q, 1:2], ALU.subtract, ALU.mult).then_inc(xr_norm, 1)

                def body(i, p):
                    q = 1 - p
                    if inside(i, 0):
                        for k in range(4):
                            v.wait_ge(sm_done, 4 * i + k + 1)
                            reached(v, mt_done, i)
                            m0 = 64 * (k // 2) + 4 * (k % 2)
                            v.tensor_reduce(mx[:, m0:m0 + 4], bank[k][:, 0:4 * C].rearrange("p (g k) -> p g k", g=4),
                                            AX, ALU.max).then_inc(max_done, 1)
                            if k == 1 and inside(i, -1):
                                norm_r(i, q)
                    elif inside(i, -1):
                        norm_r(i, q)
                    if inside(i, 0):
                        v.wait_ge(mt_done, i + 1)
                        v.tensor_copy(mT[:], bank[7][:, 0:64].bitcast(BF16)).then_inc(mt_out, 1)
                    if inside(i, 1):
                        v.wait_ge(q_done, 2 * i + 4)
                        v.tensor_copy(qf[:, q, 512:1024], bank[5][:, :]).then_inc(q_out_v, 1)
                    if inside(i, 2):
                        xi = x[:, bass.ds(i + 2, 1), :].rearrange("p b d -> p (b d)")
                        ci = cx[:, bass.ds(i + 2, 1), :].rearrange("p b d -> p (b d)")
                        v.wait_ge(gath[p], 8 * (i + 2 - p) + 16)
                        v.scalar_tensor_tensor(out=xi, in0=yg[:, p, 0, :], scalar=gate[:, 0, bass.ds(i + 2, 1)],
                                               in1=xi, op0=ALU.mult, op1=ALU.add).then_inc(x2_done, 1)
                        v.bn_stats(st6[0:C, 2, :], ci).then_inc(c_stat, 1)
                        alone(v, tick, (x2_done, i + 3))
                        v.bn_stats(st6[:, 0, :], xi).then_inc(x_stat, 1)
                        alone(v, tick, (c_stat, 2 * (i + 2) + 1))
                        v.bn_aggr(mvc[0:C, p, :], st6[0:C, 2, :]).then_inc(c_stat, 1)
                        alone(v, tick, (x_stat, 2 * (i + 2) + 1))
                        v.bn_aggr(mv[:, p, :], st6[:, 0, :]).then_inc(x_stat, 1)
                    if inside(i, -1):
                        v.wait_ge(lg_done, i)
                        route(1, v, q, i - 1, ROUTE1, 0)
                    if inside(i, 2):
                        reached(v, tf_done, i + 1)
                        v.wait_ge(x_rstd, 4 * (i + 2) + 4)
                        v.tensor_scalar(xn[:, p, :], xi, mv[:, p, 0:1], rst[:, p, 0:1], ALU.subtract,
                                        ALU.mult).then_inc(x_norm, 1)
                        v.tensor_scalar(cn[:, p, :], ci, mvc[0:C, p, 0:1], rst[0:C, p, 2:3], ALU.subtract,
                                        ALU.mult).then_inc(c_norm, 1)

                    def norm_o(k):
                        r, c0 = k // 2, 4 * (k % 2)
                        o = bank[k][:, 0:4 * 65].rearrange("p (c e) -> p c e", e=65)
                        rk = rec[:, 4 * k:4 * k + 4].rearrange("p (c e) -> p c e", e=1)
                        v.wait_ge(pv_done, 4 * i + k + 1)
                        v.reciprocal(rk, o[:, :, 64:65]).then_inc(rec_done, 1)
                        v.wait_ge(rec_done, 4 * i + k + 1)
                        if k == 0:
                            reached(v, ot_done, 2 * i)
                        dst = on[:].rearrange("p (c r e) -> p c r e", c=8, r=2)[:, c0:c0 + 4, r, :]
                        v.tensor_tensor(dst, o[:, :, 0:64], rk.broadcast_to([128, 4, 64]),
                                        ALU.mult).then_inc(on_done, 1)

                    if inside(i, 0):
                        norm_o(0)
                        norm_o(1)
                        norm_o(2)
                    if inside(i, -1):
                        v.wait_ge(rk_done, i)
                        route(1, v, q, i - 1, ROUTE1, 1)
                    if inside(i, 0):
                        norm_o(3)
                        v.wait_ge(g_exp, i + 1)
                        v.tensor_scalar(sg[:, 0, :], sg[:, 0, :], 1.0, None, ALU.add).then_inc(s_step, 1)
                        v.wait_ge(s_step, 4 * i + 1)
                        v.reciprocal(sg[:, 1, :], sg[:, 0, :]).then_inc(s_step, 1)
                        v.wait_ge(s_step, 4 * i + 2)
                        v.tensor_tensor(sg[:, 1, :], bank[4][:, :], sg[:, 1, :], ALU.mult).then_inc(s_step, 1)
                        v.wait_ge(s_step, 4 * i + 3)
                        v.wait_ge(ff_done, 2 * i + 2)
                        reached(v, acc_done, i)
                        v.tensor_tensor(sg[:, 2, :], bank[5][:, :], sg[:, 1, :], ALU.mult).then_inc(s_step, 1)
                        v.wait_ge(ot_done, 2 * i + 1)
                        v.tensor_copy(oT[:, 512:1024], bank[6][:, :]).then_inc(ot_out_v, 1)
                        v.wait_ge(acc_done, i + 1)
                        xo = x[:, bass.ds(i, 1), :].rearrange("p b d -> p (b d)")
                        v.tensor_tensor(xo, bank[0][:, 0:D], xo, ALU.add).then_inc(x3_done, 1)
                        alone(v, tick, (x3_done, i + 1))
                        v.bn_stats(st6[:, 1, :], xo).then_inc(xr_stat, 1)
                        alone(v, tick, (xr_stat, 2 * i + 1))
                        v.bn_aggr(mv1[:, p, :], st6[:, 1, :]).then_inc(xr_stat, 1)

                steps(v, -2, 3, 28, B, 2, body)

            @block.gpsimd
            def _(pool):
                def gather(b, p):
                    pool.tensor_copy(gidx[:, p, 0:1], slot[:, bass.ds(b, 1), 0:1].rearrange(
                        "p a b -> p (a b)")).then_inc(gi_done, 1)
                    alone(pool, tick, (gi_done, b + 1))
                    pool.indirect_dma_start(yg[:, p, 0, :], None, ys[0], bass.IndirectOffsetOnAxis(
                        ap=gidx[:, p, 0:1], axis=0)).then_inc(gath[p], 16)

                def body(i, p):
                    q = 1 - p
                    if at_step(i, -2):
                        gather(0, 0)
                        gather(1, 1)
                    if inside(i, 1):
                        alone(pool, tick, (kv_out, 2 * i + 3))
                        pool.tensor_copy(kb[:, q, 0:C], kf[:, q, 0:C]).then_inc(qk_cast, 1)
                        alone(pool, tick, (q_out, i + 2))
                        pool.tensor_copy(qb[:, q, 0:512], qf[:, q, 0:512]).then_inc(qk_cast, 1)
                        alone(pool, tick, (q_out_v, i + 2))
                        pool.tensor_copy(qb[:, q, 512:1024], qf[:, q, 512:1024]).then_inc(qk_cast, 1)
                    if inside(i, 2):
                        alone(pool, tick, (x_stat, 2 * (i + 2) + 2), (c_stat, 2 * (i + 2) + 2))
                        pool.tensor_scalar(rstt[:, 0:1], mv[:, p, 1:2], 1.0 + EPS, EPS * EPS, ALU.mult,
                                           ALU.add).then_inc(x_rstd, 1)
                        pool.tensor_scalar(rstt[0:C, 2:3], mvc[0:C, p, 1:2], EPS, None, ALU.add).then_inc(x_rstd, 1)
                        pool.wait_ge(x_rstd, 4 * (i + 2) + 2)
                        pool.tensor_tensor(rst[:, p, 0:1], rstt[:, 0:1], halves[:, 0:1], ALU.pow).then_inc(x_rstd, 1)
                        pool.tensor_tensor(rst[0:C, p, 2:3], rstt[0:C, 2:3], halves[0:C, 0:1],
                                           ALU.pow).then_inc(x_rstd, 1)
                    if inside(i, 4):
                        pool.wait_ge(x2_done, i + 3)
                        gather(i + 4, p)
                    if inside(i, -1):
                        alone(pool, tick, (chain, K1 * i))
                        pool.tensor_copy(slot[:, bass.ds(i - 1, 1), :].rearrange("p a b -> p (a b)"),
                                         slotp[:, q, :]).then_inc(kept1, 1)
                        for n in range(2):
                            pool.indirect_dma_start(xs[1], bass.IndirectOffsetOnAxis(ap=slotp[:, q, n:n + 1], axis=0),
                                                    xr[:, q, :], None).then_inc(scat2[q], 16)
                    if inside(i, 0):
                        alone(pool, tick, (xr_stat, 2 * i + 2))
                        pool.tensor_scalar(rstt[:, 1:2], mv1[:, p, 1:2], EPS, None, ALU.add).then_inc(xr_rstd, 1)
                        pool.wait_ge(xr_rstd, 2 * i + 1)
                        pool.tensor_tensor(rst[:, p, 1:2], rstt[:, 1:2], halves[:, 0:1], ALU.pow).then_inc(xr_rstd, 1)

                steps(pool, -2, 3, 26, B, 2, body)

        table_and_pads(1, NT1, "t1_")
        experts(1, NT1, "e1_")

        gath2 = [sem(f"c_gath{p}") for p in range(2)]
        o_step, o_store = sem("o_step"), sem("o_store")
        with nc.Block() as block:
            @block.gpsimd
            def _(pool):
                def body(b, p):
                    alone(pool, tick, (o_step, 2 * b - 2))
                    pool.tensor_copy(gidx[:, p, :], slot[:, bass.ds(b, 1), :].rearrange(
                        "p a b -> p (a b)")).then_inc(gi2_done, 1)
                    alone(pool, tick, (gi2_done, b + 1))
                    for n in range(2):
                        pool.indirect_dma_start(yg[:, p, n, :], None, ys[1], bass.IndirectOffsetOnAxis(
                            ap=gidx[:, p, n:n + 1], axis=0)).then_inc(gath2[p], 16)

                body(0, 0)
                body(1, 1)
                with pool.Fori(2, B - 1, 2) as b:
                    body(b, 0)
                    body(b + 1, 1)

            @block.vector
            def _(v):
                with v.Fori(0, B - 1, 2) as b0:
                    for p in range(2):
                        b = b0 + p if p else b0
                        xi = x[:, bass.ds(b, 1), :].rearrange("p b d -> p (b d)")
                        v.wait_ge(gath2[p], 16 * b0 + 32)
                        v.scalar_tensor_tensor(out=xi, in0=yg[:, p, 0, :], scalar=gate[:, 0, bass.ds(b, 1)], in1=xi,
                                               op0=ALU.mult, op1=ALU.add).then_inc(o_step, 1)
                        v.wait_ge(o_step, 2 * b + 1)
                        v.scalar_tensor_tensor(out=xi, in0=yg[:, p, 1, :], scalar=gate[:, 1, bass.ds(b, 1)], in1=xi,
                                               op0=ALU.mult, op1=ALU.add).then_inc(o_step, 1)

            @block.sync
            def _(sp):
                for n in range(8):
                    sp.wait_ge(o_step, 8 * n + 8)
                    sp.dma_start(A["out"][:, 4 * n:4 * n + 4, :], x[:, 4 * n:4 * n + 4, :]).then_inc(o_store, 16)
                sp.wait_ge(o_store, 128)


def shape_constants(np):
    k = np.zeros((128, K_N), np.float32)
    r = np.arange(128)
    k[:, K_ID:K_ID + 128] = np.eye(128)
    k[:, K_TRI:K_TRI + 128] = r[:, None] < r[None, :]
    k[:, K_ONE:K_ONE + 128] = 1
    for g in range(G):
        k[[32 * j + g for j in range(4)], K_SEL0 + C * g:K_SEL0 + C * g + C] = -1
    for c in range(8):
        k[[c, 64 + c], K_SEL1 + C * c:K_SEL1 + C * c + C] = -1
    k[:, K_SIGN:K_SIGN + 512] = np.where(np.arange(512) % 16 < 8, 1, -1)
    k[:, K_SCOL] = np.where(r % 32 < 8, 1, np.where(r % 32 < 16, -1, 1))
    k[:, K_IOTA8:K_IOTA8 + E] = np.arange(E)
    k[:, K_EOFF:K_EOFF + E] = np.arange(E) * REGION
    k[:, K_PART] = r
    k[:, K_TILE:K_TILE + NT1 + 1] = np.arange(NT1 + 1)
    k[:, K_QUART:K_QUART + 4] = r[:, None] // 32 == np.arange(4)
    return k


def kernel(x, ctx_1024, L0_xattn_fm_w, L0_xattn_fm_b, L0_xattn_fc_w, L0_xattn_fc_b, L0_ffn_w_red, L0_ffn_wg,
           L0_ffn_w1, L0_ffn_b1, L0_ffn_w2, L0_ffn_b2, L1_xattn_ln_g, L1_xattn_ln_b, L1_xattn_cln_g,
           L1_xattn_cln_b, L1_xattn_Wq, L1_xattn_Wkv, L1_xattn_Wo, L1_xattn_Wff1, L1_xattn_Wff2,
           L1_ffn_router_w, L1_ffn_w1, L1_ffn_w2):
    import numpy as np
    import concourse.bacc as bacc
    from concourse.bass_utils import run_bass_kernel_spmd

    n = np.asarray
    fm_w, fm_b = n(L0_xattn_fm_w), n(L0_xattn_fm_b)
    wz = np.zeros((D, G, 128), np.float32)
    zb = np.full((128, 1), OFF, np.float32)
    for h in range(H):
        g, j = divmod(h, 4)
        for s in range(2):
            wz[HD0 * h:HD0 * h + HD0, g, 32 * j + 8 * s:32 * j + 8 * s + 8] = fm_w.T
            zb[32 * j + 8 * s:32 * j + 8 * s + 8, 0] = fm_b
    wkv = n(L1_xattn_Wkv)
    w2_layout = lambda w: n(w).reshape(E, FC, 128, D).transpose(2, 0, 1, 3)
    arrays = dict(
        cst=shape_constants(np), x=n(x).transpose(1, 0, 2), cx=n(ctx_1024).transpose(1, 0, 2), wz=wz, zb=zb,
        vb=np.concatenate([fm_b] * H), fcw=n(L0_xattn_fc_w).T.reshape(2, 128, D).transpose(1, 0, 2),
        fcb=n(L0_xattn_fc_b), wred=n(L0_ffn_w_red).T, wg=n(L0_ffn_wg), w1_0=n(L0_ffn_w1).transpose(1, 0, 2),
        w2_0=w2_layout(L0_ffn_w2), b1=n(L0_ffn_b1), b2=n(L0_ffn_b2), wq=n(L1_xattn_Wq), wk=wkv[:, :HD1],
        wv=wkv[:, HD1:], wo=n(L1_xattn_Wo).reshape(8, 128, D).transpose(1, 0, 2),
        wf1=n(L1_xattn_Wff1).reshape(D, 2, F), wf2=n(L1_xattn_Wff2).reshape(FC, 128, D).transpose(1, 0, 2),
        lnp=np.stack([n(L1_xattn_ln_g), n(L1_xattn_ln_b), n(L1_xattn_cln_g), n(L1_xattn_cln_b)], 1),
        router=n(L1_ffn_router_w).T, w1_1=n(L1_ffn_w1).transpose(1, 0, 2), w2_1=w2_layout(L1_ffn_w2))
    arrays = {"in_" + k: np.ascontiguousarray(a) for k, a in arrays.items()}
    nc = bacc.Bacc("TRN2", target_bir_lowering=False, num_devices=1)
    A = {k[3:]: nc.dram_tensor(k, a.shape, mybir.dt.from_np(a.dtype), kind="ExternalInput").ap()
         for k, a in arrays.items()}
    A["out"] = nc.dram_tensor("out_x", (S, B, D), F32, kind="ExternalOutput").ap()
    build(nc, A)
    r = run_bass_kernel_spmd(nc, [arrays], core_ids=[0])
    return np.ascontiguousarray(r.results[0]["out_x"].transpose(1, 0, 2))
```

```python
from contextlib import ExitStack

import concourse.bass as bass
from concourse import mybir

F32 = mybir.dt.float32
BF16 = mybir.dt.bfloat16
F16 = mybir.dt.float16
U32 = mybir.dt.uint32
I32 = mybir.dt.int32
ALU = mybir.AluOpType
ACT = mybir.ActivationFunctionType
AX = mybir.AxisListType.X

B = 32
S = 128
D = 128
C = 120
H = 16
E = 8
F = 512
FC = F // 128
G = 4
HD0 = 8
HD1 = 64
EPS = 1e-5
FIRST_X = 7
OFF = -200.0

ROW = D + 1
PITCH = 144
REGION = B * S + 128
DUMMY = E * REGION
PADS = E + E - 1
NT0 = B + E - 1
NT1 = 2 * B + E - 1

K_ID, K_TRI, K_ONE, K_SEL1 = 0, 128, 256, 384
K_SIGN = K_SEL1 + (H // 2) * C
K_SCOL = K_SIGN + 512
K_IOTA8 = K_SCOL + 1
K_EOFF = K_IOTA8 + E
K_PART = K_EOFF + E
K_TILE = K_PART + 1
K_KEYS = K_TILE + NT1 + 1
K_BACK = K_KEYS + 1
K_PAD = K_BACK + 2 * B
K_HOT = K_PAD + 2 * PADS
K_N = K_HOT + E
W3_Q, W3_K, W3_V, W3_F = 0, 1024, 1024 + 128, 1024 + 128 + 64
W3_N = W3_F + 2 * 512
W3_STEP = W3_N // 4
W3_PARTS = range(0, W3_N, W3_STEP)
WCH = 2 * E * F // B


def reached(eng, sem, n):
    if isinstance(n, int) and n <= 0:
        return
    eng.wait_ge(sem, n)


def steps(eng, begin, first, last, end, unroll, body, before=None):
    for i in range(begin, first):
        body(i, i % unroll)
    with eng.Fori(first, last + 2 - unroll, unroll) as i:
        if before:
            before(i)
        for u in range(unroll):
            body(i + u if u else i, (first + u) % unroll)
    for i in range(last + 1, end + 1):
        body(i, i % unroll)


def alone(eng, tick, *waits):
    if all(isinstance(n, int) for _, n in waits):
        for sem, n in waits:
            reached(eng, sem, n)
        return
    for sem, n in waits:
        reached(eng, sem, n)
    eng.sem_inc(tick[eng.engine.name], 1)


def read_table(nc, engine, where, top, why):
    return nc.values_load_multi_w_load_instructions(where, engines=[engine], min_val=0, max_val=top,
                                                    skip_runtime_bounds_check_because=why)[1]


def at_step(i, n):
    return isinstance(i, int) and i == n


def inside(i, shift, n=B):
    return not isinstance(i, int) or 0 <= i + shift < n


def build(nc, A):
    ctx = ExitStack()
    with ctx:
        def sb(name, shape, dt=F32):
            return ctx.enter_context(nc.sbuf_tensor(name, shape, dt))

        def sem(name):
            return ctx.enter_context(nc.semaphore(name))

        bank = [ctx.enter_context(nc.psum_tensor(f"bank{n}", [128, 512], F32)) for n in range(8)]

        xs = [nc.dram_tensor(f"sorted{n}", (DUMMY + (E - 1) * 128, PITCH), F32, kind="Internal").ap() for n in range(2)]
        ys = [nc.dram_tensor(f"expert_out{n}", ((1 + n) * B * S + PADS * 128, D), F32, kind="Internal").ap()
              for n in range(2)]

        cst = sb("cst", [128, K_N])
        x = sb("x_sb", [S, B, D])
        cx = sb("cx", [C, B, D])
        wz = sb("wz", [D, G, 128])
        wv0 = sb("wv0", [D, 128])
        zbias = sb("zbias", [128, 1])
        vbias = sb("vbias", [128, 128])
        fcw = sb("fcw", [128, 2, D])
        fcb = sb("fcb", [128, D])
        wred = sb("wred", [16, D])
        wg = sb("wg", [E, 16])
        wgn = sb("wgn", [E, 16])
        wgT = sb("wgT", [16, E])
        wsq = sb("wsq", [E, 4])
        halves = sb("halves", [128, 2])
        router = [sb(f"router{n}", [D, E]) for n in range(2)]
        w_hi = sb("w_hi", [128, 2 * E * F], F16)
        w_lo = sb("w_lo", [128, 2 * E * F], F16)
        w_new = sb("w_new", [128, 2, WCH])
        bias = sb("bias", [64, F + D])
        bias_hl = sb("bias_hl", [64, F + D], F16)
        hotrow = sb("hotrow", [64, E, 128], F16)
        kz = sb("kz", [128, 2, 4, G * C])
        w3 = sb("w3", [D, W3_N])
        w3_hi, w3_lo = (kz[:].rearrange("p s j c -> p (s j c)").bitcast(F16)[:, W3_N * n:W3_N * (n + 1)]
                        for n in range(2))
        wo = sb("wo", [128, 8, D])
        wf2 = sb("wf2", [128, FC, D])
        lnp = sb("lnp", [D, 4])
        identb = sb("identb", [128, 128], BF16)
        trib = sb("trib", [128, 128], BF16)
        oneb = sb("oneb", [128, 128], BF16)
        kbias = sb("kbias", [128, 1])
        sel1 = sb("sel1", [128, 8, C], BF16)
        ident = cst[:, K_ID:K_ID + 128]

        base = sb("base", [128, E])
        slotp = sb("slotp", [128, 2, 2], U32)
        gsum = sb("gsum", [128, B])
        gate = sb("gate", [128, 2, B])
        padrow = sb("padrow", [1, E], I32)
        tcnt = sb("tcnt", [128, 4, E])
        tint = sb("tint", [128, E], I32)
        trow = sb("trow", [1, 3, NT1])
        trow8 = sb("trow8", [1, NT1, E])
        etab = sb("etab", [1, NT1 + 8], I32)
        rtab = sb("rtab", [1, NT1 + 8], I32)

        mv = sb("mv", [128, 2, 2])
        mvc = sb("mvc", [128, 2, 2])
        st6 = sb("st6", [128, 3, 6])
        rst = sb("rst", [128, 2, 4])
        rstt = sb("rstt", [128, 4])
        mv1 = sb("mv1", [128, 2, 2])
        xn = sb("xn", [128, 2, D])
        cn = sb("cn", [C, 2, D])
        xcT = sb("xcT", [128, 2, 256])
        xc_hi = sb("xc_hi", [128, 2, 256], F16)
        xc_lo = sb("xc_lo", [128, 2, 256], F16)
        qf = sb("qf", [128, 2, 1024])
        kf = sb("kf", [128, 2, C])
        qb = sb("qb", [128, 1, 1024], BF16)
        kb = sb("kb", [128, 1, C], BF16)
        kb0 = sb("kb0", [128, G * C], BF16)
        vz = sb("vz", [128, 128])
        v0 = sb("v0", [C, 2, H, 17])
        v1_hi = sb("v1_hi", [C, 2, HD1 + 1], F16)
        v1_lo = sb("v1_lo", [C, 2, HD1 + 1], F16)
        xpb = sb("xpb", [128, 2, D])
        mx0 = sb("mx0", [128, G, 128], BF16)
        mx = sb("mx", [128, 128], BF16)
        mT = sb("mT", [128, 128], BF16)
        PT = sb("PT", [C, 4, 512])
        rec = sb("rec", [128, H])
        on = sb("on", [128, 1024])
        oT = sb("oT", [128, 1024])
        sg = sb("sg", [128, F])
        sgo = sb("sgo", [128, 2, F])
        xr = sb("xr", [128, 2, 2, ROW])
        xrT = sb("xrT", [128, 128])
        lgs = sb("lgs", [128, 8])
        top = sb("top", [128, 8])
        topi = sb("topi", [128, 8], U32)
        topf = sb("topf", [128, 2])
        hot = sb("hot", [128, 3, E], BF16)
        pos = sb("pos", [128, E])
        junk = sb("junk", [128, 8])
        junk2 = sb("junk2", [128, 8])
        slf = sb("slf", [128, 2])
        negm = sb("negm", [128, 1])
        yg = sb("yg", [128, 2, D])
        xt = sb("xt", [128, 4, ROW])
        back = sb("back", [128, 4], U32)
        xt_hi = sb("xt_hi", [128, 4, 128], F16)
        xt_lo = sb("xt_lo", [128, 4, 128], F16)
        hg = sb("hg", [128, 2, F])
        hg_hi = sb("hg_hi", [128, 2, F], F16)
        hg_lo = sb("hg_lo", [128, 2, F], F16)
        yo = sb("yo", [128, 4, D])

        ld_cst, ld_x0, ld_x, ld_w0 = (sem(n) for n in ("ld_cst", "ld_x0", "ld_x", "ld_w0"))
        ld_w1 = sem("ld_w1")
        made = sem("made")
        made_b = sem("made_b")
        ld_wg, ld_x1 = sem("ld_wg"), sem("ld_x1")
        tick = {"DVE": sem("tick_vector"), "Pool": sem("tick_gpsimd")}
        made_p = sem("made_p")
        made_t = sem("made_t")
        made_z = sem("made_z")

        with nc.Block() as block:
            @block.sync
            def _(sp):
                sp.dma_start(cst[:], A["cst"]).then_inc(ld_cst, 16)
                sp.dma_start(x[:, 0:2, :], A["x"][:, 0:2, :]).then_inc(ld_x0, 16)
                sp.dma_start(cx[:, 0:2, :], A["cx"][:, 0:2, :]).then_inc(ld_x0, 16)

            @block.scalar
            def _(act):
                act.dma_start(wg[:], A["wg"]).then_inc(ld_wg, 16)
                for dst, src in ((wz[:], A["wz"]), (zbias[:], A["zb"]), (vbias[:], A["vb"].partition_broadcast(128)),
                                 (wred[:], A["wred"]), (fcw[:], A["fcw"]), (fcb[:], A["fcb"].partition_broadcast(128))):
                    act.dma_start(dst, src).then_inc(ld_w0, 16)

            @block.vector
            def _(v):
                v.memset(mx[:], 0.0).then_inc(made, 1)
                v.memset(mx0[:], 0.0).then_inc(made_b, 1)
                v.memset(bias[:], 0.0).then_inc(made_b, 1)
                v.memset(halves[:, 0:1], -0.5).then_inc(made, 1)
                v.memset(halves[:, 1:2], 0.5).then_inc(made, 1)
                v.memset(v0[:, :, :, 16:17], 1.0).then_inc(made, 1)
                v.memset(v1_hi[:, :, HD1:HD1 + 1], 1.0).then_inc(made, 1)
                v.memset(v1_lo[:, :, HD1:HD1 + 1], 0.0).then_inc(made_b, 1)
                v.wait_ge(ld_wg, 16)
                v.tensor_tensor_reduce(wgn[:], wg[:], wg[:], 1.0, 0.0, ALU.mult, ALU.add,
                                       wsq[:, 0:1]).then_inc(made, 1)
                v.wait_ge(made_p, 1)
                v.tensor_scalar(wsq[:, 2:3], wsq[:, 1:2], 1e-4, None, ALU.max).then_inc(made, 1)
                v.wait_ge(made, 7)
                v.reciprocal(wsq[:, 3:4], wsq[:, 2:3]).then_inc(made, 1)
                v.wait_ge(made, 8)
                v.tensor_scalar(wgn[:], wg[:], wsq[:, 3:4], None, ALU.mult).then_inc(made, 1)
                v.wait_ge(ld_cst, 16)
                v.tensor_copy(identb[:], ident).then_inc(made, 1)
                v.tensor_copy(trib[:], cst[:, K_TRI:K_TRI + 128]).then_inc(made, 1)
                v.tensor_copy(oneb[:], cst[:, K_ONE:K_ONE + 128]).then_inc(made, 1)
                v.tensor_copy(sel1[:].rearrange("p a b -> p (a b)"), cst[:, K_SEL1:K_SEL1 + 8 * C]).then_inc(made, 1)
                v.tensor_copy(base[:], cst[:, K_EOFF:K_EOFF + E]).then_inc(made, 1)
                v.wait_ge(made_t, 1)
                v.tensor_copy(wgT[:], bank[0][0:16, 0:E]).then_inc(made, 1)
                v.wait_ge(ld_w0, 96)
                v.tensor_copy(hotrow[:], cst[0:64, K_HOT:K_HOT + E].rearrange("p (e o) -> p e o", o=1).broadcast_to(
                    [64, E, 128])).then_inc(made_b, 1)
                v.tensor_tensor(wz[:].rearrange("p g c -> p (g c)"), wz[:].rearrange("p g c -> p (g c)"),
                                cst[:, K_SIGN:K_SIGN + 512], ALU.mult).then_inc(made, 1)
                v.tensor_tensor(zbias[:], zbias[:], cst[:, K_SCOL:K_SCOL + 1], ALU.mult).then_inc(made, 1)
                v.wait_ge(made, 17)
                v.tensor_copy(wv0[:].rearrange("p (g j e) -> p g j e", g=G, j=4),
                              wz[:].rearrange("p g (j e) -> p g j e", j=4)[:, :, :, 0:HD0]).then_inc(made, 1)
                v.tensor_tensor(kbias[:], zbias[:], cst[:, K_KEYS:K_KEYS + 1], ALU.add).then_inc(made, 1)
                v.wait_ge(made_t, 2)
                v.tensor_copy(router[0][:], bank[1][:, 0:E]).then_inc(made, 1)

            @block.gpsimd
            def _(pool):
                pool.wait_ge(made, 6)
                pool.tensor_tensor(wsq[:, 1:2], wsq[:, 0:1], halves[0:E, 1:2], ALU.pow).then_inc(made_p, 1)
                pool.memset(kz[:], 0.0).then_inc(made_z, 1)

            @block.tensor
            def _(pe):
                pe.wait_ge(made, 9)
                pe.wait_ge(ld_cst, 16)
                pe.transpose(bank[0][0:16, 0:E], wgn[:], ident[0:E, 0:E]).then_inc(made_t, 1)
                pe.wait_ge(ld_w0, 96)
                pe.wait_ge(made, 15)
                pe.matmul(bank[1][:, 0:E], wred[:], wgT[:], start=True, stop=True).then_inc(made_t, 1)

        def product3(pe, out, left, right, first=True, last=True):
            for n, (a, b) in enumerate(((0, 0), (0, 1), (1, 0))):
                mm = pe.matmul(out, left[a], right[b], start=(first and n == 0), stop=(last and n == 2))
            return mm

        def route(layer, v, p, b, sems, part):
            logits, ranks, totals = sems["logits"], sems["ranks"], sems["totals"]
            chain = sems["chain"]
            K = sems["K"]
            c0 = b * K

            def after(n):
                reached(v, chain, c0 + n)

            if part == 0:
                v.tensor_copy(lgs[:], logits).then_inc(chain, 1)
                alone(v, tick, (chain, c0 + 1))
                v.max(top[:], lgs[:]).then_inc(chain, 1)
                alone(v, tick, (chain, c0 + 2))
                v.max_index(topi[:], top[:], lgs[:]).then_inc(chain, 1)
                if layer == 0:
                    v.tensor_scalar(negm[:], top[:, 0:1], -1.0, None, ALU.mult).then_inc(chain, 1)
                else:
                    v.tensor_tensor(gsum[:, bass.ds(b, 1)], top[:, 1:2], top[:, 0:1],
                                    ALU.subtract).then_inc(chain, 1)
            elif part == 1:
                after(4)
                v.tensor_copy(topf[:], topi[:, 0:2]).then_inc(chain, 1)
                after(5)
                v.tensor_scalar(hot[:, 0, :], cst[:, K_IOTA8:K_IOTA8 + E], topf[:, 0:1], None,
                                ALU.is_equal).then_inc(chain, 1)
                if layer == 1:
                    v.tensor_scalar(hot[:, 1, :], cst[:, K_IOTA8:K_IOTA8 + E], topf[:, 1:2], None,
                                    ALU.is_equal).then_inc(chain, 1)
                    after(7)
                    v.tensor_tensor(hot[:, 2, :], hot[:, 0, :], hot[:, 1, :], ALU.add).then_inc(chain, 1)
            else:
                n = 6 if layer == 0 else 8
                v.tensor_tensor(pos[:], ranks, base[:], ALU.add).then_inc(chain, 1)
                after(n + 1)
                v.tensor_tensor_reduce(junk2[:], pos[:], hot[:, 0, :], 1.0, 0.0, ALU.mult, ALU.add,
                                       slf[:, 0:1]).then_inc(chain, 1)
                if layer == 1:
                    v.tensor_tensor_reduce(junk[:], pos[:], hot[:, 1, :], 1.0, 0.0, ALU.mult, ALU.add,
                                           slf[:, 1:2]).then_inc(chain, 1)
                v.tensor_tensor(base[:], base[:], totals, ALU.add).then_inc(chain, 1)
                n += 3 + layer
                after(n)
                v.tensor_copy(slotp[:, p, 0:1 + layer], slf[:, 0:1 + layer]).then_inc(chain, 1)

        (x_stat, x_rstd, x_norm, tf_done, tf_out, zq_done, zk_done, zv_done, q_exp, k_exp, vz_done, v_exp,
         q_cast, xpb_done) = (sem("a_" + n) for n in (
             "x_stat", "x_rstd", "x_norm", "tf_done", "tf_out", "zq_done", "zk_done", "zv_done", "q_exp",
             "k_exp", "vz_done", "v_exp", "q_cast", "xpb_done"))
        (sm_done, max_done, mt_done, mt_out, st_done, p_exp, pv_done, rec_done, on_done, ot_done, ot_out,
         fc_done, x1_done) = (sem("a_" + n) for n in (
             "sm_done", "max_done", "mt_done", "mt_out", "st_done", "p_exp", "pv_done", "rec_done", "on_done",
             "ot_done", "ot_out", "fc_done", "x1_done"))
        (xr_stat, xr_rstd, xr_norm, tr_done, tr_out, lg_done, rk_done, chain, gexp) = (sem("a_" + n) for n in (
            "xr_stat", "xr_rstd", "xr_norm", "tr_done", "tr_out", "lg_done", "rk_done", "chain", "gexp"))
        scat = [sem(f"a_scat{p}") for p in range(2)]
        c_copy = sem("a_c_copy")
        back0, back1 = sem("a_back"), sem("b_back")
        lo3_out, w3_hi_done = sem("b_lo_out"), sem("w3_hi")
        ROUTE0 = dict(logits=bank[0][:, 0:E], ranks=bank[2][:, 0:E], totals=bank[2][:, 64:64 + E], chain=chain, K=10)

        w_in = [[sem(f"w{layer}_in{p}") for p in range(2)] for layer in range(2)]
        w_split = [sem(f"w{layer}_split") for layer in range(2)]

        def load_weights(eng, layer):
            def load(n, p):
                reached(eng, w_split[layer], 3 * (n - 1))
                eng.dma_start(w_new[:, p, :], A[f"w12_{layer}"][:, bass.ds(n * WCH, WCH)]).then_inc(w_in[layer][p], 16)

            load(0, 0)
            load(1, 1)
            with eng.Fori(2, B - 1, 2) as n:
                load(n, 0)
                load(n + 1, 1)

        def split_weights(pool, layer, n, p):
            alone(pool, tick, (w_in[layer][p], 8 * (n - p) + 16))
            part = bass.ds(n * WCH, WCH)
            pool.tensor_copy(w_hi[:, part], w_new[:, p, :]).then_inc(w_split[layer], 1)
            alone(pool, tick, (w_split[layer], 3 * n + 1))
            pool.tensor_tensor(w_lo[:, part], w_new[:, p, :], w_hi[:, part], ALU.subtract).then_inc(w_split[layer], 2)

        with nc.Block() as block:
            @block.sync
            def _(sp):
                for b0, b1_, ready in ((2, FIRST_X, ld_x1), (FIRST_X, B, ld_x)):
                    sp.dma_start(x[:, b0:b1_, :], A["x"][:, b0:b1_, :]).then_inc(ready, 16)
                    sp.dma_start(cx[:, b0:b1_, :], A["cx"][:, b0:b1_, :]).then_inc(ready, 16)
                for row in (0, 32):
                    sp.dma_start(bias[row:row + E, 0:F], A["b1"]).then_inc(ld_w1, 16)
                    sp.dma_start(bias[row:row + E, F:F + D], A["b2"]).then_inc(ld_w1, 16)
                for dst, src in ((w3[:, W3_Q:W3_K], A["wq"]), (w3[:, W3_K:W3_K + HD1], A["wk"]),
                                 (w3[:, W3_K + HD1:W3_V], A["wk"]), (w3[:, W3_V:W3_F], A["wv"]),
                                 (wo[:], A["wo"]), (w3[:, W3_F:W3_N], A["wf1"]), (wf2[:], A["wf2"]), (lnp[:], A["lnp"]),
                                 (router[1][:], A["router"])):
                    sp.dma_start(dst, src).then_inc(ld_w1, 16)
                load_weights(sp, 0)

            @block.tensor
            def _(pe):
                mtp = bank[3][:, 0:256].bitcast(BF16)

                def body(i, p):
                    q = 1 - p
                    nxt = i + 1 if inside(i, 1) else B - 1

                    def st(j):
                        pe.wait_ge(k_exp, 5 * i + j + 2)
                        for g in range(G):
                            mm = pe.matmul(bank[j][0:C, 128 * g:128 * g + 128], kz[:, p, j, C * g:C * g + C],
                                           qf[:, p, 128 * g:128 * g + 128], start=True, stop=True)
                        mm.then_inc(st_done, 1)

                    def pv(j):
                        pe.wait_ge(p_exp, 4 * i + j + 1)
                        for g in range(G):
                            h = 4 * g + j
                            mm = pe.matmul(bank[7][:, 17 * h:17 * h + 17], PT[:, j, 128 * g:128 * g + 128],
                                           v0[:, p, h, :], start=True, stop=True)
                        mm.then_inc(pv_done, 1)

                    if inside(i, 0):
                        pe.wait_ge(q_exp, i + 1)
                        pe.wait_ge(mt_out, i + 1)
                        st(0)
                        st(1)
                    if inside(i, -2):
                        pe.wait_ge(xr_norm, i - 1)
                        pe.wait_ge(q_exp, nxt + 1)
                        pe.transpose(bank[6][:, 256:384], xr[:, p, 0, 0:D], ident).then_inc(tr_done, 1)
                    if inside(i, -1):
                        pe.wait_ge(q_exp, nxt + 1)
                        pe.wait_ge(on_done, i)
                        for c in range(2):
                            mm = pe.transpose(bank[6][:, 128 * c:128 * c + 128], on[:, 128 * c:128 * c + 128], ident)
                        mm.then_inc(ot_done, 1)
                    if inside(i, 0):
                        pe.wait_ge(v_exp, 2 * i + 2)
                        pv(0)
                        st(2)
                    if inside(i, -2):
                        pe.wait_ge(tr_out, i - 1)
                        pe.matmul(ROUTE0["logits"], xrT[:], router[0][:], start=True, stop=True).then_inc(lg_done, 1)
                    if inside(i, 2):
                        pe.wait_ge(x_norm, i + 3)
                        pe.wait_ge(c_copy, i + 3)
                        reached(pe, vz_done, i + 2)
                        pe.transpose(bank[4][:, 0:128], xn[:, p, :], ident)
                        pe.transpose(bank[4][:, 128:128 + C], cn[:, p, :], ident[0:C, 0:C]).then_inc(tf_done, 1)
                    if inside(i, 0):
                        pv(1)
                        st(3)
                    if inside(i, -2):
                        pe.wait_ge(chain, 10 * (i - 2) + 6)
                        if inside(i, 0):
                            pe.wait_ge(p_exp, 4 * i + 3)
                        pe.matmul(ROUTE0["ranks"], trib[:], hot[:, 0, :], start=True, stop=True)
                        pe.matmul(ROUTE0["totals"], oneb[:], hot[:, 0, :], start=True, stop=True).then_inc(rk_done, 1)
                    if inside(i, -1):
                        pe.wait_ge(ot_out, i)
                        reached(pe, x1_done, i - 1)
                        for c in range(2):
                            mm = pe.matmul(bank[1][:, 0:D], oT[:, 128 * c:128 * c + 128], fcw[:, c, :],
                                           start=(c == 0), stop=(c == 1))
                        mm.then_inc(fc_done, 1)
                    if inside(i, 0):
                        pv(2)
                    if inside(i, 1):
                        pe.wait_ge(q_cast, i + 2)
                        pe.wait_ge(k_exp, 5 * i + 6)
                        for j in range(4):
                            reached(pe, p_exp, 4 * i + j + 1)
                            if j == 1:
                                reached(pe, x1_done, i)
                            if j == 2:
                                reached(pe, chain, 10 * (i - 2) + 9)
                            for g in range(G):
                                mm = pe.matmul(bank[j][:, C * g:C * g + C], qb[32 * j:32 * j + 16, 0, 128 * g:128 * g + 128],
                                               kb0[32 * j:32 * j + 16, C * g:C * g + C], start=True, stop=True)
                            mm.then_inc(sm_done, 1)
                    if inside(i, 2):
                        pe.wait_ge(tf_out, i + 3)
                        for g in range(G):
                            mm = pe.matmul(bank[6][:, 128 * g:128 * g + 128], wz[:, g, :], xcT[:, p, 0:128],
                                           start=True, stop=True)
                        mm.then_inc(zq_done, 1)
                        reached(pe, k_exp, 5 * (i + 2))
                        for g in range(G):
                            mm = pe.matmul(bank[5][:, C * g:C * g + C], wz[:, g, :], xcT[:, p, 128:128 + C],
                                           start=True, stop=True)
                        mm.then_inc(zk_done, 1)
                        pe.matmul(bank[4][0:C, 256:384], xcT[:, p, 128:128 + C], wv0[:], start=True,
                                  stop=True).then_inc(zv_done, 1)
                    if inside(i, 1):
                        pe.wait_ge(max_done, 4 * i + 8)
                        for g in range(G):
                            mm = pe.transpose(mtp[:, 128 * g:128 * g + 128], mx0[:, g, :], identb[:])
                        mm.then_inc(mt_done, 1)
                    if inside(i, 0):
                        pv(3)

                steps(pe, -3, 5, 28, B + 1, 2, body)

            @block.scalar
            def _(act):
                def body(i, p):
                    q = 1 - p

                    def probs(j):
                        act.wait_ge(st_done, 4 * i + j + 1)
                        reached(act, pv_done, 4 * i + j - 3)
                        act.activation(PT[:, j, :], bank[j][0:C, :], ACT.Exp, scale=float(D) ** -0.5).then_inc(p_exp, 1)

                    def keys(s, j):
                        r = 32 * j
                        act.activation(kz[r:r + 32, s, j, :], bank[5][r:r + 32, 0:G * C], ACT.Exp,
                                       bias=kbias[r:r + 32]).then_inc(k_exp, 1)

                    if inside(i, 0):
                        probs(0)
                    if inside(i, 1):
                        keys(q, 2)
                    if inside(i, -2):
                        act.wait_ge(tr_done, i - 1)
                        if inside(i, -1):
                            act.wait_ge(ot_done, i)
                        act.activation(xrT[:], bank[6][:, 256:384], ACT.Copy).then_inc(tr_out, 1)
                    if inside(i, 0):
                        probs(1)
                    if inside(i, 1):
                        keys(q, 3)
                    if inside(i, -1):
                        act.wait_ge(ot_done, i)
                        act.activation(oT[:, 0:256], bank[6][:, 0:256], ACT.Copy).then_inc(ot_out, 1)
                    if inside(i, 0):
                        probs(2)
                    if inside(i, 2):
                        act.wait_ge(tf_done, i + 3)
                        act.activation(xcT[:, p, 0:128 + C], bank[4][:, 0:128 + C], ACT.Copy).then_inc(tf_out, 1)
                    if inside(i, 0):
                        probs(3)
                    if inside(i, 2):
                        act.wait_ge(zq_done, i + 3)
                        act.activation(qf[:, p, 0:512], bank[6][:, :], ACT.Exp, bias=zbias[:]).then_inc(q_exp, 1)
                        act.wait_ge(zk_done, i + 3)
                        act.activation(kb0[:], bank[5][:, 0:G * C], ACT.Exp, bias=zbias[:]).then_inc(k_exp, 1)
                        if at_step(i, -2):
                            act.wait_ge(made_z, 1)
                        keys(p, 0)
                        keys(p, 1)
                        act.wait_ge(vz_done, i + 3)
                        reached(act, pv_done, 4 * i + 4)
                        zv = vz[0:C, :].rearrange("p (h e) -> p h e", e=HD0)
                        act.activation(v0[:, p, :, 0:HD0], zv, ACT.Exp).then_inc(v_exp, 1)
                        act.activation(v0[:, p, :, HD0:16], zv, ACT.Exp, scale=-1.0).then_inc(v_exp, 1)
                    if inside(i, -2):
                        act.wait_ge(chain, 10 * (i - 2) + 4)
                        act.activation(junk[:], lgs[:], ACT.Exp, bias=negm[:],
                                       accum_out=gsum[:, bass.ds(i - 2, 1)]).then_inc(gexp, 1)

                steps(act, -3, 5, 28, B + 1, 2, body)

            @block.vector
            def _(v):
                def body(i, p):
                    q = 1 - p
                    if inside(i, -1):
                        v.wait_ge(pv_done, 4 * i)
                        o = bank[7][:, 0:H * 17].rearrange("p (h e) -> p h e", e=17)
                        v.reciprocal(rec[:].rearrange("p (h e) -> p h e", e=1), o[:, :, 16:17]).then_inc(rec_done, 1)
                        v.wait_ge(rec_done, i)
                        v.tensor_tensor(on[:, 0:256].rearrange("p (h e) -> p h e", e=16), o[:, :, 0:16],
                                        rec[:].rearrange("p (h e) -> p h e", e=1).broadcast_to([128, H, 16]),
                                        ALU.mult).then_inc(on_done, 1)
                    if inside(i, -2):
                        v.wait_ge(xr_rstd, 2 * (i - 1))
                        if inside(i, -4):
                            v.wait_ge(scat[p], 8 * (i - 2 - p))
                        v.tensor_scalar(xr[:, p, 0, 0:D], x[:, bass.ds(i - 2, 1), :].rearrange("p b d -> p (b d)"),
                                        mv1[:, p, 0:1], rst[:, p, 1:2], ALU.subtract, ALU.mult).then_inc(xr_norm, 1)
                    if inside(i, 3):
                        if at_step(i, -3):
                            v.wait_ge(ld_x0, 32)
                            v.wait_ge(made, 20)
                        elif at_step(i, -1):
                            v.wait_ge(ld_x1, 32)
                        elif at_step(i, FIRST_X - 3):
                            v.wait_ge(ld_x, 32)
                        xi = x[:, bass.ds(i + 3, 1), :].rearrange("p b d -> p (b d)")
                        v.bn_stats(st6[:, 0, :], xi).then_inc(x_stat, 1)
                        alone(v, tick, (x_stat, 2 * (i + 3) + 1))
                        v.bn_aggr(mv[:, q, :], st6[:, 0, :]).then_inc(x_stat, 1)
                    if inside(i, -2):
                        v.wait_ge(lg_done, i - 1)
                        reached(v, gexp, i - 2)
                        route(0, v, p, i - 2, ROUTE0, 0)
                        route(0, v, p, i - 2, ROUTE0, 1)
                    if inside(i, -2):
                        v.wait_ge(rk_done, i - 1)
                        route(0, v, p, i - 2, ROUTE0, 2)
                    if inside(i, -1):
                        v.wait_ge(fc_done, i)
                        v.wait_ge(xpb_done, i)
                        xo = x[:, bass.ds(i - 1, 1), :].rearrange("p b d -> p (b d)")
                        v.tensor_tensor(xo, bank[1][:, 0:D], xpb[:, q, :], ALU.add).then_inc(x1_done, 1)

                    def maxima(j):
                        v.wait_ge(sm_done, 4 * i + j + 5)
                        v.tensor_reduce(mx0[:, :, 32 * j + 16], bank[j][:, 0:G * C].rearrange("p (g k) -> p g k", g=G),
                                        AX, ALU.max).then_inc(max_done, 1)

                    if inside(i, 1):
                        maxima(0)
                    if inside(i, -1):
                        alone(v, tick, (x1_done, i))
                        v.bn_stats(st6[:, 1, :], xo).then_inc(xr_stat, 1)
                    if inside(i, 1):
                        maxima(1)
                    if inside(i, -1):
                        alone(v, tick, (xr_stat, 2 * i - 1))
                        v.bn_aggr(mv1[:, q, :], st6[:, 1, :]).then_inc(xr_stat, 1)
                    if inside(i, 1):
                        maxima(2)
                        maxima(3)
                    if inside(i, 2):
                        v.wait_ge(zv_done, i + 3)
                        reached(v, v_exp, 2 * i + 4)
                        v.tensor_tensor(vz[0:C, :], bank[4][0:C, 256:384], vbias[0:C, :], ALU.add).then_inc(vz_done, 1)
                    if inside(i, 1):
                        v.wait_ge(mt_done, i + 2)
                        v.wait_ge(q_cast, i + 2)
                        v.tensor_tensor(qf[:, q, 0:512], qf[:, q, 0:512], mtp_v, ALU.subtract).then_inc(mt_out, 1)
                    if at_step(i, 4):
                        v.wait_ge(ld_w1, 208)
                        v.tensor_copy(bias_hl[:], bias[:]).then_inc(made_b, 1)
                        v.wait_ge(made_b, 5)
                        v.tensor_tensor(bias_hl[32:64, :], bias[32:64, :], bias_hl[32:64, :],
                                           ALU.subtract).then_inc(made_b, 1)
                    if inside(i, 3):
                        v.wait_ge(x_rstd, 2 * (i + 3) + 2)
                        reached(v, tf_done, i + 2)
                        v.tensor_scalar(xn[:, q, :], xi, mv[:, q, 0:1], rst[:, q, 0:1], ALU.subtract,
                                        ALU.mult).then_inc(x_norm, 1)

                mtp_v = bank[3][:, 0:256].bitcast(BF16)
                steps(v, -3, 5, 28, B + 1, 2, body)

            @block.gpsimd
            def _(pool):
                def body(i, p):
                    q = 1 - p
                    if inside(i, 1):
                        reached(pool, sm_done, 4 * (i + 1))
                        alone(pool, tick, (q_exp, i + 2))
                        pool.tensor_copy(qb[:, 0, 0:512], qf[:, q, 0:512]).then_inc(q_cast, 1)
                    if inside(i, 3):
                        if at_step(i, -3):
                            pool.wait_ge(ld_x0, 32)
                        elif at_step(i, -1):
                            pool.wait_ge(ld_x1, 32)
                        elif at_step(i, FIRST_X - 3):
                            pool.wait_ge(ld_x, 32)
                        reached(pool, tf_done, i + 2)
                        pool.tensor_copy(cn[:, q, :], cx[:, bass.ds(i + 3, 1), :].rearrange(
                            "p b d -> p (b d)")).then_inc(c_copy, 1)
                        alone(pool, tick, (x_stat, 2 * (i + 3) + 2), (x_norm, i + 2))
                        pool.tensor_scalar(rstt[:, 0:1], mv[:, q, 1:2], EPS, None, ALU.add).then_inc(x_rstd, 1)
                        pool.wait_ge(x_rstd, 2 * (i + 3) + 1)
                        pool.tensor_tensor(rst[:, q, 0:1], rstt[:, 0:1], halves[:, 0:1], ALU.pow).then_inc(x_rstd, 1)
                    if inside(i, 0):
                        split_weights(pool, 0, i, p)
                    if inside(i, 0):
                        reached(pool, x1_done, i - 1)
                        pool.tensor_tensor(xpb[:, p, :], x[:, bass.ds(i, 1), :].rearrange("p b d -> p (b d)"),
                                           fcb[:], ALU.add).then_inc(xpb_done, 1)
                    if inside(i, -1):
                        alone(pool, tick, (xr_stat, 2 * i))
                        pool.tensor_scalar(rstt[:, 1:2], mv1[:, q, 1:2], EPS, None, ALU.add).then_inc(xr_rstd, 1)
                        pool.wait_ge(xr_rstd, 2 * i - 1)
                        pool.tensor_tensor(rst[:, q, 1:2], rstt[:, 1:2], halves[:, 0:1], ALU.pow).then_inc(xr_rstd, 1)
                    if inside(i, -2):
                        alone(pool, tick, (xr_norm, i - 1))
                        pool.tensor_copy(xr[:, p, 0, D:ROW].bitcast(U32),
                                         cst[:, bass.ds(K_BACK + 2 * (i - 2), 1)]).then_inc(back0, 1)
                        alone(pool, tick, (chain, 10 * (i - 1)), (back0, i - 1))
                        pool.indirect_dma_start(xs[0], bass.IndirectOffsetOnAxis(ap=slotp[:, p, 0:1], axis=0),
                                                xr[:, p, 0, :], None).then_inc(scat[p], 16)

                steps(pool, -3, 5, 28, B + 1, 2, body)

        def table_and_pads(layer, NT, tag):
            tab, pads, pad_zero = sem(tag + "tab"), sem(tag + "pads"), sem(tag + "pad_zero")
            pad = qf[:].rearrange("p a b -> p (a b)")[:, 0:PADS * ROW].rearrange("p (k a) -> p k a", a=ROW)
            if layer == 1:
                ge = sem(tag + "gate_exp")
            with nc.Block() as block:
                @block.vector
                def _(v):
                    count = [0]

                    def step(ins):
                        count[0] += 1
                        ins.then_inc(tab, 1)
                        v.wait_ge(tab, count[0])

                    n, tl, cum, dd = (tcnt[:, k, :] for k in range(4))
                    step(v.tensor_copy(padrow[:], base[0:1, :]))
                    step(v.memset(pad[:, E:PADS, :], 0.0))
                    v.wait_ge(pad_zero, 1)
                    step(v.tensor_copy(pad[:, :, D:ROW].bitcast(U32).rearrange("p k a -> p (k a)"),
                                       cst[:, K_PAD + layer * PADS:K_PAD + (layer + 1) * PADS]))
                    step(v.memset(junk[:], 1.0))
                    step(v.tensor_tensor(n, base[:], cst[:, K_EOFF:K_EOFF + E], ALU.subtract))
                    step(v.tensor_scalar(n, n, 127.0, None, ALU.add))
                    step(v.tensor_copy(tint[:], n))
                    step(v.tensor_scalar(tint[:], tint[:], 7, None, ALU.arith_shift_right))
                    step(v.tensor_copy(tl, tint[:]))
                    step(v.tensor_tensor_scan(cum, junk[:], tl, 0.0, ALU.mult, ALU.add))
                    step(v.tensor_scalar(dd, tl, -128.0, float(REGION), ALU.mult, ALU.add))
                    t = cst[0:1, K_TILE:K_TILE + NT]
                    ex, row, s1 = (trow[:, k, 0:NT] for k in range(3))
                    behind = trow8[:, 0:NT, :]
                    by_expert = lambda a: a[0:1, :].rearrange("p (o e) -> p o e", o=1).broadcast_to([1, NT, E])
                    step(v.tensor_tensor(behind, t.rearrange("p (n o) -> p n o", o=1).broadcast_to([1, NT, E]),
                                         by_expert(cum), ALU.is_ge))
                    step(v.tensor_reduce(ex, behind, AX, ALU.add))
                    step(v.tensor_tensor(behind, behind, by_expert(dd), ALU.mult))
                    step(v.tensor_reduce(s1, behind, AX, ALU.add))
                    step(v.scalar_tensor_tensor(out=row, in0=t, scalar=128.0, in1=s1, op0=ALU.mult, op1=ALU.add))
                    step(v.tensor_copy(rtab[:, 0:NT], row))
                    step(v.tensor_scalar(ex, ex, float(E - 1), None, ALU.min))
                    step(v.tensor_copy(etab[:, 0:NT], ex))
                    step(v.tensor_copy(base[:], cst[:, K_EOFF:K_EOFF + E]))
                    if layer == 0:
                        step(v.reciprocal(gate[:, 0, :], gsum[:]))
                    else:
                        v.wait_ge(ge, 1)
                        step(v.tensor_scalar(gsum[:], gate[:, 1, :], 1.0, None, ALU.add))
                        step(v.reciprocal(gate[:, 0, :], gsum[:]))
                        step(v.tensor_tensor(gate[:, 1, :], gate[:, 1, :], gate[:, 0, :], ALU.mult))

                @block.sync
                def _(sp):
                    sp.wait_ge(tab, 1)
                    rows = read_table(nc, mybir.EngineType.SP, padrow[0:1, :], DUMMY - 128,
                                      "an expert has at most B*S tokens, and its region a tile more")
                    sp.wait_ge(tab, 3)
                    for e in range(E):
                        sp.dma_start(xs[layer][bass.ds(rows[e], 128), 0:ROW], pad[:, e, :]).then_inc(pads, 16)
                    sp.dma_start(xs[layer][DUMMY:DUMMY + (E - 1) * 128, 0:ROW].rearrange("(k s) a -> s k a", s=128),
                                 pad[:, E:PADS, :]).then_inc(pads, 16)
                    sp.wait_ge(pads, 16 * (E + 1))

                @block.scalar
                def _(act):
                    if layer == 0:
                        act.wait_ge(ld_w1, 208)
                        for c0 in W3_PARTS:
                            act.activation(w3_hi[:, c0:c0 + W3_STEP], w3[:, c0:c0 + W3_STEP],
                                           ACT.Copy).then_inc(w3_hi_done, 1)
                    else:
                        act.activation(gate[:, 1, :], gsum[:], ACT.Exp).then_inc(ge, 1)

                @block.gpsimd
                def _(pool):
                    pool.memset(pad[:, 0:E, :], 0.0).then_inc(pad_zero, 1)
                    if layer == 0:
                        for n, c0 in enumerate(W3_PARTS):
                            pool.wait_ge(w3_hi_done, n + 1)
                            pool.tensor_tensor(w3_lo[:, c0:c0 + W3_STEP], w3[:, c0:c0 + W3_STEP],
                                               w3_hi[:, c0:c0 + W3_STEP], ALU.subtract)
                    for q in range(2):
                        if layer == 0:
                            pool.wait_ge(scat[q], 8 * B)
                        else:
                            pool.wait_ge(scat2[q], 16 * B)

        table_and_pads(0, NT0, "t0_")

        def experts(layer, NT, tag):
            last = NT - 7
            x_in = [sem(f"{tag}x_in{k}") for k in range(4)]
            y_out = [sem(f"{tag}y_out{k}") for k in range(4)]
            back_out = sem(tag + "back_out")
            xbank = bank[2], bank[3], bank[6], bank[7]
            (t_done, hi_out, lo_out, h_done, g_done, lo_done, y_done, y_sb) = (
                sem(tag + n) for n in ("t_done", "hi_out", "lo_out", "h_done", "g_done", "lo_done", "y_done", "y_sb"))
            with nc.Block() as block:
                @block.sync
                def _(sp):
                    ahead = []

                    def table(where):
                        return read_table(nc, mybir.EngineType.SP, rtab[0:1, where], DUMMY + (E - 2) * 128,
                                          "rows of tiles in use and of the E-1 behind them")

                    def before(t):
                        ahead[:] = table(bass.ds(t + 4, 4))

                    def load(t, k, r):
                        reached(sp, t_done, t - 3)
                        reached(sp, back_out, t - 3)
                        sp.dma_start(xt[:, k, :], xs[layer][bass.ds(r, 128), 0:ROW]).then_inc(x_in[k], 16)

                    def body(t, k):
                        if at_step(t, -3):
                            first = table(slice(0, 4))
                            for n in range(4):
                                load(n, n, first[n])
                        elif at_step(t, -2) or at_step(t, -1):
                            pass
                        elif inside(t, 4, NT):
                            load(t + 4, k, table(slice(t + 4, t + 5))[0] if isinstance(t, int) else ahead[(k - 1) % 4])

                    steps(sp, -3, 5, last, NT, 4, body, before)

                @block.gpsimd
                def _(pool):
                    def body(t, k):
                        k1 = (k - 1) % 4
                        if inside(t, 1, NT):
                            k1 = (k + 1) % 4
                            if inside(t, -3, NT):
                                pool.wait_ge(y_out[k1], 4 * (t + 1 - k1))
                            alone(pool, tick, (t_done, t + 2))
                            pool.tensor_copy(back[:, k1:k1 + 1], xt[:, k1, D:ROW].bitcast(U32)).then_inc(back_out, 1)
                        if inside(t, -1, NT):
                            k1 = (k - 1) % 4
                            alone(pool, tick, (y_sb, t), (back_out, t))
                            pool.indirect_dma_start(ys[layer], bass.IndirectOffsetOnAxis(ap=back[:, k1:k1 + 1], axis=0),
                                                    yo[:, k1, :], None).then_inc(y_out[k1], 16)

                    steps(pool, -3, 5, last, NT, 4, body)
                    for k in range(4):
                        pool.wait_ge(y_out[k], 16 * len(range(k, NT, 4)))

                @block.tensor
                def _(pe):
                    U = 8
                    ahead = []

                    def table(where):
                        return read_table(nc, mybir.EngineType.PE, etab[0:1, where], E - 1,
                                          "the table's numbers were cut to 0..E-1")

                    def before(t):
                        ahead[:] = table(bass.ds(t - 1, U + 2))

                    def expert(t, k, shift):
                        return table(slice(t + shift, t + shift + 1))[0] if isinstance(t, int) else ahead[(k - 5) % U + shift + 1]

                    def body(t, k):
                        p = k % 2
                        k4 = k % 4
                        if inside(t, 3, NT):
                            k3 = (k4 + 3) % 4
                            pe.wait_ge(x_in[k3], 4 * (t + 3 - k3) + 16)
                            pe.transpose(xbank[k3][:, 0:128], xt[:, k3, 0:D], ident).then_inc(t_done, 1)
                        if inside(t, -1, NT):
                            e = expert(t, k, -1)
                            pe.wait_ge(lo_done, t)
                            o = bank[5 - p][:, 0:D]
                            if layer == 0:
                                pe.matmul(o, hotrow[:].rearrange("p e n -> p (e n)")[:, bass.ds(e * 128, 128)],
                                          bias_hl[:, F:F + D], start=True, stop=False)
                            for c in range(FC):
                                at = bass.ds(e * F + (E * F + c * 128), 128)
                                hi, lo = (h[:, 1 - p, 128 * c:128 * c + 128] for h in (hg_hi, hg_lo))
                                pe.matmul(o, hi, w_hi[:, at], start=(layer == 1 and c == 0), stop=False)
                                pe.matmul(o, hi, w_lo[:, at], start=False, stop=False)
                                mm = pe.matmul(o, lo, w_hi[:, at], start=False, stop=(c == FC - 1))
                            mm.then_inc(y_done, 1)
                        if inside(t, 1, NT):
                            e = expert(t, k, 1)
                            pe.wait_ge(lo_out, t + 2)
                            for c in range(FC):
                                o = bank[1 - p][:, 128 * c:128 * c + 128]
                                if layer == 0:
                                    pe.matmul(o, bias_hl[:, 128 * c:128 * c + 128],
                                              hotrow[:].rearrange("p e n -> p (e n)")[:, bass.ds(e * 128, 128)],
                                              start=True, stop=False)
                                at = bass.ds(e * F + c * 128, 128)
                                pe.matmul(o, w_hi[:, at], xt_hi[:, (k4 + 1) % 4, :], start=(layer == 1), stop=False)
                                pe.matmul(o, w_hi[:, at], xt_lo[:, (k4 + 1) % 4, :], start=False, stop=False)
                                mm = pe.matmul(o, w_lo[:, at], xt_hi[:, (k4 + 1) % 4, :], start=False, stop=True)
                            mm.then_inc(h_done, 1)

                    steps(pe, -3, 5, 4 + (last - 4) // U * U, NT, U, body, before)

                @block.scalar
                def _(act):
                    def body(t, k):
                        p = k % 2
                        if inside(t, 3, NT):
                            k3 = (k + 3) % 4
                            act.wait_ge(t_done, t + 4)
                            reached(act, h_done, t)
                            act.activation(xt_hi[:, k3, :], xbank[k3][:, 0:128], ACT.Copy).then_inc(hi_out, 1)
                        if inside(t, 1, NT):
                            act.wait_ge(h_done, t + 2)
                            reached(act, lo_done, t)
                            act.activation(hg[:, 1 - p, :], bank[1 - p][:, :], ACT.Gelu).then_inc(g_done, 1)
                            reached(act, y_done, t)
                            act.activation(hg_hi[:, 1 - p, :], bank[1 - p][:, :], ACT.Gelu).then_inc(g_done, 1)

                    steps(act, -3, 5, last, NT, 4, body)

                @block.vector
                def _(v):
                    def body(t, k):
                        p = k % 2
                        if inside(t, 3, NT):
                            k3 = (k + 3) % 4
                            v.wait_ge(hi_out, t + 4)
                            v.tensor_tensor(xt_lo[:, k3, :], xbank[k3][:, 0:128], xt_hi[:, k3, :],
                                            ALU.subtract).then_inc(lo_out, 1)
                        if inside(t, -1, NT):
                            v.wait_ge(y_done, t)
                            k1 = (k - 1) % 4
                            if inside(t, -5, NT):
                                v.wait_ge(y_out[k1], 4 * (t - 1 - k1))
                            v.tensor_copy(yo[:, k1, :], bank[5 - p][:, 0:D]).then_inc(y_sb, 1)
                        if inside(t, 1, NT):
                            v.wait_ge(g_done, 2 * t + 4)
                            reached(v, y_done, t)
                            v.tensor_tensor(hg_lo[:, 1 - p, :], hg[:, 1 - p, :], hg_hi[:, 1 - p, :],
                                            ALU.subtract).then_inc(lo_done, 1)

                    steps(v, -3, 5, last, NT, 4, body)

        experts(0, NT0, "e0_")

        scat2 = [sem(f"b_scat{p}") for p in range(2)]
        y_in = [sem(f"b_y_in{p}") for p in range(2)]
        (x2_done, x_stat, c_stat, x_rstd, x_norm, c_norm, tf_done, tf_out, q_done, q_out, kv_done, kv_out,
         q_cast) = (sem("b_" + n) for n in (
             "x2_done", "x_stat", "c_stat", "x_rstd", "x_norm", "c_norm", "tf_done", "tf_out", "q_done", "q_out",
             "kv_done", "kv_out", "q_cast"))
        (sm_done, max_done, mt_done, mt_out, st_done, p_exp, pv_done, rec_done, on_done, ot_done, ot_out,
         ff_done, g_tanh, s_step, x3_done, acc_done) = (sem("b_" + n) for n in (
             "sm_done", "max_done", "mt_done", "mt_out", "st_done", "p_exp", "pv_done", "rec_done", "on_done",
             "ot_done", "ot_out", "ff_done", "g_tanh", "s_step", "x3_done", "acc_done"))
        p_lo, v_lo = sem("b_p_lo"), sem("b_v_lo")
        (xr_stat, xr_rstd, xr_norm, xr_copy, tr_done, tr_out, lg_done, rk_done, chain) = (sem("b_" + n) for n in (
            "xr_stat", "xr_rstd", "xr_norm", "xr_copy", "tr_done", "tr_out", "lg_done", "rk_done", "chain"))
        K1 = 13
        ROUTE1 = dict(logits=bank[7][:, 0:E], ranks=bank[7][:, 128:128 + E],
                      totals=bank[7][:, 256:256 + E], chain=chain, K=K1)

        P_hi = hg[:].rearrange("p a f -> p (a f)").bitcast(F16).rearrange("p (k f) -> p k f", k=4)
        P_lo = [(hg_hi, hg_lo)[k // 2][:, k % 2, :] for k in range(4)]

        with nc.Block() as block:
            @block.sync
            def _(sp):
                def load(b, p):
                    reached(sp, x2_done, b - 1)
                    sp.dma_start(yg[:, p, :], ys[0][bass.ds(b * S, S), :]).then_inc(y_in[p], 16)

                def load_w(b, p):
                    reached(sp, w_split[1], 3 * (b - 1))
                    sp.dma_start(w_new[:, p, :], A["w12_1"][:, bass.ds(b * WCH, WCH)]).then_inc(w_in[1][p], 16)

                for b in range(6):
                    load(b, b % 2)
                    if b >= 4:
                        load_w(b - 4, b % 2)
                with sp.Fori(6, B - 1, 2) as b:
                    for p in range(2):
                        load(b + p if p else b, p)
                        load_w(b + (p - 4), p)
                for b in range(B - 4, B):
                    load_w(b, b % 2)

            @block.tensor
            def _(pe):
                mtp = bank[2][:, 0:64].bitcast(BF16)

                def body(i, p):
                    q = 1 - p
                    nxt = i + 1 if inside(i, 1) else B - 1
                    xT, cT = (tuple(h[:, p, part] for h in (xc_hi, xc_lo)) for part in (slice(0, 128), slice(128, 128 + C)))

                    def w(c0, n):
                        return w3_hi[:, c0:c0 + n], w3_lo[:, c0:c0 + n]

                    def smax(k):
                        r, c0 = 64 * (k // 2), 4 * (k % 2)
                        if k < 2:
                            reached(pe, on_done, 4 * i + k + 1)
                        else:
                            pe.wait_ge(max_done, 4 * i + k + 3)
                        for c in range(4):
                            mm = pe.matmul(bank[k % 2][:, C * c:C * c + C], qb[r:r + 64, 0, 128 * (c0 + c):128 * (c0 + c) + 128],
                                           kb[r:r + 64, 0, 0:C], start=True, stop=True)
                        mm.then_inc(sm_done, 1)

                    def st(k):
                        r, c0 = 64 * (k // 2), 4 * (k % 2)
                        for c in range(4):
                            o = bank[k][0:C, 128 * c:128 * c + 128]
                            pe.matmul(o, kf[r:r + 64, p, 0:C],
                                      qf[r:r + 64, p, 128 * (c0 + c):128 * (c0 + c) + 128], start=True, stop=False)
                            mm = pe.matmul(o, sel1[r:r + 64, c0 + c, :], mT[r:r + 64, :], start=False, stop=True)
                        mm.then_inc(st_done, 1)

                    def pv(k):
                        pe.wait_ge(p_lo, 4 * i + k + 1)
                        for c in range(4):
                            o = bank[k][:, 65 * c:65 * c + 65]
                            hi, lo = P_hi[0:C, k, 128 * c:128 * c + 128], P_lo[k][0:C, 128 * c:128 * c + 128]
                            pe.matmul(o, hi, v1_hi[:, p, :], start=True, stop=False)
                            pe.matmul(o, hi, v1_lo[:, p, :], start=False, stop=False)
                            mm = pe.matmul(o, lo, v1_hi[:, p, :], start=False, stop=True)
                        mm.then_inc(pv_done, 1)

                    if inside(i, 0):
                        pe.wait_ge(kv_out, 3 * i + 3)
                        pe.wait_ge(q_out, 2 * i + 2)
                        pe.wait_ge(mt_out, i + 1)
                        st(0)
                        st(1)
                    if inside(i, -1):
                        reached(pe, x3_done, i - 1)
                        pe.wait_ge(on_done, 4 * i)
                        for c in range(4):
                            mm = pe.transpose(bank[6][:, 128 * c:128 * c + 128], on[:, 128 * c:128 * c + 128], ident)
                        mm.then_inc(ot_done, 1)
                        pe.wait_ge(kv_out, 3 * nxt + 3)
                        pe.wait_ge(v_lo, nxt + 1)
                        for c in range(4):
                            mm = pe.transpose(bank[7][:, 128 * c:128 * c + 128], on[:, 512 + 128 * c:512 + 128 * c + 128], ident)
                        mm.then_inc(ot_done, 1)
                    if inside(i, 0):
                        pe.wait_ge(q_out, 2 * nxt + 2)
                        for k, half in enumerate((1, 0)):
                            for c in range(FC):
                                mm = product3(pe, bank[4 + k][:, 128 * c:128 * c + 128],
                                              w(W3_F + half * F + 128 * c, 128), xT)
                            mm.then_inc(ff_done, 1)
                    if inside(i, -1):
                        pe.wait_ge(ot_out, 2 * i)
                    if inside(i, -2):
                        pe.wait_ge(xr_norm, i - 1)
                        pe.transpose(bank[7][:, 256:384], xr[:, p, 0, 0:D], ident).then_inc(tr_done, 1)
                    if inside(i, 0):
                        pe.wait_ge(v_lo, i + 1)
                        pv(0)
                        st(2)
                    if inside(i, -2):
                        pe.wait_ge(tr_out, i - 1)
                        pe.matmul(ROUTE1["logits"], xrT[:], router[1][:], start=True, stop=True).then_inc(lg_done, 1)
                    if inside(i, 0):
                        st(3)
                    if inside(i, 2):
                        pe.wait_ge(x_norm, i + 3)
                        pe.wait_ge(c_norm, i + 3)
                        if inside(i, -2):
                            pe.wait_ge(chain, K1 * (i - 2) + 1)
                        else:
                            reached(pe, kv_out, 3 * (i + 2))
                            reached(pe, v_lo, i + 2)
                        pe.transpose(bank[7][:, 0:128], xn[:, p, :], ident)
                        pe.transpose(bank[7][:, 128:128 + C], cn[:, p, :], ident[0:C, 0:C]).then_inc(tf_done, 1)
                    if inside(i, 0):
                        pv(1)
                        pv(2)
                    if inside(i, 1):
                        pe.wait_ge(q_cast, 2 * i + 4)
                        pe.wait_ge(kv_out, 3 * i + 6)
                        smax(0)
                    if inside(i, -1):
                        pe.wait_ge(s_step, 2 * i)
                        pe.wait_ge(ot_out, 2 * i)
                        for c in range(FC):
                            pe.matmul(bank[6][:, 0:D], sgo[:, q, 128 * c:128 * c + 128], wf2[:, c, :],
                                      start=(c == 0), stop=False)
                    if inside(i, 1):
                        smax(1)
                    if inside(i, 0):
                        pv(3)
                    if inside(i, -2):
                        pe.wait_ge(chain, K1 * (i - 2) + 8)
                        if inside(i, 2):
                            pe.wait_ge(tf_out, 4 * i + 12)
                        pe.matmul(ROUTE1["ranks"], trib[:], hot[:, 2, :], start=True, stop=True)
                        pe.matmul(ROUTE1["totals"], oneb[:], hot[:, 2, :], start=True, stop=True).then_inc(rk_done, 1)
                    if inside(i, 1):
                        smax(2)
                    if inside(i, -1):
                        for c in range(4):
                            pe.matmul(bank[6][:, 0:D], oT[:, 128 * c:128 * c + 128], wo[:, c, :],
                                      start=False, stop=False)
                    if inside(i, 1):
                        smax(3)
                    if inside(i, 2):
                        pe.wait_ge(lo3_out, i + 3)
                        reached(pe, s_step, 2 * i + 2)
                        for k in range(2):
                            for c in range(4):
                                mm = product3(pe, bank[4 + k][:, 128 * c:128 * c + 128],
                                              w(W3_Q + 128 * (4 * k + c), 128), xT)
                            mm.then_inc(q_done, 1)
                    if inside(i, 1):
                        pe.wait_ge(max_done, 4 * i + 8)
                        reached(pe, on_done, 4 * i + 3)
                        pe.transpose(mtp, mx[:], identb[:]).then_inc(mt_done, 1)
                    if inside(i, -1):
                        for c in range(4, 8):
                            mm = pe.matmul(bank[6][:, 0:D], oT[:, 128 * c:128 * c + 128], wo[:, c, :],
                                           start=False, stop=(c == 7))
                        mm.then_inc(acc_done, 1)
                    if inside(i, 2):
                        if inside(i, -2):
                            pe.wait_ge(chain, K1 * (i - 2) + 12)
                        product3(pe, bank[7][:, 0:C], w(W3_K, 128), cT)
                        product3(pe, bank[7][0:C, 128:128 + HD1], cT, w(W3_V, HD1)).then_inc(kv_done, 1)

                pe.wait_ge(ld_w1, 208)
                steps(pe, -3, 5, 28, B + 1, 2, body)

            @block.scalar
            def _(act):
                def body(i, p):
                    q = 1 - p

                    def probs(k):
                        act.wait_ge(st_done, 4 * i + k + 1)
                        reached(act, pv_done, 4 * i + k - 3)
                        act.activation(PT[:, k, :], bank[k][0:C, :], ACT.Exp, scale=float(HD1) ** -0.5).then_inc(p_exp, 1)
                        act.activation(P_hi[0:C, k, :], bank[k][0:C, :], ACT.Exp,
                                       scale=float(HD1) ** -0.5).then_inc(p_exp, 1)

                    if inside(i, 0):
                        probs(0)
                        probs(1)
                    if inside(i, -1):
                        act.wait_ge(ot_done, 2 * i - 1)
                        act.activation(oT[:, 0:512], bank[6][:, :], ACT.Copy).then_inc(ot_out, 1)
                        act.wait_ge(ot_done, 2 * i)
                        act.activation(oT[:, 512:1024], bank[7][:, :], ACT.Copy).then_inc(ot_out, 1)
                    if inside(i, 0):
                        act.wait_ge(ff_done, 2 * i + 1)
                        act.activation(sg[:], bank[4][:, :], ACT.Tanh, scale=0.5).then_inc(g_tanh, 1)
                    if inside(i, -2):
                        act.wait_ge(tr_done, i - 1)
                        act.activation(xrT[:], bank[7][:, 256:384], ACT.Copy).then_inc(tr_out, 1)
                    if inside(i, 0):
                        probs(2)
                        probs(3)
                    if inside(i, 2):
                        act.wait_ge(tf_done, i + 3)
                        reached(act, lo3_out, i + 2)
                        for dst in (xcT[:, 0, :], xc_hi[:, p, :]):
                            act.activation(dst[:, 0:128], bank[7][:, 0:128], ACT.Identity, bias=lnp[:, 1:2],
                                           scale=lnp[:, 0:1]).then_inc(tf_out, 1)
                            act.activation(dst[:, 128:128 + C], bank[7][:, 128:128 + C], ACT.Identity,
                                           bias=lnp[:, 3:4], scale=lnp[:, 2:3]).then_inc(tf_out, 1)
                    if inside(i, 2):
                        for k in range(2):
                            act.wait_ge(q_done, 2 * i + 5 + k)
                            act.activation(qf[:, p, 512 * k:512 * k + 512], bank[4 + k][:, :], ACT.Copy).then_inc(q_out, 1)
                        act.wait_ge(kv_done, i + 3)
                        act.activation(kf[:, p, 0:C], bank[7][:, 0:C], ACT.Copy).then_inc(kv_out, 1)
                        act.activation(kb[:, 0, 0:C], bank[7][:, 0:C], ACT.Copy).then_inc(kv_out, 1)
                        act.activation(v1_hi[:, p, 0:HD1], bank[7][0:C, 128:128 + HD1], ACT.Copy).then_inc(kv_out, 1)

                act.wait_ge(ld_w1, 208)
                steps(act, -3, 5, 28, B + 1, 2, body)

            @block.vector
            def _(v):
                def body(i, p):
                    q = 1 - p

                    def norm_o(k):
                        r, c0 = k // 2, 4 * (k % 2)
                        o = bank[k][:, 0:4 * 65].rearrange("p (c e) -> p c e", e=65)
                        rk = rec[:, 4 * k:4 * k + 4].rearrange("p (c e) -> p c e", e=1)
                        v.wait_ge(pv_done, 4 * i + k + 1)
                        v.reciprocal(rk, o[:, :, 64:65]).then_inc(rec_done, 1)
                        v.wait_ge(rec_done, 4 * i + k + 1)
                        if k == 0:
                            reached(v, ot_done, 2 * i)
                        dst = on[:].rearrange("p (c r e) -> p c r e", c=8, r=2)[:, c0:c0 + 4, r, :]
                        v.tensor_tensor(dst, o[:, :, 0:64], rk.broadcast_to([128, 4, 64]),
                                        ALU.mult).then_inc(on_done, 1)

                    def top(k):
                        v.wait_ge(sm_done, 4 * i + k + 5)
                        m0 = 64 * (k // 2) + 4 * (k % 2)
                        v.tensor_reduce(mx[:, m0:m0 + 4], bank[k % 2][:, 0:4 * C].rearrange("p (g k) -> p g k", g=4),
                                        AX, ALU.max).then_inc(max_done, 1)

                    if inside(i, -2):
                        v.wait_ge(acc_done, i - 1)
                        xo = x[:, bass.ds(i - 2, 1), :].rearrange("p b d -> p (b d)")
                        v.tensor_tensor(xo, bank[6][:, 0:D], xo, ALU.add).then_inc(x3_done, 1)
                        alone(v, tick, (x3_done, i - 1))
                        v.bn_stats(st6[:, 1, :], xo).then_inc(xr_stat, 1)
                        alone(v, tick, (xr_stat, 2 * (i - 2) + 1))
                        v.bn_aggr(mv1[:, p, :], st6[:, 1, :]).then_inc(xr_stat, 1)
                    if inside(i, 3):
                        xi = x[:, bass.ds(i + 3, 1), :].rearrange("p b d -> p (b d)")
                        ci = cx[:, bass.ds(i + 3, 1), :].rearrange("p b d -> p (b d)")
                        v.wait_ge(y_in[q], 8 * (i + 3 - q) + 16)
                        v.scalar_tensor_tensor(out=xi, in0=yg[:, q, :], scalar=gate[:, 0, bass.ds(i + 3, 1)],
                                               in1=xi, op0=ALU.mult, op1=ALU.add).then_inc(x2_done, 1)
                        v.bn_stats(st6[0:C, 2, :], ci).then_inc(c_stat, 1)
                        alone(v, tick, (x2_done, i + 4))
                        v.bn_stats(st6[:, 0, :], xi).then_inc(x_stat, 1)
                        alone(v, tick, (c_stat, 2 * (i + 3) + 1))
                        v.bn_aggr(mvc[0:C, q, :], st6[0:C, 2, :]).then_inc(c_stat, 1)
                        alone(v, tick, (x_stat, 2 * (i + 3) + 1))
                        v.bn_aggr(mv[:, q, :], st6[:, 0, :]).then_inc(x_stat, 1)
                    if inside(i, -2):
                        v.wait_ge(xr_rstd, 2 * (i - 1))
                        if inside(i, -4):
                            v.wait_ge(scat2[p], 16 * (i - 2 - p))
                        v.tensor_scalar(xr[:, p, 0, 0:D], x[:, bass.ds(i - 2, 1), :].rearrange("p b d -> p (b d)"),
                                        mv1[:, p, 0:1], rst[:, p, 1:2], ALU.subtract, ALU.mult).then_inc(xr_norm, 1)

                    def low(k):
                        v.wait_ge(p_exp, 8 * i + 2 * k + 2)
                        reached(v, pv_done, 4 * i + k - 3)
                        v.tensor_tensor(P_lo[k][0:C, :], PT[:, k, :], P_hi[0:C, k, :], ALU.subtract).then_inc(p_lo, 1)

                    if inside(i, 0):
                        low(0)
                        low(1)
                    if inside(i, 0):
                        v.wait_ge(g_tanh, i + 1)
                        v.scalar_tensor_tensor(out=sg[:], in0=sg[:], scalar=1.0, in1=bank[4][:, :], op0=ALU.add,
                                               op1=ALU.mult).then_inc(s_step, 1)
                        v.wait_ge(s_step, 2 * i + 1)
                        v.wait_ge(ff_done, 2 * i + 2)
                        v.scalar_tensor_tensor(out=sgo[:, p, :], in0=sg[:], scalar=0.5, in1=bank[5][:, :],
                                               op0=ALU.mult, op1=ALU.mult).then_inc(s_step, 1)
                        norm_o(0)
                    if inside(i, -2):
                        v.wait_ge(lg_done, i - 1)
                        route(1, v, p, i - 2, ROUTE1, 0)
                    if inside(i, 0):
                        low(2)
                    if inside(i, -2):
                        route(1, v, p, i - 2, ROUTE1, 1)
                    if inside(i, 0):
                        norm_o(1)
                        low(3)
                    if inside(i, 1):
                        top(0)
                    if inside(i, 0):
                        norm_o(2)
                    if inside(i, 1):
                        top(1)
                    if inside(i, 0):
                        norm_o(3)
                    if inside(i, 1):
                        top(2)
                        top(3)
                    if inside(i, -2):
                        v.wait_ge(rk_done, i - 1)
                        route(1, v, p, i - 2, ROUTE1, 2)
                    if inside(i, 1):
                        v.wait_ge(mt_done, i + 2)
                        v.tensor_copy(mT[:], bank[2][:, 0:64].bitcast(BF16)).then_inc(mt_out, 1)
                    if inside(i, 3):
                        v.wait_ge(x_rstd, 4 * (i + 3) + 4)
                        reached(v, tf_done, i + 2)
                        v.tensor_scalar(xn[:, q, :], xi, mv[:, q, 0:1], rst[:, q, 0:1], ALU.subtract,
                                        ALU.mult).then_inc(x_norm, 1)
                        v.tensor_scalar(cn[:, q, :], ci, mvc[0:C, q, 0:1], rst[0:C, q, 2:3], ALU.subtract,
                                        ALU.mult).then_inc(c_norm, 1)
                    if inside(i, 2):
                        v.wait_ge(kv_out, 3 * i + 9)
                        v.tensor_tensor(v1_lo[:, p, 0:HD1], bank[7][0:C, 128:128 + HD1], v1_hi[:, p, 0:HD1],
                                        ALU.subtract).then_inc(v_lo, 1)

                steps(v, -3, 5, 28, B + 1, 2, body)

            @block.gpsimd
            def _(pool):
                def body(i, p):
                    q = 1 - p
                    if inside(i, -2):
                        alone(pool, tick, (xr_stat, 2 * (i - 1)))
                        pool.tensor_scalar(rstt[:, 1:2], mv1[:, p, 1:2], EPS, None, ALU.add).then_inc(xr_rstd, 1)
                        pool.wait_ge(xr_rstd, 2 * (i - 2) + 1)
                        pool.tensor_tensor(rst[:, p, 1:2], rstt[:, 1:2], halves[:, 0:1], ALU.pow).then_inc(xr_rstd, 1)
                    if inside(i, 1):
                        reached(pool, sm_done, 4 * (i + 1))
                        alone(pool, tick, (q_out, 2 * i + 3))
                        pool.tensor_copy(qb[:, 0, 0:512], qf[:, q, 0:512]).then_inc(q_cast, 1)
                    if inside(i, 3):
                        alone(pool, tick, (x_stat, 2 * (i + 3) + 2), (c_stat, 2 * (i + 3) + 2))
                        pool.tensor_scalar(rstt[:, 0:1], mv[:, q, 1:2], 1.0 + EPS, EPS * EPS, ALU.mult,
                                           ALU.add).then_inc(x_rstd, 1)
                        pool.tensor_scalar(rstt[0:C, 2:3], mvc[0:C, q, 1:2], EPS, None, ALU.add).then_inc(x_rstd, 1)
                        pool.wait_ge(x_rstd, 4 * (i + 3) + 2)
                        pool.tensor_tensor(rst[:, q, 0:1], rstt[:, 0:1], halves[:, 0:1], ALU.pow).then_inc(x_rstd, 1)
                        pool.tensor_tensor(rst[0:C, q, 2:3], rstt[0:C, 2:3], halves[0:C, 0:1],
                                           ALU.pow).then_inc(x_rstd, 1)
                    if inside(i, 1):
                        alone(pool, tick, (q_out, 2 * i + 4))
                        pool.tensor_copy(qb[:, 0, 512:1024], qf[:, q, 512:1024]).then_inc(q_cast, 1)
                    if inside(i, 2):
                        alone(pool, tick, (tf_out, 4 * i + 12))
                        pool.tensor_tensor(xc_lo[:, p, 0:128 + C], xcT[:, 0, 0:128 + C], xc_hi[:, p, 0:128 + C],
                                           ALU.subtract).then_inc(lo3_out, 1)
                    if inside(i, 0) and not inside(i, -2):
                        split_weights(pool, 1, i, p)
                    if inside(i, -2):
                        alone(pool, tick, (xr_norm, i - 1))
                        pool.tensor_copy(xr[:, p, 1, 0:D], xr[:, p, 0, 0:D]).then_inc(xr_copy, 1)
                        pool.tensor_copy(xr[:, p, :, D:ROW].bitcast(U32).rearrange("p a b -> p (a b)"),
                                         cst[:, bass.ds(K_BACK + 2 * (i - 2), 2)]).then_inc(back1, 1)
                        if inside(i, 0):
                            split_weights(pool, 1, i, p)
                        alone(pool, tick, (chain, K1 * (i - 1)), (back1, i - 1), (xr_copy, i - 1))
                        for n in range(2):
                            pool.indirect_dma_start(xs[1], bass.IndirectOffsetOnAxis(ap=slotp[:, p, n:n + 1], axis=0),
                                                    xr[:, p, n, :], None).then_inc(scat2[p], 16)

                steps(pool, -3, 5, 28, B + 1, 2, body)

        table_and_pads(1, NT1, "t1_")
        experts(1, NT1, "e1_")

        CH = 8
        y1, y2 = (w[:].bitcast(F32).rearrange("p (b d) -> p b d", d=D) for w in (w_hi, w_lo))
        y_in = [sem(f"c_y_in{n}") for n in range(B // CH)]
        first, second, o_store = sem("c_first"), sem("c_second"), sem("o_store")
        with nc.Block() as block:
            def load(eng, n, y, row0):
                src = ys[1][row0 + n * CH * S:row0 + (n + 1) * CH * S, :]
                eng.dma_start(y[:, n * CH:(n + 1) * CH, :],
                              src.rearrange("(b s) d -> s b d", s=S)).then_inc(y_in[n], 16)

            @block.scalar
            def _(act):
                for n in range(B // CH):
                    load(act, n, y2, B * S)

            @block.vector
            def _(v):
                for n in range(B // CH):
                    v.wait_ge(y_in[n], 32)
                    for b in range(n * CH, (n + 1) * CH):
                        v.scalar_tensor_tensor(out=x[:, b, :], in0=y1[:, b, :], scalar=gate[:, 0, b:b + 1],
                                               in1=x[:, b, :], op0=ALU.mult, op1=ALU.add).then_inc(first, 1)
                    v.wait_ge(first, (n + 1) * CH)
                    for b in range(n * CH, (n + 1) * CH):
                        v.scalar_tensor_tensor(out=x[:, b, :], in0=y2[:, b, :], scalar=gate[:, 1, b:b + 1],
                                               in1=x[:, b, :], op0=ALU.mult, op1=ALU.add).then_inc(second, 1)

            @block.sync
            def _(sp):
                for n in range(B // CH):
                    load(sp, n, y1, 0)
                for n in range(B // CH):
                    sp.wait_ge(second, (n + 1) * CH)
                    sp.dma_start(A["out"][:, n * CH:(n + 1) * CH, :],
                                 x[:, n * CH:(n + 1) * CH, :]).then_inc(o_store, 16)
                sp.wait_ge(o_store, 16 * (B // CH))


def shape_constants(np):
    k = np.zeros((128, K_N), np.float32)
    r = np.arange(128)
    k[:, K_ID:K_ID + 128] = np.eye(128)
    k[:, K_TRI:K_TRI + 128] = r[:, None] < r[None, :]
    k[:, K_ONE:K_ONE + 128] = 1
    for c in range(8):
        k[[c, 64 + c], K_SEL1 + C * c:K_SEL1 + C * c + C] = -1
    k[:, K_SIGN:K_SIGN + 512] = np.where(np.arange(512) % 16 < 8, 1, -1)
    k[:, K_SCOL] = np.where(r % 32 < 8, 1, np.where(r % 32 < 16, -1, 1))
    k[:, K_IOTA8:K_IOTA8 + E] = np.arange(E)
    k[:, K_EOFF:K_EOFF + E] = np.arange(E) * REGION
    k[:, K_PART] = r
    k[:, K_TILE:K_TILE + NT1 + 1] = np.arange(NT1 + 1)
    k[:, K_KEYS] = np.where(r % 32 == 16, -OFF, 0)
    k[:, K_BACK:K_BACK + 2 * B] = r[:, None] + (S * np.arange(B)[:, None] + [0, B * S]).reshape(-1)
    k[:, K_PAD:K_PAD + 2 * PADS] = r[:, None] + (np.array([[1], [2]]) * B * S + 128 * np.arange(PADS)).reshape(-1)
    k[:64, K_HOT:K_HOT + E] = r[:64, None] % 32 == np.arange(E)
    return k


def kernel(x, ctx_1024, L0_xattn_fm_w, L0_xattn_fm_b, L0_xattn_fc_w, L0_xattn_fc_b, L0_ffn_w_red, L0_ffn_wg,
           L0_ffn_w1, L0_ffn_b1, L0_ffn_w2, L0_ffn_b2, L1_xattn_ln_g, L1_xattn_ln_b, L1_xattn_cln_g,
           L1_xattn_cln_b, L1_xattn_Wq, L1_xattn_Wkv, L1_xattn_Wo, L1_xattn_Wff1, L1_xattn_Wff2,
           L1_ffn_router_w, L1_ffn_w1, L1_ffn_w2):
    import numpy as np
    import concourse.bacc as bacc
    from concourse.bass_utils import run_bass_kernel_spmd

    n = np.asarray
    fm_w, fm_b = n(L0_xattn_fm_w), n(L0_xattn_fm_b)
    wz = np.zeros((D, G, 128), np.float32)
    zb = np.full((128, 1), OFF, np.float32)
    for h in range(H):
        g, j = divmod(h, 4)
        for s in range(2):
            wz[HD0 * h:HD0 * h + HD0, g, 32 * j + 8 * s:32 * j + 8 * s + 8] = fm_w.T
            zb[32 * j + 8 * s:32 * j + 8 * s + 8, 0] = fm_b
    wkv = n(L1_xattn_Wkv)
    def experts_layout(w1, w2):
        first = n(w1).transpose(1, 0, 2).reshape(D, E * F)
        return np.concatenate([first, n(w2).reshape(E, FC, 128, D).transpose(2, 0, 1, 3).reshape(128, E * F)], 1)

    arrays = dict(
        cst=shape_constants(np), x=n(x).transpose(1, 0, 2), cx=n(ctx_1024).transpose(1, 0, 2), wz=wz, zb=zb,
        vb=np.concatenate([fm_b] * H), fcw=n(L0_xattn_fc_w).T.reshape(2, 128, D).transpose(1, 0, 2),
        fcb=n(L0_xattn_fc_b), wred=n(L0_ffn_w_red).T, wg=n(L0_ffn_wg), w12_0=experts_layout(L0_ffn_w1, L0_ffn_w2),
        b1=n(L0_ffn_b1), b2=n(L0_ffn_b2), wq=n(L1_xattn_Wq), wk=wkv[:, :HD1],
        wv=wkv[:, HD1:], wo=n(L1_xattn_Wo).reshape(8, 128, D).transpose(1, 0, 2),
        wf1=n(L1_xattn_Wff1), wf2=n(L1_xattn_Wff2).reshape(FC, 128, D).transpose(1, 0, 2),
        lnp=np.stack([n(L1_xattn_ln_g), n(L1_xattn_ln_b), n(L1_xattn_cln_g), n(L1_xattn_cln_b)], 1),
        router=n(L1_ffn_router_w).T, w12_1=experts_layout(L1_ffn_w1, L1_ffn_w2))
    arrays = {"in_" + k: np.ascontiguousarray(a) for k, a in arrays.items()}
    nc = bacc.Bacc("TRN2", target_bir_lowering=False, num_devices=1)
    A = {k[3:]: nc.dram_tensor(k, a.shape, mybir.dt.from_np(a.dtype), kind="ExternalInput").ap()
         for k, a in arrays.items()}
    A["out"] = nc.dram_tensor("out_x", (S, B, D), F32, kind="ExternalOutput").ap()
    build(nc, A)
    r = run_bass_kernel_spmd(nc, [arrays], core_ids=[0])
    return np.ascontiguousarray(r.results[0]["out_x"].transpose(1, 0, 2))
```
